# Optimizing a Trainium2 kernel written in Bass

```python
import numpy as np
import jax
import jax.numpy as jnp

def _softmax(x, axis=-1):
    return jax.nn.softmax(x, axis=axis)

def _gelu(x):
    return jax.nn.gelu(x, approximate=True)

def _silu(x):
    return jax.nn.silu(x)

def _sigmoid(x):
    return jax.nn.sigmoid(x)

def _layernorm(x, axis=-1, eps=1e-05):
    m = jnp.mean(x, axis=axis, keepdims=True)
    v = jnp.var(x, axis=axis, keepdims=True)
    return (x - m) / jnp.sqrt(v + eps)

def _scatter_add(tgt, idx, src, axis=0):
    return tgt.at[idx].add(src)

def _segment_sum(src, seg, n):
    return jax.ops.segment_sum(src, seg, n)
kernel_name = 'mk_xattn_seq_d4_seqx_r8_778f7b'

def setup_inputs(seed: int=0):
    np.random.seed(seed)
    _w = jnp.asarray

    def _rec_inputs():
        import jax
        import jax.numpy as jnp
        _rk = jax.random.key(seed)
        x = -0.0005207 + 1.001 * jax.random.normal(jax.random.fold_in(_rk, 1), (4, 256, 256), jnp.float32)
        _lenS = 256 - jax.random.randint(jax.random.fold_in(_rk, 7), (4,), 0, max(1, 256 // 4) + 1, jnp.int32)
        _lenS2 = 256 - jax.random.randint(jax.random.fold_in(_rk, 8), (4,), 0, max(1, 256 // 4) + 1, jnp.int32)
        _ctx_2048P = jax.random.normal(jax.random.fold_in(_rk, 11), (4, 16, 256), jnp.float32)
        _ctx_2048c = jax.random.dirichlet(jax.random.fold_in(_rk, 511), 0.3 * jnp.ones((16,), jnp.float32), (4, 256))
        _ctx_2048t = jnp.einsum('bsk,bkd->bsd', _ctx_2048c, _ctx_2048P)
        _ctx_2048t = _ctx_2048t * jax.lax.rsqrt(jnp.mean(jnp.square(_ctx_2048t)) + 1e-12) * 0.953939
        ctx_2048 = 2.81802e-05 + 1.00001 * (_ctx_2048t + 0.3 * jax.random.normal(jax.random.fold_in(_rk, 611), (4, 256, 256), jnp.float32))
        _validS = jnp.arange(256)[None, :] < _lenS[:, None]
        _validS2 = jnp.arange(256)[None, :] < _lenS2[:, None]
        _causal = jnp.tril(jnp.ones((256, 256), dtype=bool))
        mask_BxS2_ik0 = jnp.where(jnp.broadcast_to(_validS2[:, :], (4, 256)), 0, 1).astype(jnp.int32)
        mask_Bx1xSxS2_ff0 = jnp.where(jnp.ones((4, 1, 256, 256), dtype=bool), 0.0, -1000000000.0).astype(jnp.float32)
        return (x, ctx_2048, mask_BxS2_ik0, mask_Bx1xSxS2_ff0)
    x, ctx_2048, mask_BxS2_ik0, mask_Bx1xSxS2_ff0 = _rec_inputs()

    def _L0_xattn_setup():
        import jax, jax.numpy as jnp
        import numpy as np
        B, Q, S1, S2 = (4, 32, 256, 256)
        D, H, K, F = (256, 16, 128, 1024)
        LN_EPS = 1e-05

        def _layer_norm(x, scale, offset):
            mu = jnp.mean(x, axis=-1, keepdims=True)
            var = jnp.var(x, axis=-1, keepdims=True)
            return (x - mu) * jax.lax.rsqrt(var + LN_EPS) * scale + offset

        def _cross_attention(q_in, kv_in, wq, bq, wk, bk, wv, bv, wo, bo, bias_k, bias_v):
            b, q_len, _ = q_in.shape
            t = kv_in.shape[1]
            qh = (q_in @ wq + bq).reshape(b, q_len, H, K)
            kh = (kv_in @ wk + bk).reshape(b, t, H, K)
            vh = (kv_in @ wv + bv).reshape(b, t, H, K)
            kh = jnp.concatenate([kh, jnp.broadcast_to(bias_k, (b, 1, H, K))], axis=1)
            vh = jnp.concatenate([vh, jnp.broadcast_to(bias_v, (b, 1, H, K))], axis=1)
            scale = jnp.sqrt(jnp.asarray(K, q_in.dtype))
            logits = jnp.einsum('bqhk,bthk->bhqt', qh, kh) / scale
            weights = jax.nn.softmax(logits, axis=-1)
            ctx = jnp.einsum('bhqt,bthk->bqhk', weights, vh).reshape(b, q_len, H * K)
            return ctx @ wo + bo

        def _forward(x, xf_1, xf_2, ln1_scale, ln1_offset, wq1, bq1, wk1, bk1, wv1, bv1, wo1, bo1, bias_k1, bias_v1, ln2_scale, ln2_offset, wq2, bq2, wk2, bk2, wv2, bv2, wo2, bo2, bias_k2, bias_v2, ln_mlp_scale, ln_mlp_offset, w_fc1, b_fc1, w_fc2, b_fc2):
            res = x
            h = _layer_norm(x, ln1_scale, ln1_offset)
            x = res + _cross_attention(h, xf_1, wq1, bq1, wk1, bk1, wv1, bv1, wo1, bo1, bias_k1, bias_v1)
            res = x
            h = _layer_norm(x, ln2_scale, ln2_offset)
            x = res + _cross_attention(h, xf_2, wq2, bq2, wk2, bk2, wv2, bv2, wo2, bo2, bias_k2, bias_v2)
            h = _layer_norm(x, ln_mlp_scale, ln_mlp_offset)
            h = jax.nn.gelu(h @ w_fc1 + b_fc1, approximate=False) @ w_fc2 + b_fc2
            return x + h
        key = jax.random.key(seed)
        ks = iter(jax.random.split(key, 64))

        def rn(shape, s=0.02):
            return jax.random.normal(next(ks), shape, jnp.float32) * s
        inp = {'x': rn((B, Q, D), 1.0), 'xf_1': rn((B, S1, D), 1.0), 'xf_2': rn((B, S2, D), 1.0)}
        for i in (1, 2):
            inp[f'ln{i}_scale'] = jnp.ones((D,), jnp.float32)
            inp[f'ln{i}_offset'] = jnp.zeros((D,), jnp.float32)
            inp[f'wq{i}'] = rn((D, H * K))
            inp[f'bq{i}'] = jnp.zeros((H * K,), jnp.float32)
            inp[f'wk{i}'] = rn((D, H * K))
            inp[f'bk{i}'] = jnp.zeros((H * K,), jnp.float32)
            inp[f'wv{i}'] = rn((D, H * K))
            inp[f'bv{i}'] = jnp.zeros((H * K,), jnp.float32)
            inp[f'wo{i}'] = rn((H * K, D))
            inp[f'bo{i}'] = jnp.zeros((D,), jnp.float32)
            inp[f'bias_k{i}'] = rn((1, 1, H, K))
            inp[f'bias_v{i}'] = rn((1, 1, H, K))
        inp['ln_mlp_scale'] = jnp.ones((D,), jnp.float32)
        inp['ln_mlp_offset'] = jnp.zeros((D,), jnp.float32)
        inp['w_fc1'] = rn((D, F))
        inp['b_fc1'] = jnp.zeros((F,), jnp.float32)
        inp['w_fc2'] = rn((F, D))
        inp['b_fc2'] = jnp.zeros((D,), jnp.float32)
        return inp
    _L0_xattn_all = _L0_xattn_setup()
    _L0_xattn_in = {k: v for k, v in _L0_xattn_all.items() if k in ('ln1_scale', 'ln1_offset', 'wq1', 'bq1', 'wk1', 'bk1', 'wv1', 'bv1', 'wo1', 'bo1', 'bias_k1', 'bias_v1', 'ln2_scale', 'ln2_offset', 'wq2', 'bq2', 'wk2', 'bk2', 'wv2', 'bv2', 'wo2', 'bo2', 'bias_k2', 'bias_v2', 'ln_mlp_scale', 'ln_mlp_offset', 'w_fc1', 'b_fc1', 'w_fc2', 'b_fc2')}
    del _L0_xattn_all

    def _L1_xattn_setup():
        import jax, jax.numpy as jnp
        import numpy as np
        B, P, K, H, NH = (4, 256, 32, 256, 16)
        DH = H // NH
        EPS = 1e-06

        def rmsnorm(x, w):
            var = jnp.mean(jnp.square(x), axis=-1, keepdims=True)
            return x * jax.lax.rsqrt(var + EPS) * w
        key = jax.random.key(seed)
        ks = jax.random.split(key, 12)
        s = 0.02
        return {'x': jax.random.normal(ks[0], (B, P, H), jnp.float32), 'latents': jax.random.normal(ks[1], (B, K, H), jnp.float32), 'attention_mask': jax.random.randint(ks[2], (B, P), 0, 2, jnp.int32), 'q_w': s * jax.random.normal(ks[3], (H, H), jnp.float32), 'q_b': jnp.zeros((H,), jnp.float32), 'kv_w': s * jax.random.normal(ks[4], (H, 2 * H), jnp.float32), 'kv_b': jnp.zeros((2 * H,), jnp.float32), 'out_w': s * jax.random.normal(ks[5], (H, H), jnp.float32), 'out_b': jnp.zeros((H,), jnp.float32), 'postnorm_w': jnp.ones((H,), jnp.float32), 'mlp_w1': s * jax.random.normal(ks[6], (H, 4 * H), jnp.float32), 'mlp_b1': jnp.zeros((4 * H,), jnp.float32), 'mlp_w2': s * jax.random.normal(ks[7], (4 * H, H), jnp.float32), 'mlp_b2': jnp.zeros((H,), jnp.float32)}
    _L1_xattn_all = _L1_xattn_setup()
    _L1_xattn_in = {k: v for k, v in _L1_xattn_all.items() if k in ('q_w', 'q_b', 'kv_w', 'kv_b', 'out_w', 'out_b', 'postnorm_w', 'mlp_w1', 'mlp_b1', 'mlp_w2', 'mlp_b2')}
    del _L1_xattn_all

    def _L2_xattn_setup():
        import jax, jax.numpy as jnp
        import numpy as np
        H = 256
        NH = 32
        KVH = 8
        HD = H // NH
        GROUPS = NH // KVH
        EPS = 1e-06
        B, L, S = (4, 128, 128)

        def _gqa_forward(hidden_state, encoder_hidden_state, encoder_attention_mask, Wq, bq, Wk, bk, Wv, bv, Wo, bo, gamma, beta):
            b, l, _ = hidden_state.shape
            s = encoder_hidden_state.shape[1]
            q = hidden_state @ Wq + bq
            k = encoder_hidden_state @ Wk + bk
            v = encoder_hidden_state @ Wv + bv
            q = q.reshape(b, l, KVH, GROUPS, HD).transpose(0, 2, 3, 1, 4)
            k = k.reshape(b, s, KVH, HD).transpose(0, 2, 1, 3)
            v = v.reshape(b, s, KVH, HD).transpose(0, 2, 1, 3)
            scale = 1.0 / jnp.sqrt(jnp.asarray(HD, q.dtype))
            scores = jnp.einsum('bkgld,bksd->bkgls', q, k) * scale
            scores = scores + encoder_attention_mask[:, :, None, :, :]
            attn = jax.nn.softmax(scores, axis=-1)
            out = jnp.einsum('bkgls,bksd->bkgld', attn, v)
            out = out.transpose(0, 3, 1, 2, 4).reshape(b, l, H)
            out = out @ Wo + bo
            x = out + hidden_state
            mu = jnp.mean(x, axis=-1, keepdims=True)
            var = jnp.var(x, axis=-1, keepdims=True)
            return (x - mu) * jax.lax.rsqrt(var + EPS) * gamma + beta
        key = jax.random.key(seed)
        ks = jax.random.split(key, 12)
        sd = 0.02
        return {'hidden_state': jax.random.normal(ks[0], (B, L, H), jnp.float32), 'encoder_hidden_state': jax.random.normal(ks[1], (B, S, H), jnp.float32), 'encoder_attention_mask': jnp.zeros((B, 1, L, S), jnp.float32), 'Wq': jax.random.normal(ks[2], (H, H), jnp.float32) * sd, 'bq': jnp.zeros((H,), jnp.float32), 'Wk': jax.random.normal(ks[3], (H, KVH * HD), jnp.float32) * sd, 'bk': jnp.zeros((KVH * HD,), jnp.float32), 'Wv': jax.random.normal(ks[4], (H, KVH * HD), jnp.float32) * sd, 'bv': jnp.zeros((KVH * HD,), jnp.float32), 'Wo': jax.random.normal(ks[5], (H, H), jnp.float32) * sd, 'bo': jnp.zeros((H,), jnp.float32), 'gamma': jnp.ones((H,), jnp.float32), 'beta': jnp.zeros((H,), jnp.float32)}
    _L2_xattn_all = _L2_xattn_setup()
    _L2_xattn_in = {k: v for k, v in _L2_xattn_all.items() if k in ('Wq', 'bq', 'Wk', 'bk', 'Wv', 'bv', 'Wo', 'bo', 'gamma', 'beta')}
    del _L2_xattn_all

    def _L3_xattn_setup():
        import jax, jax.numpy as jnp
        import numpy as np
        B, P, K, H, NH = (4, 256, 32, 256, 16)
        DH = H // NH
        EPS = 1e-06

        def rmsnorm(x, w):
            var = jnp.mean(jnp.square(x), axis=-1, keepdims=True)
            return x * jax.lax.rsqrt(var + EPS) * w
        key = jax.random.key(seed)
        ks = jax.random.split(key, 12)
        s = 0.02
        return {'x': jax.random.normal(ks[0], (B, P, H), jnp.float32), 'latents': jax.random.normal(ks[1], (B, K, H), jnp.float32), 'attention_mask': jax.random.randint(ks[2], (B, P), 0, 2, jnp.int32), 'q_w': s * jax.random.normal(ks[3], (H, H), jnp.float32), 'q_b': jnp.zeros((H,), jnp.float32), 'kv_w': s * jax.random.normal(ks[4], (H, 2 * H), jnp.float32), 'kv_b': jnp.zeros((2 * H,), jnp.float32), 'out_w': s * jax.random.normal(ks[5], (H, H), jnp.float32), 'out_b': jnp.zeros((H,), jnp.float32), 'postnorm_w': jnp.ones((H,), jnp.float32), 'mlp_w1': s * jax.random.normal(ks[6], (H, 4 * H), jnp.float32), 'mlp_b1': jnp.zeros((4 * H,), jnp.float32), 'mlp_w2': s * jax.random.normal(ks[7], (4 * H, H), jnp.float32), 'mlp_b2': jnp.zeros((H,), jnp.float32)}
    _L3_xattn_all = _L3_xattn_setup()
    _L3_xattn_in = {k: v for k, v in _L3_xattn_all.items() if k in ('q_w', 'q_b', 'kv_w', 'kv_b', 'out_w', 'out_b', 'postnorm_w', 'mlp_w1', 'mlp_b1', 'mlp_w2', 'mlp_b2')}
    del _L3_xattn_all
    return {'x': x, 'ctx_2048': ctx_2048, 'mask_BxS2_ik0': mask_BxS2_ik0, 'mask_Bx1xSxS2_ff0': mask_Bx1xSxS2_ff0, 'L0_xattn_ln1_scale': _L0_xattn_in['ln1_scale'], 'L0_xattn_ln1_offset': _L0_xattn_in['ln1_offset'], 'L0_xattn_wq1': _L0_xattn_in['wq1'], 'L0_xattn_bq1': _L0_xattn_in['bq1'], 'L0_xattn_wk1': _L0_xattn_in['wk1'], 'L0_xattn_bk1': _L0_xattn_in['bk1'], 'L0_xattn_wv1': _L0_xattn_in['wv1'], 'L0_xattn_bv1': _L0_xattn_in['bv1'], 'L0_xattn_wo1': _L0_xattn_in['wo1'], 'L0_xattn_bo1': _L0_xattn_in['bo1'], 'L0_xattn_bias_k1': _L0_xattn_in['bias_k1'], 'L0_xattn_bias_v1': _L0_xattn_in['bias_v1'], 'L0_xattn_ln2_scale': _L0_xattn_in['ln2_scale'], 'L0_xattn_ln2_offset': _L0_xattn_in['ln2_offset'], 'L0_xattn_wq2': _L0_xattn_in['wq2'], 'L0_xattn_bq2': _L0_xattn_in['bq2'], 'L0_xattn_wk2': _L0_xattn_in['wk2'], 'L0_xattn_bk2': _L0_xattn_in['bk2'], 'L0_xattn_wv2': _L0_xattn_in['wv2'], 'L0_xattn_bv2': _L0_xattn_in['bv2'], 'L0_xattn_wo2': _L0_xattn_in['wo2'], 'L0_xattn_bo2': _L0_xattn_in['bo2'], 'L0_xattn_bias_k2': _L0_xattn_in['bias_k2'], 'L0_xattn_bias_v2': _L0_xattn_in['bias_v2'], 'L0_xattn_ln_mlp_scale': _L0_xattn_in['ln_mlp_scale'], 'L0_xattn_ln_mlp_offset': _L0_xattn_in['ln_mlp_offset'], 'L0_xattn_w_fc1': _L0_xattn_in['w_fc1'], 'L0_xattn_b_fc1': _L0_xattn_in['b_fc1'], 'L0_xattn_w_fc2': _L0_xattn_in['w_fc2'], 'L0_xattn_b_fc2': _L0_xattn_in['b_fc2'], 'L1_xattn_q_w': _L1_xattn_in['q_w'], 'L1_xattn_q_b': _L1_xattn_in['q_b'], 'L1_xattn_kv_w': _L1_xattn_in['kv_w'], 'L1_xattn_kv_b': _L1_xattn_in['kv_b'], 'L1_xattn_out_w': _L1_xattn_in['out_w'], 'L1_xattn_out_b': _L1_xattn_in['out_b'], 'L1_xattn_postnorm_w': _L1_xattn_in['postnorm_w'], 'L1_xattn_mlp_w1': _L1_xattn_in['mlp_w1'], 'L1_xattn_mlp_b1': _L1_xattn_in['mlp_b1'], 'L1_xattn_mlp_w2': _L1_xattn_in['mlp_w2'], 'L1_xattn_mlp_b2': _L1_xattn_in['mlp_b2'], 'L2_xattn_Wq': _L2_xattn_in['Wq'], 'L2_xattn_bq': _L2_xattn_in['bq'], 'L2_xattn_Wk': _L2_xattn_in['Wk'], 'L2_xattn_bk': _L2_xattn_in['bk'], 'L2_xattn_Wv': _L2_xattn_in['Wv'], 'L2_xattn_bv': _L2_xattn_in['bv'], 'L2_xattn_Wo': _L2_xattn_in['Wo'], 'L2_xattn_bo': _L2_xattn_in['bo'], 'L2_xattn_gamma': _L2_xattn_in['gamma'], 'L2_xattn_beta': _L2_xattn_in['beta'], 'L3_xattn_q_w': _L3_xattn_in['q_w'], 'L3_xattn_q_b': _L3_xattn_in['q_b'], 'L3_xattn_kv_w': _L3_xattn_in['kv_w'], 'L3_xattn_kv_b': _L3_xattn_in['kv_b'], 'L3_xattn_out_w': _L3_xattn_in['out_w'], 'L3_xattn_out_b': _L3_xattn_in['out_b'], 'L3_xattn_postnorm_w': _L3_xattn_in['postnorm_w'], 'L3_xattn_mlp_w1': _L3_xattn_in['mlp_w1'], 'L3_xattn_mlp_b1': _L3_xattn_in['mlp_b1'], 'L3_xattn_mlp_w2': _L3_xattn_in['mlp_w2'], 'L3_xattn_mlp_b2': _L3_xattn_in['mlp_b2']}

def reference(x, ctx_2048, mask_BxS2_ik0, mask_Bx1xSxS2_ff0, L0_xattn_ln1_scale, L0_xattn_ln1_offset, L0_xattn_wq1, L0_xattn_bq1, L0_xattn_wk1, L0_xattn_bk1, L0_xattn_wv1, L0_xattn_bv1, L0_xattn_wo1, L0_xattn_bo1, L0_xattn_bias_k1, L0_xattn_bias_v1, L0_xattn_ln2_scale, L0_xattn_ln2_offset, L0_xattn_wq2, L0_xattn_bq2, L0_xattn_wk2, L0_xattn_bk2, L0_xattn_wv2, L0_xattn_bv2, L0_xattn_wo2, L0_xattn_bo2, L0_xattn_bias_k2, L0_xattn_bias_v2, L0_xattn_ln_mlp_scale, L0_xattn_ln_mlp_offset, L0_xattn_w_fc1, L0_xattn_b_fc1, L0_xattn_w_fc2, L0_xattn_b_fc2, L1_xattn_q_w, L1_xattn_q_b, L1_xattn_kv_w, L1_xattn_kv_b, L1_xattn_out_w, L1_xattn_out_b, L1_xattn_postnorm_w, L1_xattn_mlp_w1, L1_xattn_mlp_b1, L1_xattn_mlp_w2, L1_xattn_mlp_b2, L2_xattn_Wq, L2_xattn_bq, L2_xattn_Wk, L2_xattn_bk, L2_xattn_Wv, L2_xattn_bv, L2_xattn_Wo, L2_xattn_bo, L2_xattn_gamma, L2_xattn_beta, L3_xattn_q_w, L3_xattn_q_b, L3_xattn_kv_w, L3_xattn_kv_b, L3_xattn_out_w, L3_xattn_out_b, L3_xattn_postnorm_w, L3_xattn_mlp_w1, L3_xattn_mlp_b1, L3_xattn_mlp_w2, L3_xattn_mlp_b2):
    import jax
    import jax.numpy as jnp

    def _L0_xattn_ref(x, xf_1, xf_2, ln1_scale, ln1_offset, wq1, bq1, wk1, bk1, wv1, bv1, wo1, bo1, bias_k1, bias_v1, ln2_scale, ln2_offset, wq2, bq2, wk2, bk2, wv2, bv2, wo2, bo2, bias_k2, bias_v2, ln_mlp_scale, ln_mlp_offset, w_fc1, b_fc1, w_fc2, b_fc2):
        import jax, jax.numpy as jnp
        import numpy as np
        B, Q, S1, S2 = (4, 32, 256, 256)
        D, H, K, F = (256, 16, 128, 1024)
        LN_EPS = 1e-05

        def _layer_norm(x, scale, offset):
            mu = jnp.mean(x, axis=-1, keepdims=True)
            var = jnp.var(x, axis=-1, keepdims=True)
            return (x - mu) * jax.lax.rsqrt(var + LN_EPS) * scale + offset

        def _cross_attention(q_in, kv_in, wq, bq, wk, bk, wv, bv, wo, bo, bias_k, bias_v):
            b, q_len, _ = q_in.shape
            t = kv_in.shape[1]
            qh = (q_in @ wq + bq).reshape(b, q_len, H, K)
            kh = (kv_in @ wk + bk).reshape(b, t, H, K)
            vh = (kv_in @ wv + bv).reshape(b, t, H, K)
            kh = jnp.concatenate([kh, jnp.broadcast_to(bias_k, (b, 1, H, K))], axis=1)
            vh = jnp.concatenate([vh, jnp.broadcast_to(bias_v, (b, 1, H, K))], axis=1)
            scale = jnp.sqrt(jnp.asarray(K, q_in.dtype))
            logits = jnp.einsum('bqhk,bthk->bhqt', qh, kh) / scale
            weights = jax.nn.softmax(logits, axis=-1)
            ctx = jnp.einsum('bhqt,bthk->bqhk', weights, vh).reshape(b, q_len, H * K)
            return ctx @ wo + bo

        def _forward(x, xf_1, xf_2, ln1_scale, ln1_offset, wq1, bq1, wk1, bk1, wv1, bv1, wo1, bo1, bias_k1, bias_v1, ln2_scale, ln2_offset, wq2, bq2, wk2, bk2, wv2, bv2, wo2, bo2, bias_k2, bias_v2, ln_mlp_scale, ln_mlp_offset, w_fc1, b_fc1, w_fc2, b_fc2):
            res = x
            h = _layer_norm(x, ln1_scale, ln1_offset)
            x = res + _cross_attention(h, xf_1, wq1, bq1, wk1, bk1, wv1, bv1, wo1, bo1, bias_k1, bias_v1)
            res = x
            h = _layer_norm(x, ln2_scale, ln2_offset)
            x = res + _cross_attention(h, xf_2, wq2, bq2, wk2, bk2, wv2, bv2, wo2, bo2, bias_k2, bias_v2)
            h = _layer_norm(x, ln_mlp_scale, ln_mlp_offset)
            h = jax.nn.gelu(h @ w_fc1 + b_fc1, approximate=False) @ w_fc2 + b_fc2
            return x + h
        return _forward(x, xf_1, xf_2, ln1_scale, ln1_offset, wq1, bq1, wk1, bk1, wv1, bv1, wo1, bo1, bias_k1, bias_v1, ln2_scale, ln2_offset, wq2, bq2, wk2, bk2, wv2, bv2, wo2, bo2, bias_k2, bias_v2, ln_mlp_scale, ln_mlp_offset, w_fc1, b_fc1, w_fc2, b_fc2)

    def _L1_xattn_ref(x, latents, attention_mask, q_w, q_b, kv_w, kv_b, out_w, out_b, postnorm_w, mlp_w1, mlp_b1, mlp_w2, mlp_b2):
        import jax, jax.numpy as jnp
        import numpy as np
        B, P, K, H, NH = (4, 256, 32, 256, 16)
        DH = H // NH
        EPS = 1e-06

        def rmsnorm(x, w):
            var = jnp.mean(jnp.square(x), axis=-1, keepdims=True)
            return x * jax.lax.rsqrt(var + EPS) * w
        b, p, _ = x.shape
        k_len = latents.shape[1]
        residual = latents
        h = jnp.concatenate([x, latents], axis=1)
        q = (latents @ q_w + q_b).reshape(b, k_len, NH, DH)
        kv = (h @ kv_w + kv_b).reshape(b, p + k_len, NH, DH, 2)
        kmat, v = (kv[..., 0], kv[..., 1])
        attn = jnp.einsum('bkhd,bnhd->bhkn', q, kmat) / DH
        full_mask = jnp.concatenate([attention_mask.astype(bool), jnp.ones((b, k_len), bool)], axis=-1)
        attn = jnp.where(full_mask[:, None, None, :], attn, -jnp.inf)
        attn = jax.nn.softmax(attn.astype(jnp.float32), axis=-1).astype(q.dtype)
        attn_out = jnp.einsum('bhkn,bnhd->bkhd', attn, v).reshape(b, k_len, H)
        attn_out = attn_out @ out_w + out_b + residual
        out = rmsnorm(attn_out, postnorm_w)
        out = jax.nn.gelu(out @ mlp_w1 + mlp_b1) @ mlp_w2 + mlp_b2
        return out + residual

    def _L2_xattn_ref(hidden_state, encoder_hidden_state, encoder_attention_mask, Wq, bq, Wk, bk, Wv, bv, Wo, bo, gamma, beta):
        import jax, jax.numpy as jnp
        import numpy as np
        H = 256
        NH = 32
        KVH = 8
        HD = H // NH
        GROUPS = NH // KVH
        EPS = 1e-06
        B, L, S = (4, 128, 128)

        def _gqa_forward(hidden_state, encoder_hidden_state, encoder_attention_mask, Wq, bq, Wk, bk, Wv, bv, Wo, bo, gamma, beta):
            b, l, _ = hidden_state.shape
            s = encoder_hidden_state.shape[1]
            q = hidden_state @ Wq + bq
            k = encoder_hidden_state @ Wk + bk
            v = encoder_hidden_state @ Wv + bv
            q = q.reshape(b, l, KVH, GROUPS, HD).transpose(0, 2, 3, 1, 4)
            k = k.reshape(b, s, KVH, HD).transpose(0, 2, 1, 3)
            v = v.reshape(b, s, KVH, HD).transpose(0, 2, 1, 3)
            scale = 1.0 / jnp.sqrt(jnp.asarray(HD, q.dtype))
            scores = jnp.einsum('bkgld,bksd->bkgls', q, k) * scale
            scores = scores + encoder_attention_mask[:, :, None, :, :]
            attn = jax.nn.softmax(scores, axis=-1)
            out = jnp.einsum('bkgls,bksd->bkgld', attn, v)
            out = out.transpose(0, 3, 1, 2, 4).reshape(b, l, H)
            out = out @ Wo + bo
            x = out + hidden_state
            mu = jnp.mean(x, axis=-1, keepdims=True)
            var = jnp.var(x, axis=-1, keepdims=True)
            return (x - mu) * jax.lax.rsqrt(var + EPS) * gamma + beta
        return _gqa_forward(hidden_state, encoder_hidden_state, encoder_attention_mask, Wq, bq, Wk, bk, Wv, bv, Wo, bo, gamma, beta)

    def _L3_xattn_ref(x, latents, attention_mask, q_w, q_b, kv_w, kv_b, out_w, out_b, postnorm_w, mlp_w1, mlp_b1, mlp_w2, mlp_b2):
        import jax, jax.numpy as jnp
        import numpy as np
        B, P, K, H, NH = (4, 256, 32, 256, 16)
        DH = H // NH
        EPS = 1e-06

        def rmsnorm(x, w):
            var = jnp.mean(jnp.square(x), axis=-1, keepdims=True)
            return x * jax.lax.rsqrt(var + EPS) * w
        b, p, _ = x.shape
        k_len = latents.shape[1]
        residual = latents
        h = jnp.concatenate([x, latents], axis=1)
        q = (latents @ q_w + q_b).reshape(b, k_len, NH, DH)
        kv = (h @ kv_w + kv_b).reshape(b, p + k_len, NH, DH, 2)
        kmat, v = (kv[..., 0], kv[..., 1])
        attn = jnp.einsum('bkhd,bnhd->bhkn', q, kmat) / DH
        full_mask = jnp.concatenate([attention_mask.astype(bool), jnp.ones((b, k_len), bool)], axis=-1)
        attn = jnp.where(full_mask[:, None, None, :], attn, -jnp.inf)
        attn = jax.nn.softmax(attn.astype(jnp.float32), axis=-1).astype(q.dtype)
        attn_out = jnp.einsum('bhkn,bnhd->bkhd', attn, v).reshape(b, k_len, H)
        attn_out = attn_out @ out_w + out_b + residual
        out = rmsnorm(attn_out, postnorm_w)
        out = jax.nn.gelu(out @ mlp_w1 + mlp_b1) @ mlp_w2 + mlp_b2
        return out + residual
    x = _L0_xattn_ref(x, ctx_2048, ctx_2048, L0_xattn_ln1_scale, L0_xattn_ln1_offset, L0_xattn_wq1, L0_xattn_bq1, L0_xattn_wk1, L0_xattn_bk1, L0_xattn_wv1, L0_xattn_bv1, L0_xattn_wo1, L0_xattn_bo1, L0_xattn_bias_k1, L0_xattn_bias_v1, L0_xattn_ln2_scale, L0_xattn_ln2_offset, L0_xattn_wq2, L0_xattn_bq2, L0_xattn_wk2, L0_xattn_bk2, L0_xattn_wv2, L0_xattn_bv2, L0_xattn_wo2, L0_xattn_bo2, L0_xattn_bias_k2, L0_xattn_bias_v2, L0_xattn_ln_mlp_scale, L0_xattn_ln_mlp_offset, L0_xattn_w_fc1, L0_xattn_b_fc1, L0_xattn_w_fc2, L0_xattn_b_fc2)
    x = _L1_xattn_ref(ctx_2048, x, mask_BxS2_ik0, L1_xattn_q_w, L1_xattn_q_b, L1_xattn_kv_w, L1_xattn_kv_b, L1_xattn_out_w, L1_xattn_out_b, L1_xattn_postnorm_w, L1_xattn_mlp_w1, L1_xattn_mlp_b1, L1_xattn_mlp_w2, L1_xattn_mlp_b2)
    x = _L2_xattn_ref(x, ctx_2048, mask_Bx1xSxS2_ff0, L2_xattn_Wq, L2_xattn_bq, L2_xattn_Wk, L2_xattn_bk, L2_xattn_Wv, L2_xattn_bv, L2_xattn_Wo, L2_xattn_bo, L2_xattn_gamma, L2_xattn_beta)
    x = _L3_xattn_ref(ctx_2048, x, mask_BxS2_ik0, L3_xattn_q_w, L3_xattn_q_b, L3_xattn_kv_w, L3_xattn_kv_b, L3_xattn_out_w, L3_xattn_out_b, L3_xattn_postnorm_w, L3_xattn_mlp_w1, L3_xattn_mlp_b1, L3_xattn_mlp_w2, L3_xattn_mlp_b2)
    return x

_drawn_inputs = setup_inputs


def setup_inputs(seed=0):
    import zlib

    import numpy as np

    out = dict(_drawn_inputs(seed))
    spreads = {'L0_xattn_ln1_scale': (1.0, 0.6),
     'L0_xattn_ln1_offset': (0.0, 0.8),
     'L0_xattn_bq1': (0.0, 0.8),
     'L0_xattn_bk1': (0.0, 2.0),
     'L0_xattn_bv1': (0.0, 0.1),
     'L0_xattn_bo1': (0.0, 0.1),
     'L0_xattn_ln2_scale': (1.0, 0.6),
     'L0_xattn_ln2_offset': (0.0, 0.8),
     'L0_xattn_bq2': (0.0, 0.8),
     'L0_xattn_bk2': (0.0, 2.0),
     'L0_xattn_bv2': (0.0, 0.1),
     'L0_xattn_bo2': (0.0, 0.1),
     'L0_xattn_ln_mlp_scale': (1.0, 0.6),
     'L0_xattn_ln_mlp_offset': (0.0, 0.703),
     'L0_xattn_b_fc1': (0.0, 0.1),
     'L0_xattn_b_fc2': (0.0, 0.1),
     'L1_xattn_q_b': (0.0, 2.0),
     'L1_xattn_kv_b': (0.0, 0.8),
     'L1_xattn_out_b': (0.0, 2.0),
     'L1_xattn_postnorm_w': (1.0, 0.6),
     'L1_xattn_mlp_b1': (0.0, 0.1),
     'L1_xattn_mlp_b2': (0.0, 0.1),
     'L2_xattn_bq': (0.0, 0.8),
     'L2_xattn_bk': (0.0, 2.0),
     'L2_xattn_bv': (0.0, 0.268),
     'L2_xattn_bo': (0.0, 0.1),
     'L2_xattn_gamma': (1.0, 0.2),
     'L2_xattn_beta': (0.0, 0.1),
     'L3_xattn_q_b': (0.0, 2.0),
     'L3_xattn_kv_b': (0.0, 0.8),
     'L3_xattn_out_b': (0.0, 2.0),
     'L3_xattn_postnorm_w': (1.0, 0.6),
     'L3_xattn_mlp_b1': (0.0, 0.1),
     'L3_xattn_mlp_b2': (0.0, 0.1)}
    factors = {'L0_xattn_wq1': 8.0,
     'L0_xattn_wk1': 8.0,
     'L0_xattn_bias_k1': 64.0,
     'L0_xattn_bias_v1': 64.0,
     'L0_xattn_wq2': 8.0,
     'L0_xattn_wk2': 8.0,
     'L0_xattn_bias_k2': 64.0,
     'L0_xattn_bias_v2': 64.0,
     'L1_xattn_q_w': 8.0,
     'L1_xattn_kv_w': 8.0,
     'L1_xattn_out_w': 8.0,
     'L2_xattn_Wq': 8.0,
     'L2_xattn_Wk': 8.0,
     'L3_xattn_q_w': 8.0,
     'L3_xattn_kv_w': 8.0,
     'L3_xattn_out_w': 8.0}
    for name, (base, spread) in spreads.items():
        noise = np.random.default_rng([zlib.crc32(name.encode()), seed]).standard_normal(out[name].shape)
        drawn = base * np.exp(spread * noise) if base else spread * noise
        out[name] = jnp.asarray(drawn.astype(out[name].dtype))
    for name, factor in factors.items():
        out[name] = (out[name] * factor).astype(out[name].dtype)
    return out
```

```python
from contextlib import ExitStack

import concourse.bass as bass
from concourse import mybir

P = 128
B = 4
S = 256
D = 256
T = B * S
TT = T // P
KT = D // P
QT = S // P

H0, K0 = 16, 128
E0 = H0 * K0
F = 1024
FT = F // P
LN_EPS0 = 1e-5
EPS = 1e-6
MASKED = -1e30

ALU = mybir.AluOpType
ACT = mybir.ActivationFunctionType
AX = mybir.AxisListType
F32 = mybir.dt.float32
F32R = mybir.dt.float32r
I32 = mybir.dt.int32


def wait(eng, sem, count):
    if isinstance(count, int) and count <= 0:
        return
    eng.wait_ge(sem, count)


class Core:

    def __init__(self, nc, ctx, ins):
        self.nc, self.ctx, self.ins = nc, ctx, ins
        self.used = []
        self.x = self.sb("x_tok", [P, TT, D])
        self.xT = self.sb("xT", [P, KT, T])
        self.cT = self.sb("ctxT", [P, KT, T])
        self.ident = self.sb("ident", [P, P])
        self.cols = self.sb("cols", [P, 2, P])
        self.maskrow = nc.dram_tensor("maskrow", (B, 2 * S), F32).ap()

    def sb(self, name, shape, dt=F32):
        return self.ctx.enter_context(self.nc.sbuf_tensor(name, shape, dt))

    def stage(self, name, holds_others=False):
        return Stage(self, name, holds_others)

    def clear_used(self, pool):
        for handle in self.used:
            pool.sem_clear(handle)


class Stage:

    def __init__(self, core, name, holds_others):
        self.core, self.name, self.ctx, self.holds_others = core, name, ExitStack(), holds_others
        self.sems = []

    def __enter__(self):
        return self

    def __exit__(self, *a):
        self.ctx.close()
        if not self.holds_others:
            for handle in self.core.used:
                self.core.nc.release_semaphore(handle)
            self.core.used = self.sems

    def sb(self, name, shape, dt=F32):
        return self.ctx.enter_context(self.core.nc.sbuf_tensor(f"{self.name}_{name}", shape, dt))

    def psum(self, name, shape):
        return self.ctx.enter_context(self.core.nc.psum_tensor(f"{self.name}_{name}", shape, F32))

    def sem(self, name):
        self.sems.append(self.core.nc.alloc_semaphore(name=f"{self.name}_{name}"))
        return self.sems[-1]

    def slot_sems(self, name, count):
        return [self.sem(f"{name}{n}") for n in range(count)]


COLS0 = [("L0_xattn_ln1_scale", KT), ("L0_xattn_ln1_offset", KT), ("L0_xattn_bq1", H0), ("L0_xattn_bk1", H0),
         ("L0_xattn_bias_k1", H0), ("L0_xattn_bv1", H0), ("L0_xattn_ln_mlp_scale", KT),
         ("L0_xattn_ln_mlp_offset", KT), ("L0_xattn_b_fc1", FT), ("L1_xattn_q_b", KT), ("L1_kv_b_k", KT),
         ("L1_xattn_postnorm_w", KT), ("L1_xattn_mlp_b1", FT), ("L2_xattn_bq", KT)]
COLS1 = [("L0_xattn_ln2_scale", KT), ("L0_xattn_ln2_offset", KT), ("L0_xattn_bq2", H0), ("L0_xattn_bk2", H0),
         ("L0_xattn_bias_k2", H0), ("L0_xattn_bv2", H0), ("L3_xattn_q_b", KT), ("L3_kv_b_k", KT),
         ("L3_xattn_postnorm_w", KT), ("L3_xattn_mlp_b1", FT), ("L2_xattn_bk", 1)]
L2_BK = 64


def column_places():
    places = {}
    for n, group in enumerate((COLS0, COLS1)):
        at = 0
        for name, count in group:
            places[name] = (n, at, count)
            at += count
    return places


PLACES = column_places()


def columns(core, name):
    n, at, count = PLACES[name]
    return core.cols[:, n, at:at + count]


def setup(core):
    nc, ins = core.nc, core.ins
    with core.stage("setup") as st:
        c_tok = st.sb("c_tok", [P, TT, D])
        rows = st.sb("rows", [P, 2, P])
        mask_i = st.sb("mask_i", [B, S], I32)
        mask_f = st.sb("mask_f", [B, 2 * S], F32R)
        turned = st.psum("turned", [P, 4, 512])
        turned_cols = st.psum("turned_cols", [P, 2, P])
        ctx_in, rows_in, x_in = st.sem("ctx_in"), st.sem("rows_in"), st.sem("x_in")
        zeroed, ident_made, rows_zeroed = st.sem("zeroed"), st.sem("ident_made"), st.sem("rows_zeroed")
        cols_turned, ctx_turned, masked, mask_out = (
            st.sem("cols_turned"), st.sem("ctx_turned"), st.sem("masked"), st.sem("mask_out"))
        n_rows = 0
        with nc.Block() as block:
            @block.sync
            def _(sp):
                sp.dma_start(c_tok[:], ins["ctx_2048"].rearrange("b (t p) d -> p (b t) d", p=P)).then_inc(ctx_in, 16)
                sp.dma_start(mask_i[:], ins["mask_BxS2_ik0"]).then_inc(ctx_in, 16)
                sp.dma_start(core.x[:], ins["x"].rearrange("b (t p) d -> p (b t) d", p=P)).then_inc(x_in, 16)
                sp.wait_ge(masked, 2)
                sp.dma_start(core.maskrow, mask_f[:].bitcast(F32)).then_inc(mask_out, 16)
                sp.wait_ge(mask_out, 16)
                sp.wait_ge(x_in, 16)

            @block.scalar
            def _(act):
                act.wait_ge(rows_zeroed, 1)
                nonlocal n_rows
                for name, (n, at, count) in PLACES.items():
                    if name.endswith("kv_b_k"):
                        src = ins[name[:2] + "_xattn_kv_b"].rearrange("(c p two) -> c p two", p=P, two=2)[:, :, 0]
                        act.dma_start(rows[at:at + count, n, :], src, allow_slow_non_contiguous=True).then_inc(rows_in, 16)
                    elif name == "L2_xattn_bk":
                        src = ins[name].rearrange("(c p) -> c p", c=1)
                        act.dma_start(rows[at:at + 1, n, 0:L2_BK], src).then_inc(rows_in, 16)
                    else:
                        flat = ins[name]
                        if len(flat.shape) == 4:
                            flat = flat.rearrange("a b h k -> (a b h k)")
                        act.dma_start(rows[at:at + count, n, :], flat.rearrange("(c p) -> c p", p=P)
                                      ).then_inc(rows_in, 16)
                    n_rows += 1

            @block.gpsimd
            def _(pool):
                core.clear_used(pool)
                nc.gpsimd.memset(rows[:], 0.0).then_inc(rows_zeroed, 1)
                nc.gpsimd.memset(core.ident[:], 0.0).then_inc(zeroed, 1)
                pool.wait_ge(zeroed, 1)
                nc.gpsimd.affine_select(out=core.ident[:], in_=core.ident[:], compare_op=ALU.not_equal, fill=1.0,
                                        base=0, pattern=[[-1, P]], channel_multiplier=1).then_inc(ident_made, 1)

            @block.tensor
            def _(pe):
                pe.wait_ge(ident_made, 1)
                pe.wait_ge(ctx_in, 32)
                for kt in range(KT):
                    for half in range(2):
                        for i in range(4):
                            t = 4 * half + i
                            mm = nc.tensor.transpose(turned[:, 2 * kt + half, i * P:(i + 1) * P],
                                                     c_tok[:, t, kt * P:(kt + 1) * P], core.ident[:])
                        mm.then_inc(ctx_turned, 1)
                pe.wait_ge(rows_in, 16 * len(PLACES))
                for n in range(2):
                    mm = nc.tensor.transpose(turned_cols[:, n, :], rows[:, n, :], core.ident[:])
                mm.then_inc(cols_turned, 1)

            @block.vector
            def _(dve):
                nc.vector.memset(mask_f[:, S:2 * S].bitcast(F32), 0.0).then_inc(masked, 1)
                dve.wait_ge(ctx_in, 32)
                nc.vector.tensor_scalar(mask_f[:, 0:S], mask_i[:], 0.0, MASKED, ALU.is_equal, ALU.mult
                                        ).then_inc(masked, 1)
                for kt in range(KT):
                    for half in range(2):
                        dve.wait_ge(ctx_turned, 2 * kt + half + 1)
                        nc.vector.tensor_copy(core.cT[:, kt, half * 512:(half + 1) * 512],
                                              turned[:, 2 * kt + half, :])
                dve.wait_ge(cols_turned, 1)
                nc.vector.tensor_copy(core.cols[:], turned_cols[:])


def turn(core, name, src, norm=None, eps=0.0, scale=None, offset=None, factor=1.0):
    nc, ident = core.nc, core.ident
    with core.stage(name) as st:
        stats = st.sb("stats", [P, TT, 6])
        mv = st.sb("mv", [P, TT, 2])
        msq = st.sb("msq", [P, TT])
        base = st.sb("base", [P, TT])
        power = st.sb("power", [P, TT])
        rstd = st.sb("rstd", [P, TT])
        normed = st.sb("normed", [P, TT, D])
        sc = st.sb("sc", [P, 2 * KT])
        turned = st.psum("turned", [P, 4, 512])
        stats_done, mv_done, msq_done, base_done, power_set, rstd_done, normed_done, sc_done, tile_turned = [
            st.sem(n) for n in ("stats_done", "mv_done", "msq_done", "base_done", "power_set", "rstd_done",
                                "normed_done", "sc_done", "tile_turned")]
        with nc.Block() as block:
            @block.gpsimd
            def _(pool):
                core.clear_used(pool)
                if norm:
                    nc.gpsimd.memset(power[:], -0.5).then_inc(power_set, 1)
                    pool.wait_ge(power_set, 1)
                    pool.wait_ge(base_done, 1)
                    nc.gpsimd.tensor_tensor(out=rstd[:], in0=base[:], in1=power[:], op=ALU.pow).then_inc(rstd_done, 1)

            @block.vector
            def _(dve):
                if scale is not None:
                    nc.vector.tensor_scalar(sc[:, 0:KT], scale, factor, None, ALU.mult).then_inc(sc_done, 1)
                    if offset is not None:
                        nc.vector.tensor_scalar(sc[:, KT:2 * KT], offset, factor, None, ALU.mult).then_inc(sc_done, 1)
                if norm:
                    for t in range(TT):
                        nc.vector.bn_stats(stats[:, t, :], src[:, t, :]).then_inc(stats_done, 1)
                    for t in range(TT):
                        dve.wait_ge(stats_done, t + 1)
                        nc.vector.bn_aggr(mv[:, t, :], stats[:, t, :]).then_inc(mv_done, 1)
                    dve.wait_ge(mv_done, TT)
                    if norm == "rms":
                        nc.vector.tensor_tensor(msq[:], mv[:, :, 0], mv[:, :, 0], ALU.mult).then_inc(msq_done, 1)
                        dve.wait_ge(msq_done, 1)
                        nc.vector.scalar_tensor_tensor(out=base[:], in0=msq[:], scalar=eps, in1=mv[:, :, 1],
                                                       op0=ALU.add, op1=ALU.add).then_inc(base_done, 1)
                    else:
                        nc.vector.tensor_scalar(base[:], mv[:, :, 1], eps, None, ALU.add).then_inc(base_done, 1)
                    dve.wait_ge(rstd_done, 1)
                    for t in range(TT):
                        if norm == "rms":
                            nc.vector.tensor_scalar(normed[:, t, :], src[:, t, :], rstd[:, t:t + 1], None, ALU.mult
                                                    ).then_inc(normed_done, 1)
                        else:
                            nc.vector.tensor_scalar(normed[:, t, :], src[:, t, :], mv[:, t, 0:1], rstd[:, t:t + 1],
                                                    ALU.subtract, ALU.mult).then_inc(normed_done, 1)
                if scale is not None:
                    dve.wait_ge(sc_done, 1 if offset is None else 2)
                for half in range(2):
                    for kt in range(KT):
                        out = core.xT[:, kt, half * 512:(half + 1) * 512]
                        dve.wait_ge(tile_turned, KT * half + kt + 1)
                        ps = turned[:, KT * half + kt, :]
                        if scale is None:
                            nc.vector.tensor_copy(out, ps)
                        elif offset is None:
                            nc.vector.tensor_scalar(out, ps, sc[:, kt:kt + 1], None, ALU.mult)
                        else:
                            nc.vector.tensor_scalar(out, ps, sc[:, kt:kt + 1], sc[:, KT + kt:KT + kt + 1],
                                                    ALU.mult, ALU.add)

            @block.tensor
            def _(pe):
                for half in range(2):
                    if norm:
                        pe.wait_ge(normed_done, 4 * half + 4)
                    for kt in range(KT):
                        for i in range(4):
                            t = 4 * half + i
                            tile = normed[:, t, kt * P:(kt + 1) * P] if norm else src[:, t, kt * P:(kt + 1) * P]
                            mm = nc.tensor.transpose(turned[:, KT * half + kt, i * P:(i + 1) * P], tile, ident[:])
                        mm.then_inc(tile_turned, 1)


STEPS_EVEN = [("S", 0), ("G", 0), ("G", 1), ("T", 0), ("S", 1), ("G", 2), ("V", 0), ("T", 1), ("S", 2), ("X", 0),
              ("G", 3), ("V", 1), ("T", 2), ("S", 3), ("X", 1), ("G", 4), ("V", 2), ("T", 3), ("G", 5), ("X", 2),
              ("V", 3), ("X", 3)]
STEPS_ODD = [("S", 0), ("G", 0), ("G", 1), ("T", 0), ("S", 1), ("G", 2), ("V", 0), ("T", 1), ("S", 2), ("X", 0),
             ("G", 3), ("V", 1), ("T", 2), ("S", 3), ("X", 1), ("Y", 0), ("G", 4), ("V", 2), ("T", 3), ("G", 5),
             ("X", 2), ("Y", 1), ("V", 3), ("Y", 2), ("X", 3), ("Y", 3)]
NG = 6
NK = S + 1
NKP = NK + 1


def cross_attention0(core, i):
    nc, ins = core.nc, core.ins
    name = f"L0_xattn_%s{i}"
    wq, wk, wv, wo = (ins[name % w] for w in ("wq", "wk", "wv", "wo"))
    with core.stage(f"a{i}") as st:
        h_hi, h_lo = st.sb("h_hi", [P, KT, T], F32R), st.sb("h_lo", [P, KT, T], F32R)
        c_hi, c_lo = st.sb("c_hi", [P, KT, T], F32R), st.sb("c_lo", [P, KT, T], F32R)
        wqk_raw, wo_raw = st.sb("wqk_raw", [P, 2, KT, K0]), st.sb("wo_raw", [P, D])
        wqk_hi, wqk_lo = st.sb("wqk_hi", [P, 2, 2, KT, K0], F32R), st.sb("wqk_lo", [P, 2, 2, KT, K0], F32R)
        wv_sb = st.sb("wv_sb", [P, 2, KT, K0])
        wo_hi, wo_lo = st.sb("wo_hi", [P, 2, D], F32R), st.sb("wo_lo", [P, 2, D], F32R)
        q_hi, q_lo = st.sb("q_hi", [P, 2, T], F32R), st.sb("q_lo", [P, 2, T], F32R)
        k_hi, k_lo = st.sb("k_hi", [P, 2, B, NKP], F32R), st.sb("k_lo", [P, 2, B, NKP], F32R)
        v_sb = st.sb("v_sb", [P, 2, TT, K0])
        negmax, den, rden = st.sb("negmax", [P, 2, QT]), st.sb("den", [P, 2, QT]), st.sb("rden", [P, 2, QT])
        prob = st.sb("prob", [P, 2, QT, NKP])
        probT = st.sb("probT", [P, 4 * P])
        vbias = st.sb("vbias", [P, E0])
        bv_row = st.sb("bv_row", [P, E0])
        bias_part = st.sb("bias_part", [P, 2, QT, K0])
        o_sb = st.sb("o_sb", [P, QT, K0])
        oT_hi, oT_lo = st.sb("oT_hi", [P, 2, T], F32R), st.sb("oT_lo", [P, 2, T], F32R)
        bo_row = st.sb("bo_row", [P, D])
        bias_cols = st.sb("bias_cols", [P, 3, H0])
        hc = st.sb("hc", [P, 2, 3])
        vb = st.sb("vb", [P, 2, K0])
        pbn = st.sb("pbn", [P, 2, QT])
        one = st.sb("one", [P, 1])
        bk_hi, bk_lo = st.sb("bk_hi", [P, H0], F32R), st.sb("bk_lo", [P, H0], F32R)
        g_ps, s_ps = st.psum("g_ps", [P, 2, 512]), st.psum("s_ps", [P, QT, 512])
        t_ps, o_ps, x_ps, y_ps = (st.psum(n, [P, 512]) for n in ("t_ps", "o_ps", "x_ps", "y_ps"))

        sems = ("rows_in", "bo_added", "wo_in", "wqk_split", "wo_split", "hi_split", "lo_split", "consts",
                "kbias", "g_done", "g_hi", "qk_out", "v_out", "s_done", "max_done", "exp_done", "rden_done", "bias_done",
                "t_done", "t_out", "v_done", "o_out", "x_done", "x_hi", "x_out", "y_done", "y_out", "raw_hi",
                "zero_set", "vb_done", "head_set", "pbn_done")
        z = type("Semaphores", (), {n: st.sem(n) for n in sems})
        wqk_in, wv_in = st.slot_sems("wqk_in", 2), st.slot_sems("wv_in", 2)
        bq, bk, bkey, bv = (columns(core, name % v) for v in ("bq", "bk", "bias_k", "bv"))

        def pairs(eng, body):
            body(0)
            with eng.Fori(1, H0 // 2 - 1) as p:
                body(p)
            body(H0 // 2 - 1)

        def halves(p):
            last = isinstance(p, int) and p == H0 // 2 - 1
            return [(0, 2 * p, True, not last), (1, 2 * p + 1, not last, not last)]

        def head_cols(h):
            return bass.ds(h * K0, K0)

        with nc.Block() as block:
            @block.sync
            def _(sp):
                for row, src in ((vbias, "bias_v"), (bv_row, "bv"), (bo_row, "bo")):
                    flat = ins[name % src]
                    if len(flat.shape) == 4:
                        flat = flat.rearrange("a b h k -> (a b h k)")
                    sp.dma_start(row[:], flat.rearrange("(o n) -> o n", o=1).broadcast_to([P, flat.shape[0]])
                                 ).then_inc(z.rows_in, 16)

                def load_qkv(h, s):
                    wait(sp, z.wqk_split, 4 * h)
                    for n, w in enumerate((wq, wk)):
                        sp.dma_start(wqk_raw[:, n], w[:, head_cols(h)].rearrange("(t p) n -> p t n", p=P)
                                     ).then_inc(wqk_in[n], 16)
                    wait(sp, z.g_done, NG * (h - 1))
                    sp.dma_start(wv_sb[:, s], wv[:, head_cols(h)].rearrange("(t p) n -> p t n", p=P)
                                 ).then_inc(wv_in[s], 16)

                def load_o(h):
                    wait(sp, z.wo_split, 2 * h)
                    sp.dma_start(wo_raw[:], wo[head_cols(h), :]).then_inc(z.wo_in, 16)

                load_qkv(0, 0)
                load_qkv(1, 1)

                def body(p):
                    for s, h, _, after in halves(p):
                        load_o(h)
                        if after:
                            load_qkv(h + 2, s)
                pairs(sp, body)

            @block.gpsimd
            def _(pool):
                core.clear_used(pool)
                nc.gpsimd.tensor_copy(bk_hi[:], bkey).then_inc(z.raw_hi, 1)
                nc.gpsimd.memset(one[:], 1.0).then_inc(z.zero_set, 1)
                pool.wait_ge(z.zero_set, 1)
                nc.gpsimd.memset(k_hi[:, :, :, NK:NKP].bitcast(F32), 0.0).then_inc(z.zero_set, 1)
                nc.gpsimd.memset(k_lo[:, :, :, NK:NKP].bitcast(F32), 0.0).then_inc(z.zero_set, 1)
                pool.wait_ge(z.raw_hi, 1)
                nc.gpsimd.tensor_tensor(bk_lo[:], bkey, bk_hi[:].bitcast(F32), ALU.subtract).then_inc(z.raw_hi, 1)
                pool.wait_ge(z.raw_hi, 2)

                def split_qk(h, s, n):
                    pool.wait_ge(wqk_in[n], 16 * (h + 1))
                    wait(pool, z.g_done, NG * (h - 1))
                    nc.gpsimd.tensor_tensor(
                        wqk_hi[:, s, n], wqk_raw[:, n], one[:].rearrange("p (a o) -> p a o", a=1)
                        .broadcast_to([P, KT, K0]), ALU.mult).then_inc(z.wqk_split, 1)
                    wait(pool, z.wqk_split, 4 * h + 2 * n + 1)
                    nc.gpsimd.tensor_tensor(wqk_lo[:, s, n], wqk_raw[:, n], wqk_hi[:, s, n].bitcast(F32),
                                            ALU.subtract).then_inc(z.wqk_split, 1)

                def split_o(h, s):
                    wait(pool, z.wo_in, 16 * (h + 1))
                    wait(pool, z.y_done, 2 * (h - s))
                    nc.gpsimd.tensor_tensor(wo_hi[:, s], wo_raw[:], one[:].broadcast_to([P, D]), ALU.mult
                                            ).then_inc(z.wo_split, 1)
                    wait(pool, z.wo_split, 2 * h + 1)
                    nc.gpsimd.tensor_tensor(wo_lo[:, s], wo_raw[:], wo_hi[:, s].bitcast(F32), ALU.subtract
                                            ).then_inc(z.wo_split, 1)

                def key_bias(h, s):
                    wait(pool, z.s_done, B * (h - 1))
                    for part, src in ((k_hi, bk_hi), (k_lo, bk_lo)):
                        nc.gpsimd.tensor_copy(part[:, s, :, S:NK].rearrange("p b o -> p (b o)"),
                                              src[:, bass.ds(h, 1)].bitcast(F32).broadcast_to([P, B])
                                              ).then_inc(z.kbias, 1)

                def bias_part_of(h, s, b):
                    u = B * h + b
                    wait(pool, z.pbn_done, u + 1)
                    wait(pool, z.o_out, 2 * (u - 1))
                    for qt in range(QT):
                        nc.gpsimd.tensor_tensor(bias_part[:, b % 2, qt], vb[:, s],
                                                pbn[:, b % 2, qt:qt + 1].broadcast_to([P, K0]), ALU.mult
                                                ).then_inc(z.bias_done, 1)

                for h in range(2):
                    split_qk(h, h, 0)
                    split_qk(h, h, 1)
                key_bias(0, 0)
                pool.wait_ge(z.vb_done, 1)

                def body(p):
                    for s, h, more, after in halves(p):
                        if more:
                            key_bias(h + 1, 1 - s)
                        bias_part_of(h, s, 0)
                        if after:
                            split_qk(h + 2, s, 0)
                        bias_part_of(h, s, 1)
                        if after:
                            split_qk(h + 2, s, 1)
                        bias_part_of(h, s, 2)
                        split_o(h, s)
                        bias_part_of(h, s, 3)
                pairs(pool, body)

            def k_out(part, s, g):
                return part[:, s, 2 * g:2 * g + 2, 0:S]

            @block.scalar
            def _(act):
                nc.scalar.activation(h_hi[:], core.xT[:], ACT.Copy).then_inc(z.hi_split, 1)
                nc.scalar.activation(c_hi[:], core.cT[:], ACT.Copy).then_inc(z.hi_split, 1)

                def group(h, s, g):
                    if g == 0:
                        act.wait_ge(z.head_set, 2 * (h + 1))
                    act.wait_ge(z.g_done, NG * h + g + 1)
                    ps = g_ps[:, g % 2]
                    if g < 2:
                        nc.scalar.activation(q_hi[:, s, g * 512:(g + 1) * 512], ps, ACT.Identity,
                                             bias=hc[:, s, 0:1]).then_inc(z.g_hi, 1)
                    elif g < 4:
                        nc.scalar.activation(k_out(k_hi, s, g - 2), ps.rearrange("p (b t) -> p b t", t=S),
                                             ACT.Identity, bias=hc[:, s, 1:2]).then_inc(z.g_hi, 1)
                    else:
                        nc.scalar.activation(v_sb[:, s, 4 * (g - 4):4 * (g - 3)], ps.rearrange("p (t d) -> p t d", d=K0),
                                             ACT.Copy).then_inc(z.v_out, 1)

                def step(kind, n, p, s, h, more):
                    u = B * h + n
                    if kind == "S":
                        act.wait_ge(z.max_done, u + 1)
                        wait(act, z.pbn_done, u - 1)
                        for qt in range(QT):
                            nc.scalar.activation(prob[:, n % 2, qt, 0:NK], s_ps[:, qt, 0:NK], ACT.Exp,
                                                 bias=negmax[:, n % 2, qt:qt + 1],
                                                 accum_out=den[:, n % 2, qt:qt + 1]).then_inc(z.exp_done, 1)
                    elif kind == "G" and more:
                        group(h + 1, 1 - s, n)
                    elif kind == "T":
                        act.wait_ge(z.t_done, u + 1)
                        nc.scalar.activation(probT[:], t_ps[:], ACT.Copy).then_inc(z.t_out, 1)
                    elif kind == "X":
                        act.wait_ge(z.x_done, u + 1)
                        nc.scalar.activation(oT_hi[:, s, n * S:(n + 1) * S], x_ps[:, 0:S], ACT.Identity,
                                             bias=hc[:, s, 2:3]).then_inc(z.x_hi, 1)

                for g in range(NG):
                    group(0, 0, g)

                def body(p):
                    for (s, h, more, _), steps in zip(halves(p), (STEPS_EVEN, STEPS_ODD)):
                        for kind, n in steps:
                            step(kind, n, p, s, h, more)
                pairs(act, body)

            @block.vector
            def _(dve):
                nc.vector.tensor_scalar(bias_cols[:, 0], bq, float(K0) ** -0.5, None, ALU.mult).then_inc(z.consts, 1)
                nc.vector.tensor_copy(bias_cols[:, 1], bk).then_inc(z.consts, 1)
                nc.vector.tensor_copy(bias_cols[:, 2], bv).then_inc(z.consts, 1)
                dve.wait_ge(z.rows_in, 48)
                nc.vector.tensor_tensor(vbias[:], vbias[:], bv_row[:], ALU.subtract).then_inc(z.vb_done, 1)
                for t in range(TT):
                    nc.vector.tensor_tensor(core.x[:, t], core.x[:, t], bo_row[:], ALU.add).then_inc(z.bo_added, 1)
                dve.wait_ge(z.hi_split, 1)
                nc.vector.tensor_tensor(h_lo[:], core.xT[:], h_hi[:].bitcast(F32), ALU.subtract).then_inc(z.lo_split, 1)
                dve.wait_ge(z.hi_split, 2)
                nc.vector.tensor_tensor(c_lo[:], core.cT[:], c_hi[:].bitcast(F32), ALU.subtract).then_inc(z.lo_split, 1)
                dve.wait_ge(z.bo_added, TT)
                dve.wait_ge(z.consts, 3)
                dve.wait_ge(z.vb_done, 1)

                def set_head(h, s):
                    wait(dve, z.bias_done, 2 * B * (h - 1))
                    wait(dve, z.x_out, B * (h - 1))
                    nc.vector.tensor_scalar(hc[:, s], bias_cols[:, :, bass.ds(h, 1)].rearrange("p a o -> p (a o)"),
                                            1.0, None, ALU.mult).then_inc(z.head_set, 1)
                    nc.vector.tensor_scalar(vb[:, s], vbias[:, head_cols(h)], 1.0, None, ALU.mult
                                            ).then_inc(z.head_set, 1)

                def group(h, s, g):
                    if g >= 4:
                        return
                    dve.wait_ge(z.g_hi, 4 * h + g + 1)
                    ps = g_ps[:, g % 2]
                    if g < 2:
                        cols = slice(g * 512, (g + 1) * 512)
                        nc.vector.scalar_tensor_tensor(out=q_lo[:, s, cols], in0=ps, scalar=hc[:, s, 0:1],
                                                       in1=q_hi[:, s, cols].bitcast(F32), op0=ALU.add,
                                                       op1=ALU.subtract).then_inc(z.qk_out, 1)
                    else:
                        nc.vector.scalar_tensor_tensor(out=k_out(k_lo, s, g - 2),
                                                       in0=ps.rearrange("p (b t) -> p b t", t=S),
                                                       scalar=hc[:, s, 1:2],
                                                       in1=k_out(k_hi, s, g - 2).bitcast(F32), op0=ALU.add,
                                                       op1=ALU.subtract).then_inc(z.qk_out, 1)

                def step(kind, n, p, s, h, more):
                    u = B * h + n
                    if kind == "S":
                        dve.wait_ge(z.s_done, u + 1)
                        wait(dve, z.exp_done, 2 * (u - 1))
                        nc.vector.tensor_reduce(negmax[:, n % 2], s_ps[:, :, 0:NK], AX.X, ALU.max, negate=True
                                                ).then_inc(z.max_done, 1)
                    elif kind == "G" and more:
                        group(h + 1, 1 - s, n)
                    elif kind == "T":
                        dve.wait_ge(z.exp_done, 2 * (u + 1))
                        wait(dve, z.bias_done, 2 * (u - 1))
                        nc.vector.reciprocal(rden[:, n % 2], den[:, n % 2]).then_inc(z.rden_done, 1)
                        dve.wait_ge(z.rden_done, u + 1)
                        nc.vector.tensor_tensor(pbn[:, n % 2], prob[:, n % 2, :, S], rden[:, n % 2], ALU.mult
                                                ).then_inc(z.pbn_done, 1)
                    elif kind == "V":
                        dve.wait_ge(z.v_done, u + 1)
                        dve.wait_ge(z.bias_done, 2 * (u + 1))
                        wait(dve, z.x_done, u)
                        for qt in range(QT):
                            nc.vector.scalar_tensor_tensor(out=o_sb[:, qt], in0=o_ps[:, qt * K0:(qt + 1) * K0],
                                                           scalar=rden[:, n % 2, qt:qt + 1],
                                                           in1=bias_part[:, n % 2, qt], op0=ALU.mult,
                                                           op1=ALU.add).then_inc(z.o_out, 1)
                    elif kind == "X":
                        dve.wait_ge(z.x_hi, u + 1)
                        cols = slice(n * S, (n + 1) * S)
                        nc.vector.scalar_tensor_tensor(out=oT_lo[:, s, cols], in0=x_ps[:, 0:S],
                                                       scalar=hc[:, s, 2:3],
                                                       in1=oT_hi[:, s, cols].bitcast(F32), op0=ALU.add,
                                                       op1=ALU.subtract).then_inc(z.x_out, 1)
                    elif kind == "Y":
                        y = 4 * p + n
                        dve.wait_ge(z.y_done, y + 1)
                        wait(dve, z.y_out, y - 3)
                        xb = core.x[:, QT * n:QT * n + QT]
                        nc.vector.tensor_tensor(xb, y_ps[:].rearrange("p (t d) -> p t d", d=D), xb, ALU.add
                                                ).then_inc(z.y_out, 1)

                set_head(0, 0)
                dve.wait_ge(z.head_set, 2)
                for g in range(NG):
                    group(0, 0, g)

                def body(p):
                    for (s, h, more, _), steps in zip(halves(p), (STEPS_EVEN, STEPS_ODD)):
                        if more:
                            set_head(h + 1, 1 - s)
                            dve.wait_ge(z.head_set, 2 * (h + 2))
                        for kind, n in steps:
                            step(kind, n, p, s, h, more)
                pairs(dve, body)

            @block.tensor
            def _(pe):
                def product(out, left, right, start=True, stop=True):
                    (a_hi, a_lo), (b_hi, b_lo) = left, right
                    nc.tensor.matmul(out, a_hi, b_hi, start=start, stop=False)
                    nc.tensor.matmul(out, a_hi, b_lo, start=False, stop=False)
                    return nc.tensor.matmul(out, a_lo, b_hi, start=False, stop=stop)

                def group(h, s, g, use):
                    if g < 2:
                        wait(pe, z.v_out, 2 * h - 1 + g)
                    else:
                        pe.wait_ge(z.qk_out, 4 * h + g - 1)
                    if g == 0:
                        pe.wait_ge(z.wqk_split, 4 * h + 4)
                    if g == 4:
                        pe.wait_ge(wv_in[s], 16 * (use + 1))
                    if g < 4:
                        n, cols = g // 2, slice(g % 2 * 512, (g % 2 + 1) * 512)
                        src = ((h_hi, h_lo), (c_hi, c_lo))[n]
                        for kt in range(KT):
                            mm = product(g_ps[:, g % 2], (wqk_hi[:, s, n, kt], wqk_lo[:, s, n, kt]),
                                         (src[0][:, kt, cols], src[1][:, kt, cols]), kt == 0, kt == KT - 1)
                    else:
                        for j in range(4):
                            t = 4 * (g - 4) + j
                            for kt in range(KT):
                                mm = nc.tensor.matmul(g_ps[:, g % 2, j * K0:(j + 1) * K0],
                                                      core.cT[:, kt, t * P:(t + 1) * P], wv_sb[:, s, kt],
                                                      start=(kt == 0), stop=(kt == KT - 1))
                    mm.then_inc(z.g_done, 1)

                def step(kind, n, p, s, h, more):
                    u = B * h + n
                    if kind == "S":
                        if n == 0:
                            pe.wait_ge(z.qk_out, 4 * (h + 1))
                            pe.wait_ge(z.kbias, 2 * (h + 1))
                        wait(pe, z.exp_done, 2 * u)
                        for qt in range(QT):
                            cols = slice(n * S + qt * P, n * S + (qt + 1) * P)
                            mm = product(s_ps[:, qt, 0:NKP], (q_hi[:, s, cols], q_lo[:, s, cols]),
                                         (k_hi[:, s, n], k_lo[:, s, n]))
                        mm.then_inc(z.s_done, 1)
                    elif kind == "G" and more:
                        group(h + 1, 1 - s, n, p + s)
                    elif kind == "T":
                        pe.wait_ge(z.exp_done, 2 * (u + 1))
                        wait(pe, z.t_out, u)
                        for kt in range(QT):
                            for qt in range(QT):
                                at = (kt * QT + qt) * P
                                mm = nc.tensor.transpose(t_ps[:, at:at + P], prob[:, n % 2, qt, kt * P:(kt + 1) * P],
                                                         core.ident[:])
                        mm.then_inc(z.t_done, 1)
                    elif kind == "V":
                        pe.wait_ge(z.t_out, u + 1)
                        if n == 0:
                            pe.wait_ge(z.v_out, 2 * (h + 1))
                        wait(pe, z.o_out, 2 * u)
                        for qt in range(QT):
                            for kt in range(QT):
                                at = (kt * QT + qt) * P
                                mm = nc.tensor.matmul(o_ps[:, qt * K0:(qt + 1) * K0], probT[:, at:at + P],
                                                      v_sb[:, s, QT * n + kt], start=(kt == 0), stop=(kt == QT - 1))
                        mm.then_inc(z.v_done, 1)
                    elif kind == "X":
                        pe.wait_ge(z.o_out, 2 * (u + 1))
                        wait(pe, z.x_out, u)
                        for qt in range(QT):
                            mm = nc.tensor.transpose(x_ps[:, qt * P:(qt + 1) * P], o_sb[:, qt], core.ident[:])
                        mm.then_inc(z.x_done, 1)
                    elif kind == "Y":
                        pe.wait_ge(z.x_out, u + 1)
                        pe.wait_ge(z.wo_split, 2 * (h + 1))
                        wait(pe, z.y_out, 4 * p + n)
                        for qt in range(QT):
                            cols = slice(n * S + qt * P, n * S + (qt + 1) * P)
                            for w in range(2):
                                mm = product(y_ps[:, qt * D:(qt + 1) * D], (oT_hi[:, w, cols], oT_lo[:, w, cols]),
                                             (wo_hi[:, w], wo_lo[:, w]), w == 0, w == 1)
                        mm.then_inc(z.y_done, 1)

                pe.wait_ge(z.hi_split, 2)
                pe.wait_ge(z.lo_split, 2)
                pe.wait_ge(z.zero_set, 3)
                for g in range(NG):
                    group(0, 0, g, 0)

                def body(p):
                    for (s, h, more, _), steps in zip(halves(p), (STEPS_EVEN, STEPS_ODD)):
                        for kind, n in steps:
                            step(kind, n, p, s, h, more)
                pairs(pe, body)


def mlp(core, name, w1, b1, w2, b2, gelu, out=None):
    nc, ins = core.nc, core.ins
    with core.stage(name) as st:
        w1_sb, w2_sb = st.sb("w1", [P, KT, F]), st.sb("w2", [P, FT, D])
        b2_row = st.sb("b2_row", [P, D])
        hid = st.sb("hid", [P, FT, T])
        h_ps, y_ps = st.psum("h_ps", [P, 4, 512]), st.psum("y_ps", [P, 4, 512])
        w1_in, w2_in, b2_in, h_done, h_out, y_done, y_out, x_ready, stored = [
            st.sem(n) for n in ("w1_in", "w2_in", "b2_in", "h_done", "h_out", "y_done", "y_out", "x_ready", "stored")]
        with nc.Block() as block:
            @block.gpsimd
            def _(pool):
                core.clear_used(pool)

            @block.sync
            def _(sp):
                sp.dma_start(w1_sb[:], ins[w1].rearrange("(t p) f -> p t f", p=P)).then_inc(w1_in, 16)
                sp.dma_start(w2_sb[:], ins[w2].rearrange("(t p) d -> p t d", p=P)).then_inc(w2_in, 16)
                sp.dma_start(b2_row[:], ins[b2].rearrange("(o n) -> o n", o=1).broadcast_to([P, D])).then_inc(b2_in, 16)
                if out is not None:
                    dst = out.rearrange("b (t p) d -> p (b t) d", p=P)
                    for t in range(TT):
                        sp.wait_ge(y_out, t + 1)
                        sp.dma_start(dst[:, t], core.x[:, t]).then_inc(stored, 16)
                    sp.wait_ge(stored, 16 * TT)

            @block.tensor
            def _(pe):
                pe.wait_ge(w1_in, 16)
                for n in range(2 * FT):
                    half, f = n // FT, n % FT
                    if n >= 4:
                        pe.wait_ge(h_out, n - 3)
                    for kt in range(KT):
                        mm = nc.tensor.matmul(h_ps[:, n % 4], w1_sb[:, kt, f * P:(f + 1) * P],
                                              core.xT[:, kt, half * 512:(half + 1) * 512],
                                              start=(kt == 0), stop=(kt == KT - 1))
                    mm.then_inc(h_done, 1)
                pe.wait_ge(w2_in, 16)
                for t in range(TT):
                    pe.wait_ge(h_out, FT * (t // 4 + 1))
                    if t >= 4:
                        pe.wait_ge(y_out, t - 3)
                    for f in range(FT):
                        mm = nc.tensor.matmul(y_ps[:, t % 4, 0:D], hid[:, f, t * P:(t + 1) * P], w2_sb[:, f],
                                              start=(f == 0), stop=(f == FT - 1))
                    mm.then_inc(y_done, 1)

            @block.scalar
            def _(act):
                for n in range(2 * FT):
                    half, f = n // FT, n % FT
                    act.wait_ge(h_done, n + 1)
                    nc.scalar.activation(hid[:, f, half * 512:(half + 1) * 512], h_ps[:, n % 4], gelu,
                                         bias=columns(core, b1)[:, f:f + 1]).then_inc(h_out, 1)

            @block.vector
            def _(dve):
                dve.wait_ge(b2_in, 16)
                for t in range(TT):
                    nc.vector.tensor_tensor(core.x[:, t], core.x[:, t], b2_row[:], ALU.add).then_inc(x_ready, 1)
                for t in range(TT):
                    dve.wait_ge(y_done, t + 1)
                    dve.wait_ge(x_ready, t + 1)
                    nc.vector.tensor_tensor(core.x[:, t], y_ps[:, t % 4, 0:D], core.x[:, t], ALU.add).then_inc(y_out, 1)


U = 4


class Small:

    def __init__(self, layer):
        self.layer, self.grouped = layer, layer == 2
        self.HD = 8 if self.grouped else 16
        self.NQ = 8 if self.grouped else 4
        self.quads = B * self.NQ
        self.kheads = 1 if self.grouped else 4
        self.NK = S if self.grouped else 2 * S
        self.NKT = self.NK // P
        self.W = 4 * self.HD
        self.VW = self.kheads * self.HD
        self.scale = self.HD ** -0.5 if self.grouped else 1.0 / self.HD
        self.MASK_ROW, self.MAX_ROW = 3 * self.HD, P - 1


def small_projections(core, c, q_stack, k_stack, v_all, q_st, k_st, v_st):
    nc, ins, L = core.nc, core.ins, c.layer
    with core.stage(f"p{L}") as st:
        KW = 64 if c.grouped else D
        wq = st.sb("wq", [P, KT, D])
        wkv = st.sb("wkv", [P, KT, 2 * KW])
        bv_row = st.sb("bv_row", [P, 2 * KW])
        ones = st.sb("ones", [1, 512])
        n_k = c.NK // S
        KM = 1 if c.grouped else KT
        KP = 64 if c.grouped else P
        q_f, q_hi, q_lo = (st.sb("q_f", [P, KT, T]), st.sb("q_hi", [P, KT, T], F32R), st.sb("q_lo", [P, KT, T], F32R))
        k_f = st.sb("k_f", [KP, KM, B, n_k, S])
        k_hi, k_lo = st.sb("k_hi", [KP, KM, B, n_k, S], F32R), st.sb("k_lo", [KP, KM, B, n_k, S], F32R)
        qk_ps, v_ps = st.psum("qk_ps", [P, 4, 512]), st.psum("v_ps", [P, 4, 512])
        w_in, bv_in, qk_done, qk_f, qk_hi, qk_lo, v_done, v_out, stored, qs = [
            st.sem(n) for n in ("w_in", "bv_in", "qk_done", "qk_f", "qk_hi", "qk_lo", "v_done", "v_out", "stored",
                                "qs")]
        ones_set, stacks_zero, v_zero, rows_in = [st.sem(n) for n in ("ones_set", "stacks_zero", "v_zero", "rows_in")]
        bq = columns(core, f"L{L}_xattn_bq" if c.grouped else f"L{L}_xattn_q_b")
        bk = columns(core, f"L{L}_xattn_bk" if c.grouped else f"L{L}_kv_b_k")
        if c.grouped:
            k_cols = lambda kt, m: wkv[:, kt, 0:KW]
            v_cols = lambda kt: wkv[:, kt, KW:2 * KW]
            v_bias = bv_row[:, 0:KW]
        else:
            kv = wkv[:].rearrange("p t (n two) -> p t n two", two=2)
            k_cols = lambda kt, m: kv[:, kt, m * P:(m + 1) * P, 0]
            v_cols = lambda kt: kv[:, kt, :, 1]
            v_bias = bv_row[:].rearrange("p (n two) -> p n two", two=2)[:, :, 1]
        groups = [(False, m, 0, half) for m in range(KT) for half in range(2)]
        groups += [(True, m, src, half) for m in range(KM) for src in range(n_k) for half in range(2)]
        tiles = [(src, t) for src in range(n_k) for t in range(TT)]

        def places(part_q, part_k, g):
            is_k, m, src, half = groups[g]
            if is_k:
                return part_k[:, m, 2 * half:2 * half + 2, src, :]
            return part_q[:, m, half * 512:(half + 1) * 512]

        def stores(part, is_k):
            if is_k:
                for m in range(KM):
                    dst = k_stack[part].rearrange("(b c) t -> c b t", b=B)[m * KP:(m + 1) * KP]
                    yield dst, (k_hi, k_lo)[part][:, m].rearrange("p b s t -> p b (s t)")
            else:
                for m in range(KT):
                    dst = q_stack[part].rearrange("(b c) t -> c b t", b=B)[m * P:(m + 1) * P]
                    yield dst, (q_hi, q_lo)[part][:, m].rearrange("p (b t) -> p b t", b=B)

        with nc.Block() as block:
            @block.gpsimd
            def _(pool):
                core.clear_used(pool)
                nc.gpsimd.memset(ones[:], 1.0).then_inc(ones_set, 1)
                nc.gpsimd.memset(v_st[:], 0.0).then_inc(v_zero, 1)
                nc.gpsimd.memset(q_st[:].bitcast(F32), 0.0).then_inc(stacks_zero, 1)
                nc.gpsimd.memset(k_st[:].bitcast(F32), 0.0).then_inc(stacks_zero, 1)
                pool.wait_ge(v_zero, 1)
                nc.gpsimd.memset(v_st[:, :, :, :, c.HD:c.HD + 1], 1.0)

            @block.sync
            def _(sp):
                view = "(t p) n -> p t n"
                sp.dma_start(wq[:], ins[f"L{L}_xattn_Wq" if c.grouped else f"L{L}_xattn_q_w"].rearrange(view, p=P)
                             ).then_inc(w_in, 16)
                if c.grouped:
                    sp.dma_start(wkv[:, :, 0:KW], ins["L2_xattn_Wk"].rearrange(view, p=P)).then_inc(w_in, 16)
                    sp.dma_start(wkv[:, :, KW:], ins["L2_xattn_Wv"].rearrange(view, p=P)).then_inc(w_in, 16)
                    sp.dma_start(bv_row[:, 0:KW], ins["L2_xattn_bv"].rearrange("(o n) -> o n", o=1)
                                 .broadcast_to([P, KW])).then_inc(bv_in, 16)
                else:
                    sp.dma_start(wkv[:], ins[f"L{L}_xattn_kv_w"].rearrange(view, p=P)).then_inc(w_in, 16)
                    sp.dma_start(bv_row[:], ins[f"L{L}_xattn_kv_b"].rearrange("(o n) -> o n", o=1)
                                 .broadcast_to([P, 2 * KW])).then_inc(bv_in, 16)
                sp.wait_ge(ones_set, 1)
                sp.wait_ge(stacks_zero, 2)
                row = ones[:].rearrange("o (a n) -> o a n", a=1)
                if not c.grouped:
                    m = c.MASK_ROW
                    sp.dma_start(q_st[m:m + 1].bitcast(F32).rearrange("o u j t -> o (u j t)").rearrange(
                        "o (a n) -> o a n", n=512), row.broadcast_to([1, U * 2, 512])).then_inc(rows_in, 16)
                m = c.MAX_ROW
                sp.dma_start(k_st[m:m + 1].bitcast(F32).rearrange("o u j t -> o (u j t)").rearrange(
                    "o (a n) -> o a n", n=256), row[:, :, 0:256].broadcast_to([1, U * c.kheads * c.NK // 256, 256])
                    ).then_inc(rows_in, 16)
                n = 0
                for is_k, until in ((False, 4), (True, len(groups))):
                    for part in range(2):
                        sp.wait_ge((qk_hi, qk_lo)[part], until)
                        for dst, src in stores(part, is_k):
                            sp.dma_start(dst, src.bitcast(F32)).then_inc(stored, 16)
                            n += 1
                sp.wait_ge(stored, 16 * n)
                sp.wait_ge(rows_in, 16 if c.grouped else 32)

            @block.tensor
            def _(pe):
                pe.wait_ge(w_in, 48 if c.grouped else 32)
                for g, (is_k, m, src, half) in enumerate(groups):
                    if g >= 4:
                        pe.wait_ge(qk_f, g - 3)
                    rhs = core.xT if not is_k or src else core.cT
                    for kt in range(KT):
                        lhs = k_cols(kt, m) if is_k else wq[:, kt, m * P:(m + 1) * P]
                        mm = nc.tensor.matmul(qk_ps[0:KP if is_k else P, g % 4], lhs,
                                              rhs[:, kt, half * 512:(half + 1) * 512],
                                              start=(kt == 0), stop=(kt == KT - 1))
                    mm.then_inc(qk_done, 1)
                for n, (src, t) in enumerate(tiles):
                    if n >= 4:
                        pe.wait_ge(v_out, n - 3)
                    lhs = (core.cT, core.xT)[src]
                    for kt in range(KT):
                        mm = nc.tensor.matmul(v_ps[:, n % 4, 0:KW], lhs[:, kt, t * P:(t + 1) * P], v_cols(kt),
                                              start=(kt == 0), stop=(kt == KT - 1))
                    mm.then_inc(v_done, 1)

            @block.vector
            def _(dve):
                for g, (is_k, m, src, half) in enumerate(groups):
                    dve.wait_ge(qk_done, g + 1)
                    ps, out = qk_ps[0:KP if is_k else P, g % 4], places(q_f, k_f, g)
                    if is_k:
                        nc.vector.tensor_scalar(out, ps.rearrange("p (b t) -> p b t", t=S), bk[0:KP, m:m + 1], None,
                                                ALU.add).then_inc(qk_f, 1)
                    else:
                        nc.vector.tensor_scalar(out, ps, bq[:, m:m + 1], c.scale, ALU.add, ALU.mult
                                                ).then_inc(qk_f, 1)
                    if g:
                        dve.wait_ge(qk_hi, g)
                        nc.vector.tensor_tensor(places(q_lo, k_lo, g - 1), places(q_f, k_f, g - 1),
                                                places(q_hi, k_hi, g - 1).bitcast(F32), ALU.subtract
                                                ).then_inc(qk_lo, 1)
                dve.wait_ge(qk_hi, len(groups))
                g = len(groups) - 1
                nc.vector.tensor_tensor(places(q_lo, k_lo, g), places(q_f, k_f, g),
                                        places(q_hi, k_hi, g).bitcast(F32), ALU.subtract).then_inc(qk_lo, 1)
                dve.wait_ge(bv_in, 16)
                for n, (src, t) in enumerate(tiles):
                    dve.wait_ge(v_done, n + 1)
                    b, kt = t // QT, QT * src + t % QT
                    out = v_all[:, b * c.NQ:(b + 1) * c.NQ, kt, :]
                    nc.vector.tensor_tensor(out, v_ps[:, n % 4, 0:KW].rearrange("p (g w) -> p g w", w=c.VW),
                                            v_bias.rearrange("p (g w) -> p g w", w=c.VW), ALU.add).then_inc(v_out, 1)

            @block.scalar
            def _(act):
                for g in range(len(groups)):
                    act.wait_ge(qk_f, g + 1)
                    nc.scalar.activation(places(q_hi, k_hi, g), places(q_f, k_f, g), ACT.Copy).then_inc(qk_hi, 1)


def small_attention(core, c, q_stack, k_stack, v_all, o_all, q_st, k_st, v_st):
    nc, L = core.nc, c.layer
    HD, NKT, KH = c.HD, c.NKT, c.kheads
    NM = 8
    NS = 4 if c.grouped else 8
    NE = 2 if c.grouped else 4
    LQ, LK = 3, 3 if c.grouped else 4
    if c.grouped:
        steps = [("S", 0), ("E", 0), ("S", 1), ("P", 0), ("M", 0), ("S", 2), ("P", 1), ("E", 1), ("S", 3), ("X", 0)]
    else:
        steps = [("S", 0), ("E", 0), ("S", 1), ("P", 0), ("S", 2), ("P", 1), ("M", 0), ("S", 3), ("E", 1), ("P", 2),
                 ("S", 4), ("P", 3), ("S", 5), ("E", 2), ("X", 0), ("S", 6), ("S", 7), ("E", 3)]

    def turned(i):
        return not isinstance(i, int) or 1 <= i <= c.quads

    def iterations(body):
        def flags(i):
            return i < c.quads, 2 <= i <= c.quads + 1, i >= 3

        def run(eng):
            loops = (c.quads - 2 - U) // U
            for i in range(U):
                body(i // U, i, i % U, *flags(i), i + 2 < c.quads)
            with eng.Fori(1, 1 + loops) as r:
                for s in range(U):
                    body(r, U * r + s, s, True, True, True, True)
            for i in range(U * (1 + loops), c.quads + 3):
                body(i // U, i, i % U, *flags(i), i + 2 < c.quads)
        return run

    with core.stage(f"s{L}") as st:
        mx = st.sb("mx", [P, U, NM])
        mxT = st.sb("mxT", [NM, U, P], F32R)
        probT = st.sb("probT", [P, U, NE, 2 * 512])
        oT = st.sb("oT", [P, S])
        rden = st.sb("rden", [P, QT, 4])
        s_ps = st.psum("s_ps", [P, 2, 512])
        st_ps = st.psum("st_ps", [P, 4, 512])
        o_ps, x_ps = st.psum("o_ps", [P, 512]), st.psum("x_ps", [P, 512])
        names = ("v_in", "s_done", "max_done",
                 "mx_turned", "mx_out", "row_in", "st_done", "exp_done", "o_done", "o_out", "x_done", "rden_done",
                 "x_out", "mask_in", "mask_turned", "mask_hi", "mask_lo", "mask_set")
        z = type("Semaphores", (), {n: st.sem(n) for n in names})
        q_in, k_in = st.slot_sems("q_in", U), st.slot_sems("k_in", U)
        if c.grouped:
            mask = st.sb("mask", [P, B * QT, S])
            mT_hi, mT_lo = st.sb("mT_hi", [P, B, NKT, S], F32R), st.sb("mT_lo", [P, B, NKT, S], F32R)
            ident_r = st.sb("ident_r", [P, P], F32R)
            masked = st.sb("masked", [P, 2, 2, S])
            carrier = st.sb("carrier", [P, NS])
            mask_st = st.sb("mask_st", [P, U, QT, S])

        def prob_of(slot, j, kt):
            e, at = (kt, j * S) if c.grouped else (j, kt * S)
            return probT[:, slot, e, at:at + S]

        with nc.Block() as block:
            @block.sync
            def _(sp):
                if c.grouped:
                    sp.dma_start(mask[:], core.ins["mask_Bx1xSxS2_ff0"].rearrange("b o (t p) k -> p (b o t) k", p=P)
                                 ).then_inc(z.mask_in, 16)

                def load(i, s):
                    wait(sp, z.st_done, NE * (i - 3))
                    for n, part in enumerate((0, 0, 1)):
                        sp.dma_start(q_st[n * HD:(n + 1) * HD, s].bitcast(F32),
                                     q_stack[part, bass.ds(i * c.W, c.W), :].rearrange("(j d) t -> d j t", d=HD)
                                     ).then_inc(q_in[s], 16)
                    for n, part in enumerate((0, 1, 0)):
                        sp.dma_start(k_st[n * HD:(n + 1) * HD, s].bitcast(F32),
                                     k_stack[part, bass.ds(i * c.VW, c.VW), :].rearrange("(j d) t -> d j t", d=HD)
                                     ).then_inc(k_in[s], 16)
                    if not c.grouped:
                        m = c.MASK_ROW
                        sp.dma_start(k_st[m:m + 1, s].bitcast(F32),
                                     core.maskrow[bass.ds(i // c.NQ, 1), :].rearrange("b (o t) -> b o t", o=1)
                                     .broadcast_to([1, KH, c.NK])).then_inc(k_in[s], 16)

                load(0, 0)
                load(1, 1)

                def body(r, i, s, st1, st2, st3, ahead):
                    if turned(i):
                        sp.wait_ge(z.mx_out, i)
                        m, s1 = c.MAX_ROW, (s + 3) % U
                        sp.dma_start(q_st[m:m + 1, s1].bitcast(F32).rearrange("o j (t n) -> o (j t) n", n=P),
                                     mxT[:, s1].bitcast(F32)).then_inc(z.row_in, 16)
                    if ahead:
                        load(i + 2, (s + 2) % U)
                iterations(body)(sp)

            @block.gpsimd
            def _(pool):
                core.clear_used(pool)
                if c.grouped:
                    pool.wait_ge(z.mask_in, 16)

                def body(r, i, s, st1, st2, st3, ahead):
                    if st1:
                        if c.grouped:
                            wait(pool, z.max_done, NM * (i - 3))
                            nc.gpsimd.tensor_copy(mask_st[:, s], mask[:, bass.ds((i // c.NQ) * QT, QT)]
                                                  ).then_inc(z.mask_set, 1)
                        wait(pool, z.o_done, i - 3)
                        src = v_all[:, bass.ds(i, 1)].rearrange("p o k (j d) -> p (o k) j d", d=HD)
                        nc.gpsimd.tensor_copy(v_st[:, s, :, :, 0:HD], src).then_inc(z.v_in, 1)
                iterations(body)(pool)

            @block.scalar
            def _(act):
                if c.grouped:
                    for b in range(B):
                        act.wait_ge(z.mask_turned, b + 1)
                        nc.scalar.activation(mT_hi[:, b].rearrange("p k t -> p (k t)"), st_ps[:, b], ACT.Copy
                                             ).then_inc(z.mask_hi, 1)

                def step(kind, n, i, s, st1, st2, st3):
                    if kind == "X" and st3:
                        act.wait_ge(z.o_done, i - 2)
                        wait(act, z.x_done, i - 3)
                        nc.scalar.activation(oT[:], o_ps[:, 0:S], ACT.Copy).then_inc(z.o_out, 1)
                    elif kind == "E" and st2:
                        act.wait_ge(z.st_done, NE * (i - 2) + n + 1)
                        nc.scalar.activation(probT[:, (s + 2) % U, n],
                                             st_ps[:, 2 * (n % 2):2 * (n % 2) + 2].rearrange("p k t -> p (k t)"),
                                             ACT.Exp).then_inc(z.exp_done, 1)

                def body(r, i, s, st1, st2, st3, ahead):
                    for kind, n in steps:
                        if kind == "E":
                            step(kind, n, i, s, st1, st2, st3)
                        if kind == "P" and n == NKT - 1:
                            step("X", 0, i, s, st1, st2, st3)
                iterations(body)(act)

            @block.vector
            def _(dve):
                if c.grouped:
                    nc.vector.tensor_copy(ident_r[:], core.ident[:]).then_inc(z.mask_lo, 1)
                    for b in range(B):
                        dve.wait_ge(z.mask_hi, b + 1)
                        nc.vector.tensor_tensor(mT_lo[:, b].rearrange("p k t -> p (k t)"), st_ps[:, b],
                                                mT_hi[:, b].bitcast(F32).rearrange("p k t -> p (k t)"), ALU.subtract
                                                ).then_inc(z.mask_lo, 1)

                def maxima(n, i, s):
                    if c.grouped:
                        wait(dve, z.max_done, NM * i + 2 * n - 2)
                    dve.wait_ge(z.s_done, NS * i + n + 1)
                    if not c.grouped:
                        nc.vector.tensor_reduce(mx[:, s, n:n + 1], s_ps[:, n % 2, 0:c.NK], AX.X, ALU.max
                                                ).then_inc(z.max_done, 1)
                        return
                    qt, pair = n % 2, n // 2
                    if n == 0:
                        dve.wait_ge(z.mask_set, i + 1)
                    nc.vector.memset(carrier[:, n:n + 1], 0.0)
                    for jj in range(2):
                        m = QT * (2 * pair + jj) + qt
                        nc.vector.tensor_tensor_reduce(
                            out=masked[:, n % 2, jj], in0=s_ps[:, n % 2, jj * S:(jj + 1) * S],
                            in1=mask_st[:, s, qt],
                            scale=1.0, scalar=-3.0e38, op0=ALU.add, op1=ALU.max,
                            accum_out=mx[:, s, m:m + 1]).then_inc(z.max_done, 1)

                def outputs(i):
                    dve.wait_ge(z.x_done, i - 2)
                    wait(dve, z.x_out, QT * (i - 3))
                    xv = x_ps[:, 0:S].rearrange("p (t j w) -> p t j w", t=QT, j=4)
                    nc.vector.reciprocal(rden[:], xv[:, :, :, HD]).then_inc(z.rden_done, 1)
                    dve.wait_ge(z.rden_done, i - 2)
                    for qt in range(QT):
                        nc.vector.tensor_tensor(
                            o_all[:, bass.ds((i - 3) // c.NQ, 1), qt, bass.ds((i - 3) % c.NQ, 1)].rearrange(
                                "p b g (j d) -> p (b g j) d", d=HD),
                            xv[:, qt, :, 0:HD], rden[:, qt].rearrange("p (j o) -> p j o", o=1)
                            .broadcast_to([P, 4, HD]), ALU.mult).then_inc(z.x_out, 1)

                def body(r, i, s, st1, st2, st3, ahead):
                    if st1:
                        wait(dve, z.mx_turned, i - 3)
                    for kind, n in steps:
                        if kind == "S" and st1:
                            maxima(n, i, s)
                        if kind == "X" and st3:
                            outputs(i)
                        if kind == "M" and turned(i):
                            dve.wait_ge(z.mx_turned, i)
                            wait(dve, z.row_in, 16 * (i - 3))
                            nc.vector.tensor_scalar(mxT[:, (s + 3) % U], x_ps[0:NM, S:S + P], -1.0, None, ALU.mult
                                                    ).then_inc(z.mx_out, 1)
                iterations(body)(dve)

            @block.tensor
            def _(pe):
                if c.grouped:
                    pe.wait_ge(z.mask_in, 16)
                    for b in range(B):
                        for kt in range(NKT):
                            for qt in range(QT):
                                at = kt * S + qt * P
                                mm = nc.tensor.transpose(st_ps[:, b, at:at + P],
                                                         mask[:, b * QT + qt, kt * P:(kt + 1) * P], core.ident[:])
                        mm.then_inc(z.mask_turned, 1)
                    pe.wait_ge(z.mask_lo, B + 1)

                def scores(n, i, s, r):
                    if n == 0:
                        pe.wait_ge(q_in[s], 16 * LQ * (r + 1))
                        pe.wait_ge(k_in[s], 16 * LK * (r + 1))
                    wait(pe, z.max_done, NM // NS * (NS * i + n - 1))
                    m = c.MAX_ROW
                    if c.grouped:
                        qt, pair = n % 2, n // 2
                        for jj in range(2):
                            mm = nc.tensor.matmul(s_ps[:, n % 2, jj * S:(jj + 1) * S],
                                                  q_st[0:m, s, 2 * pair + jj, qt * P:(qt + 1) * P], k_st[0:m, s, 0],
                                                  start=True, stop=True)
                    else:
                        j, qt = n // 2, n % 2
                        mm = nc.tensor.matmul(s_ps[:, n % 2], q_st[0:m, s, j, qt * P:(qt + 1) * P], k_st[0:m, s, j],
                                              start=True, stop=True)
                    mm.then_inc(z.s_done, 1)

                def shifted(n, i, s):
                    if n == 0:
                        pe.wait_ge(z.row_in, 16 * (i - 1))
                    wait(pe, z.exp_done, NE * (i - 2) + n - 1)
                    for h in range(2):
                        out = st_ps[:, 2 * (n % 2) + h]
                        if c.grouped:
                            mm = nc.tensor.matmul(out, k_st[:, s, 0, n * P:(n + 1) * P],
                                                  q_st[:, s, 2 * h:2 * h + 2].rearrange("p j t -> p (j t)"),
                                                  start=True, stop=False)
                            for part in (mT_hi, mT_lo):
                                rhs = part[:, bass.ds((i - 2) // c.NQ, 1), n].broadcast_to([P, 2, S])
                                mm = nc.tensor.matmul(out, ident_r[:], rhs, start=False, stop=(part is mT_lo))
                        else:
                            for k in range(2):
                                kt = 2 * h + k
                                mm = nc.tensor.matmul(out[:, k * S:(k + 1) * S],
                                                      k_st[:, s, n, kt * P:(kt + 1) * P], q_st[:, s, n],
                                                      start=True, stop=True)
                    mm.then_inc(z.st_done, 1)

                def values(kt, i, s):
                    if kt == 0:
                        pe.wait_ge(z.exp_done, NE * (i - 2))
                        pe.wait_ge(z.v_in, i - 2)
                        wait(pe, z.o_out, i - 3)
                    for j in range(4):
                        mm = nc.tensor.matmul(o_ps[32 * j:32 * j + 32, 0:S], v_st[:, s, kt, j % KH],
                                              prob_of(s, j, kt), start=(kt == 0), stop=(kt == NKT - 1))
                    if kt == NKT - 1:
                        mm.then_inc(z.o_done, 1)

                def body(r, i, s, st1, st2, st3, ahead):
                    for kind, n in steps:
                        if kind == "S" and st1:
                            scores(n, i, s, r)
                        elif kind == "E" and st2:
                            shifted(n, i, (s + 2) % U)
                        elif kind == "P" and st3:
                            values(n, i, (s + 1) % U)
                        elif kind == "X" and st3:
                            pe.wait_ge(z.o_out, i - 2)
                            wait(pe, z.mx_out, min(i, c.quads) if isinstance(i, int) else i)
                            wait(pe, z.x_out, QT * (i - 3))
                            for qt in range(QT):
                                mm = nc.tensor.transpose(x_ps[:, qt * P:(qt + 1) * P], oT[:, qt * P:(qt + 1) * P],
                                                         core.ident[:])
                            mm.then_inc(z.x_done, 1)
                        elif kind == "M" and turned(i):
                            pe.wait_ge(z.max_done, NM * i)
                            wait(pe, z.x_out, QT * (i - 3))
                            wait(pe, z.mx_out, i - 1)
                            nc.tensor.transpose(x_ps[0:NM, S:S + P], mx[:, (s + 3) % U], core.ident[:]).then_inc(z.mx_turned, 1)
                iterations(body)(pe)


def project_out(core, name, c, o_all, wo, bo, dst):
    nc, ins = core.nc, core.ins
    with core.stage(name) as st:
        w_sb, b_row = st.sb("w", [P, KT, D]), st.sb("b_row", [P, D])
        t_ps, y_ps = st.psum("t_ps", [P, 4, 512]), st.psum("y_ps", [P, 4, 512])
        w_in, b_in, turned, t_out, x_ready, y_done, y_out = [
            st.sem(n) for n in ("w_in", "b_in", "turned", "t_out", "x_ready", "y_done", "y_out")]
        per = P // c.W
        with nc.Block() as block:
            @block.gpsimd
            def _(pool):
                core.clear_used(pool)

            @block.sync
            def _(sp):
                sp.dma_start(w_sb[:], ins[wo].rearrange("(t p) n -> p t n", p=P)).then_inc(w_in, 16)
                sp.dma_start(b_row[:], ins[bo].rearrange("(o n) -> o n", o=1).broadcast_to([P, D])).then_inc(b_in, 16)

            @block.tensor
            def _(pe):
                for half in range(2):
                    for kt in range(KT):
                        for n in range(4):
                            b, qt = 2 * half + n // QT, n % QT
                            mm = nc.tensor.transpose(t_ps[:, KT * half + kt, n * P:(n + 1) * P],
                                                     o_all[:, b, qt, kt * per:(kt + 1) * per].rearrange(
                                                         "p g w -> p (g w)"), core.ident[:])
                        mm.then_inc(turned, 1)
                pe.wait_ge(w_in, 16)
                for t in range(TT):
                    pe.wait_ge(t_out, KT * (t // 4 + 1))
                    if t >= 4:
                        pe.wait_ge(y_out, t - 3)
                    for kt in range(KT):
                        mm = nc.tensor.matmul(y_ps[:, t % 4, 0:D], core.xT[:, kt, t * P:(t + 1) * P], w_sb[:, kt],
                                              start=(kt == 0), stop=(kt == KT - 1))
                    mm.then_inc(y_done, 1)

            @block.vector
            def _(dve):
                for half in range(2):
                    for kt in range(KT):
                        dve.wait_ge(turned, KT * half + kt + 1)
                        nc.vector.tensor_copy(core.xT[:, kt, half * 512:(half + 1) * 512],
                                              t_ps[:, KT * half + kt]).then_inc(t_out, 1)
                dve.wait_ge(b_in, 16)
                for t in range(TT):
                    nc.vector.tensor_tensor(dst[:, t], core.x[:, t], b_row[:], ALU.add).then_inc(x_ready, 1)
                for t in range(TT):
                    dve.wait_ge(y_done, t + 1)
                    dve.wait_ge(x_ready, t + 1)
                    nc.vector.tensor_tensor(dst[:, t], y_ps[:, t % 4, 0:D], dst[:, t], ALU.add).then_inc(y_out, 1)


def final_norm(core, name, gamma, beta):
    nc, ins = core.nc, core.ins
    with core.stage(name) as st:
        g_row, b_row = st.sb("g_row", [P, D]), st.sb("b_row", [P, D])
        stats, mv = st.sb("stats", [P, TT, 6]), st.sb("mv", [P, TT, 2])
        base, power, rstd = st.sb("base", [P, TT]), st.sb("power", [P, TT]), st.sb("rstd", [P, TT])
        rows_in, stats_done, mv_done, base_done, power_set, rstd_done, x_norm, x_scaled = [
            st.sem(n) for n in ("rows_in", "stats_done", "mv_done", "base_done", "power_set", "rstd_done", "x_norm",
                                "x_scaled")]
        with nc.Block() as block:
            @block.sync
            def _(sp):
                for row, src in ((g_row, gamma), (b_row, beta)):
                    sp.dma_start(row[:], ins[src].rearrange("(o n) -> o n", o=1).broadcast_to([P, D])
                                 ).then_inc(rows_in, 16)

            @block.gpsimd
            def _(pool):
                core.clear_used(pool)
                nc.gpsimd.memset(power[:], -0.5).then_inc(power_set, 1)
                pool.wait_ge(power_set, 1)
                pool.wait_ge(base_done, 1)
                nc.gpsimd.tensor_tensor(out=rstd[:], in0=base[:], in1=power[:], op=ALU.pow).then_inc(rstd_done, 1)

            @block.vector
            def _(dve):
                for t in range(TT):
                    nc.vector.bn_stats(stats[:, t, :], core.x[:, t, :]).then_inc(stats_done, 1)
                for t in range(TT):
                    dve.wait_ge(stats_done, t + 1)
                    nc.vector.bn_aggr(mv[:, t, :], stats[:, t, :]).then_inc(mv_done, 1)
                dve.wait_ge(mv_done, TT)
                nc.vector.tensor_scalar(base[:], mv[:, :, 1], EPS, None, ALU.add).then_inc(base_done, 1)
                dve.wait_ge(rstd_done, 1)
                dve.wait_ge(rows_in, 32)
                for t in range(TT):
                    nc.vector.tensor_scalar(core.x[:, t], core.x[:, t], mv[:, t, 0:1], rstd[:, t:t + 1], ALU.subtract,
                                            ALU.mult).then_inc(x_norm, 1)
                for t in range(TT):
                    dve.wait_ge(x_norm, t + 1)
                    nc.vector.tensor_tensor(core.x[:, t], core.x[:, t], g_row[:], ALU.mult).then_inc(x_scaled, 1)
                for t in range(TT):
                    dve.wait_ge(x_scaled, t + 1)
                    nc.vector.tensor_tensor(core.x[:, t], core.x[:, t], b_row[:], ALU.add)


def small_layer(core, layer, wo, bo):
    nc = core.nc
    c = Small(layer)
    turn(core, f"t{layer}", core.x)
    KC = 64 if c.grouped else D
    q_stack = nc.dram_tensor(f"q_stack{layer}", (2, B * D, S), F32).ap()
    k_stack = nc.dram_tensor(f"k_stack{layer}", (2, B * KC, c.NK), F32).ap()
    with core.stage(f"l{layer}", holds_others=True) as st:
        v_all = st.sb("v_all", [P, c.quads, c.NKT, c.VW])
        o_all = st.sb("o_all", [P, B, QT, c.NQ, c.W])
        q_st = st.sb("q_st", [P, U, 4, S], F32R)
        k_st = st.sb("k_st", [P, U, c.kheads, c.NK], F32R)
        v_st = st.sb("v_st", [P, U, c.NKT, c.kheads, 32])
        small_projections(core, c, q_stack, k_stack, v_all, q_st, k_st, v_st)
        small_attention(core, c, q_stack, k_stack, v_all, o_all, q_st, k_st, v_st)
        if c.grouped:
            project_out(core, f"o{layer}", c, o_all, wo, bo, core.x)
            final_norm(core, f"n{layer}", "L2_xattn_gamma", "L2_xattn_beta")
        else:
            a_tok = st.sb("a_tok", [P, TT, D])
            project_out(core, f"o{layer}", c, o_all, wo, bo, a_tok)
            turn(core, f"r{layer}", a_tok, norm="rms", eps=EPS, scale=columns(core, f"L{layer}_xattn_postnorm_w"))


def program(nc, ins, out):
    with ExitStack() as ctx:
        core = Core(nc, ctx, ins)
        setup(core)
        for i in (1, 2):
            turn(core, f"n0{i}", core.x, norm="ln", eps=LN_EPS0, scale=columns(core, f"L0_xattn_ln{i}_scale"),
                 offset=columns(core, f"L0_xattn_ln{i}_offset"), factor=float(K0) ** -0.5)
            cross_attention0(core, i)
        turn(core, "n0m", core.x, norm="ln", eps=LN_EPS0, scale=columns(core, "L0_xattn_ln_mlp_scale"),
             offset=columns(core, "L0_xattn_ln_mlp_offset"))
        mlp(core, "m0", "L0_xattn_w_fc1", "L0_xattn_b_fc1", "L0_xattn_w_fc2", "L0_xattn_b_fc2", ACT.Gelu)
        small_layer(core, 1, "L1_xattn_out_w", "L1_xattn_out_b")
        mlp(core, "m1", "L1_xattn_mlp_w1", "L1_xattn_mlp_b1", "L1_xattn_mlp_w2", "L1_xattn_mlp_b2",
            ACT.Gelu_apprx_tanh)
        small_layer(core, 2, "L2_xattn_Wo", "L2_xattn_bo")
        small_layer(core, 3, "L3_xattn_out_w", "L3_xattn_out_b")
        mlp(core, "m3", "L3_xattn_mlp_w1", "L3_xattn_mlp_b1", "L3_xattn_mlp_w2", "L3_xattn_mlp_b2",
            ACT.Gelu_apprx_tanh, out)


def kernel(**inputs):
    import numpy as np
    import concourse.bacc as bacc
    from concourse.bass_utils import run_bass_kernel_spmd

    nc = bacc.Bacc("TRN2", target_bir_lowering=False, num_devices=1)
    arrays, ins = {}, {}
    for name, value in inputs.items():
        a = np.ascontiguousarray(value)
        arrays[name] = a
        ins[name] = nc.dram_tensor(name, a.shape, mybir.dt.from_np(a.dtype), kind="ExternalInput").ap()
    out = nc.dram_tensor("y", (B, S, D), F32, kind="ExternalOutput").ap()
    program(nc, ins, out)
    r = run_bass_kernel_spmd(nc, [arrays], core_ids=[0])
    return r.results[0]["y"]
```

```python
from contextlib import ExitStack

import concourse.bass as bass
from concourse import mybir

P = 128
B = 4
S = 256
D = 256
T = B * S
TT = T // P
KT = D // P
QT = S // P

H0, K0 = 16, 128
E0 = H0 * K0
F = 1024
FT = F // P
LN_EPS0 = 1e-5
EPS = 1e-6
MASKED = -1e30

ALU = mybir.AluOpType
ACT = mybir.ActivationFunctionType
AX = mybir.AxisListType
F32 = mybir.dt.float32
F32R = mybir.dt.float32r
I32 = mybir.dt.int32


def wait(eng, sem, count):
    if isinstance(count, int) and count <= 0:
        return
    eng.wait_ge(sem, count)


class Core:

    def __init__(self, nc, ctx, ins):
        self.nc, self.ctx, self.ins = nc, ctx, ins
        self.used = []
        self.x = self.sb("x_tok", [P, TT, D])
        self.xT = self.sb("xT", [P, KT, T])
        self.cT = self.sb("ctxT", [P, KT, T])
        self.c_hi, self.c_lo = None, None
        self.ident = self.sb("ident", [P, P])
        self.cols = self.sb("cols", [P, 2, P])
        self.maskrow = nc.dram_tensor("maskrow", (B, 2 * S), F32).ap()

    def sb(self, name, shape, dt=F32):
        return self.ctx.enter_context(self.nc.sbuf_tensor(name, shape, dt))

    def stage(self, name, holds_others=False):
        return Stage(self, name, holds_others)

    def clear_used(self, pool):
        for handle in self.used:
            pool.sem_clear(handle)


class Stage:

    def __init__(self, core, name, holds_others):
        self.core, self.name, self.ctx, self.holds_others = core, name, ExitStack(), holds_others
        self.sems = []

    def __enter__(self):
        return self

    def __exit__(self, *a):
        self.ctx.close()
        if not self.holds_others:
            for handle in self.core.used:
                self.core.nc.release_semaphore(handle)
            self.core.used = self.sems

    def sb(self, name, shape, dt=F32):
        return self.ctx.enter_context(self.core.nc.sbuf_tensor(f"{self.name}_{name}", shape, dt))

    def psum(self, name, shape):
        return self.ctx.enter_context(self.core.nc.psum_tensor(f"{self.name}_{name}", shape, F32))

    def sem(self, name):
        self.sems.append(self.core.nc.alloc_semaphore(name=f"{self.name}_{name}"))
        return self.sems[-1]

    def slot_sems(self, name, count):
        return [self.sem(f"{name}{n}") for n in range(count)]


COLS0 = [("L0_xattn_ln1_scale", KT), ("L0_xattn_ln1_offset", KT), ("L0_xattn_bq1", H0), ("L0_xattn_bk1", H0),
         ("L0_xattn_bias_k1", H0), ("L0_xattn_bias_v1", H0), ("L0_xattn_ln_mlp_scale", KT),
         ("L0_xattn_ln_mlp_offset", KT), ("L0_xattn_b_fc1", FT), ("L1_xattn_q_b", KT), ("L1_kv_b_k", KT),
         ("L1_xattn_postnorm_w", KT), ("L1_xattn_mlp_b1", FT), ("L2_xattn_bq", KT)]
COLS1 = [("L0_xattn_ln2_scale", KT), ("L0_xattn_ln2_offset", KT), ("L0_xattn_bq2", H0), ("L0_xattn_bk2", H0),
         ("L0_xattn_bias_k2", H0), ("L0_xattn_bias_v2", H0), ("L3_xattn_q_b", KT), ("L3_kv_b_k", KT),
         ("L3_xattn_postnorm_w", KT), ("L3_xattn_mlp_b1", FT), ("L2_xattn_bk", 1)]
L2_BK = 64


def column_places():
    places = {}
    for n, group in enumerate((COLS0, COLS1)):
        at = 0
        for name, count in group:
            places[name] = (n, at, count)
            at += count
    return places


PLACES = column_places()


def columns(core, name):
    n, at, count = PLACES[name]
    return core.cols[:, n, at:at + count]


def setup(core):
    nc, ins = core.nc, core.ins
    with core.stage("setup") as st:
        c_tok = st.sb("c_tok", [P, TT, D])
        rows = st.sb("rows", [P, 2, P])
        mask_i = st.sb("mask_i", [B, S], I32)
        mask_f = st.sb("mask_f", [B, 2 * S], F32R)
        turned = st.psum("turned", [P, 4, 512])
        turned_cols = st.psum("turned_cols", [P, 2, P])
        ctx_in, rows_in, x_in = st.sem("ctx_in"), st.sem("rows_in"), st.sem("x_in")
        zeroed, ident_made, rows_zeroed = st.sem("zeroed"), st.sem("ident_made"), st.sem("rows_zeroed")
        cols_turned, ctx_turned, masked, mask_out = (
            st.sem("cols_turned"), st.sem("ctx_turned"), st.sem("masked"), st.sem("mask_out"))
        n_rows = 0
        with nc.Block() as block:
            @block.sync
            def _(sp):
                sp.dma_start(c_tok[:], ins["ctx_2048"].rearrange("b (t p) d -> p (b t) d", p=P)).then_inc(ctx_in, 16)
                sp.dma_start(mask_i[:], ins["mask_BxS2_ik0"]).then_inc(ctx_in, 16)
                sp.dma_start(core.x[:], ins["x"].rearrange("b (t p) d -> p (b t) d", p=P)).then_inc(x_in, 16)
                sp.wait_ge(masked, 2)
                sp.dma_start(core.maskrow, mask_f[:].bitcast(F32)).then_inc(mask_out, 16)
                sp.wait_ge(mask_out, 16)
                sp.wait_ge(x_in, 16)

            @block.scalar
            def _(act):
                act.wait_ge(rows_zeroed, 1)
                nonlocal n_rows
                for name, (n, at, count) in PLACES.items():
                    if name.endswith("kv_b_k"):
                        src = ins[name[:2] + "_xattn_kv_b"].rearrange("(c p two) -> c p two", p=P, two=2)[:, :, 0]
                        act.dma_start(rows[at:at + count, n, :], src, allow_slow_non_contiguous=True).then_inc(rows_in, 16)
                    elif name == "L2_xattn_bk":
                        src = ins[name].rearrange("(c p) -> c p", c=1)
                        act.dma_start(rows[at:at + 1, n, 0:L2_BK], src).then_inc(rows_in, 16)
                    else:
                        flat = ins[name]
                        if len(flat.shape) == 4:
                            flat = flat.rearrange("a b h k -> (a b h k)")
                        act.dma_start(rows[at:at + count, n, :], flat.rearrange("(c p) -> c p", p=P)
                                      ).then_inc(rows_in, 16)
                    n_rows += 1

            @block.gpsimd
            def _(pool):
                core.clear_used(pool)
                nc.gpsimd.memset(rows[:], 0.0).then_inc(rows_zeroed, 1)
                nc.gpsimd.memset(core.ident[:], 0.0).then_inc(zeroed, 1)
                pool.wait_ge(zeroed, 1)
                nc.gpsimd.affine_select(out=core.ident[:], in_=core.ident[:], compare_op=ALU.not_equal, fill=1.0,
                                        base=0, pattern=[[-1, P]], channel_multiplier=1).then_inc(ident_made, 1)

            @block.tensor
            def _(pe):
                pe.wait_ge(ident_made, 1)
                pe.wait_ge(ctx_in, 32)
                for kt in range(KT):
                    for half in range(2):
                        for i in range(4):
                            t = 4 * half + i
                            mm = nc.tensor.transpose(turned[:, 2 * kt + half, i * P:(i + 1) * P],
                                                     c_tok[:, t, kt * P:(kt + 1) * P], core.ident[:])
                        mm.then_inc(ctx_turned, 1)
                pe.wait_ge(rows_in, 16 * len(PLACES))
                for n in range(2):
                    mm = nc.tensor.transpose(turned_cols[:, n, :], rows[:, n, :], core.ident[:])
                mm.then_inc(cols_turned, 1)

            @block.vector
            def _(dve):
                nc.vector.memset(mask_f[:, S:2 * S].bitcast(F32), 0.0).then_inc(masked, 1)
                dve.wait_ge(ctx_in, 32)
                nc.vector.tensor_scalar(mask_f[:, 0:S], mask_i[:], 0.0, MASKED, ALU.is_equal, ALU.mult
                                        ).then_inc(masked, 1)
                for kt in range(KT):
                    for half in range(2):
                        dve.wait_ge(ctx_turned, 2 * kt + half + 1)
                        nc.vector.tensor_copy(core.cT[:, kt, half * 512:(half + 1) * 512],
                                              turned[:, 2 * kt + half, :])
                dve.wait_ge(cols_turned, 1)
                nc.vector.tensor_copy(core.cols[:], turned_cols[:])


def turn(core, name, src, norm=None, eps=0.0, scale=None, offset=None, factor=1.0, ahead=None):
    nc, ident = core.nc, core.ident
    with core.stage(name) as st:
        stats = st.sb("stats", [P, TT, 6])
        mv = st.sb("mv", [P, TT, 2])
        msq = st.sb("msq", [P, TT])
        base = st.sb("base", [P, TT])
        power = st.sb("power", [P, TT])
        rstd = st.sb("rstd", [P, TT])
        normed = st.sb("normed", [P, TT, D])
        sc = st.sb("sc", [P, 2 * KT])
        turned = st.psum("turned", [P, 4, 512])
        stats_done, mv_done, msq_done, base_done, power_set, rstd_done, normed_done, sc_done, tile_turned = [
            st.sem(n) for n in ("stats_done", "mv_done", "msq_done", "base_done", "power_set", "rstd_done",
                                "normed_done", "sc_done", "tile_turned")]
        z = type("Semaphores", (), {n: st.sem(n) for n in ("qk_in", "v_in", "rows_in", "one_set", "split", "chunk_out",
                                                           "chunk_hi", "c_hi_done")})
        first = ahead is not None and ahead.i == 1
        chunks = [(kt, slice(half * 512, (half + 1) * 512)) for half in range(2) for kt in range(KT)]
        with nc.Block() as block:
            if ahead is not None:
                @block.sync
                def _(sp):
                    ahead.prepare_sync(sp, z)

                @block.scalar
                def _(act):
                    if first:
                        nc.scalar.activation(core.c_hi[:], core.cT[:], ACT.Copy).then_inc(z.c_hi_done, 1)
                    for n, (kt, cols) in enumerate(chunks):
                        act.wait_ge(z.chunk_out, n + 1)
                        nc.scalar.activation(ahead.h_hi[:, kt, cols], core.xT[:, kt, cols], ACT.Copy
                                             ).then_inc(z.chunk_hi, 1)

            @block.gpsimd
            def _(pool):
                core.clear_used(pool)
                if ahead is not None:
                    ahead.prepare_pool(pool, z, 0)
                if norm:
                    nc.gpsimd.memset(power[:], -0.5).then_inc(power_set, 1)
                    pool.wait_ge(power_set, 1)
                    pool.wait_ge(base_done, 1)
                    nc.gpsimd.tensor_tensor(out=rstd[:], in0=base[:], in1=power[:], op=ALU.pow).then_inc(rstd_done, 1)
                if ahead is not None:
                    ahead.prepare_pool(pool, z, 1)

            @block.vector
            def _(dve):
                if scale is not None:
                    nc.vector.tensor_scalar(sc[:, 0:KT], scale, factor, None, ALU.mult).then_inc(sc_done, 1)
                    if offset is not None:
                        nc.vector.tensor_scalar(sc[:, KT:2 * KT], offset, factor, None, ALU.mult).then_inc(sc_done, 1)
                if norm:
                    for t in range(TT):
                        nc.vector.bn_stats(stats[:, t, :], src[:, t, :]).then_inc(stats_done, 1)
                    for t in range(TT):
                        dve.wait_ge(stats_done, t + 1)
                        nc.vector.bn_aggr(mv[:, t, :], stats[:, t, :]).then_inc(mv_done, 1)
                    dve.wait_ge(mv_done, TT)
                    if norm == "rms":
                        nc.vector.tensor_tensor(msq[:], mv[:, :, 0], mv[:, :, 0], ALU.mult).then_inc(msq_done, 1)
                        dve.wait_ge(msq_done, 1)
                        nc.vector.scalar_tensor_tensor(out=base[:], in0=msq[:], scalar=eps, in1=mv[:, :, 1],
                                                       op0=ALU.add, op1=ALU.add).then_inc(base_done, 1)
                    else:
                        nc.vector.tensor_scalar(base[:], mv[:, :, 1], eps, None, ALU.add).then_inc(base_done, 1)
                    dve.wait_ge(rstd_done, 1)
                    for t in range(TT):
                        if norm == "rms":
                            nc.vector.tensor_scalar(normed[:, t, :], src[:, t, :], rstd[:, t:t + 1], None, ALU.mult
                                                    ).then_inc(normed_done, 1)
                        else:
                            nc.vector.tensor_scalar(normed[:, t, :], src[:, t, :], mv[:, t, 0:1], rstd[:, t:t + 1],
                                                    ALU.subtract, ALU.mult).then_inc(normed_done, 1)
                if scale is not None:
                    dve.wait_ge(sc_done, 1 if offset is None else 2)
                def trailing(n):
                    kt, cols = chunks[n]
                    dve.wait_ge(z.chunk_hi, n + 1)
                    nc.vector.tensor_tensor(ahead.h_lo[:, kt, cols], core.xT[:, kt, cols],
                                            ahead.h_hi[:, kt, cols].bitcast(F32), ALU.subtract)

                for n, (kt, cols) in enumerate(chunks):
                    out, ps = core.xT[:, kt, cols], turned[:, n, :]
                    dve.wait_ge(tile_turned, n + 1)
                    if scale is None:
                        nc.vector.tensor_copy(out, ps)
                    elif offset is None:
                        nc.vector.tensor_scalar(out, ps, sc[:, kt:kt + 1], None, ALU.mult)
                    else:
                        nc.vector.tensor_scalar(out, ps, sc[:, kt:kt + 1], sc[:, KT + kt:KT + kt + 1],
                                                ALU.mult, ALU.add).then_inc(z.chunk_out, 1)
                    if ahead is not None and n:
                        trailing(n - 1)
                if ahead is not None:
                    trailing(len(chunks) - 1)
                if first:
                    dve.wait_ge(z.c_hi_done, 1)
                    nc.vector.tensor_tensor(core.c_lo[:], core.cT[:], core.c_hi[:].bitcast(F32), ALU.subtract)

            @block.tensor
            def _(pe):
                for half in range(2):
                    if norm:
                        pe.wait_ge(normed_done, 4 * half + 4)
                    for kt in range(KT):
                        for i in range(4):
                            t = 4 * half + i
                            tile = normed[:, t, kt * P:(kt + 1) * P] if norm else src[:, t, kt * P:(kt + 1) * P]
                            mm = nc.tensor.transpose(turned[:, KT * half + kt, i * P:(i + 1) * P], tile, ident[:])
                        mm.then_inc(tile_turned, 1)


def steps(text):
    return [(w[0], int(w[1])) for w in text.split()]


PE_STEPS = (steps("S0 S1 G0 G1 T0 S2 S3 T1 V0 G2 G3 V1 T2 G4 V2 T3 G5 V3"),
            steps("S0 G0 G1 S1 S2 T0 G2 V0 G3 T1 S3 G4 V1 T2 Y0 V2 Y1 T3 G5 V3 Y2 Y3"))
ACT_STEPS = (steps("E0 E1 G0 C0 G1 C1 E2 H0 G2 E3 G3 H1 C2 H2 C3 H3"),
             steps("E0 G0 G1 C0 E1 G2 E2 H0 G3 C1 H1 C2 E3 H2 C3 H3"))
DVE_STEPS = (steps("M0 M1 N0 N1 G0 M2 G1 M3 N2 L0 G2 N3 L1 G3 G4 L2 G5 L3"),
             steps("M0 N0 G0 M1 G1 M2 N1 G2 N2 L0 G3 G4 M3 L1 Y0 N3 L2 Y1 G5 L3 Y2 Y3"))
NK = S + 1
NKP = NK + 1
NPAIR = H0 // 2
PW = 2 * K0


class Turns:
    AHEAD, PAIR, EVEN = 8, 16, 6

    @classmethod
    def number(cls, p, s, kind, n):
        last = isinstance(p, int) and p == NPAIR - 1
        users = [x for x in PE_STEPS[s] if x[0] == "Y" or x[0] == "G" and not (last and (s or x[1] > 3))]
        return cls.AHEAD + cls.PAIR * p + s * (4 if last else cls.EVEN) + users.index((kind, n))

    @staticmethod
    def bank(p, s, kind, n):
        last = isinstance(p, int) and p == NPAIR - 1
        users = [x for x in PE_STEPS[s] if x[0] == "Y" or x[0] == "G" and not (last and (s or x[1] > 3))]
        return users.index((kind, n)) % 2

    @classmethod
    def qk_out(cls, p, s):
        if s:
            return cls.number(p, 0, "G", 3) + 1
        return 4 if isinstance(p, int) and p == 0 else cls.number_of_full(p - 1, 1, "G", 3) + 1

    @classmethod
    def v_out(cls, p):
        return 8 if isinstance(p, int) and p == 0 else cls.number_of_full(p - 1, 1, "G", 5) + 1

    @classmethod
    def number_of_full(cls, p, s, kind, n):
        users = [x for x in PE_STEPS[s] if x[0] in "YG"]
        return cls.AHEAD + cls.PAIR * p + s * cls.EVEN + users.index((kind, n))


class CrossBuffers:

    def __init__(self, st, core, i):
        self.core, self.i = core, i
        self.h_hi, self.h_lo = st.sb("h_hi", [P, KT, T], F32R), st.sb("h_lo", [P, KT, T], F32R)
        self.wqk_raw, self.wv_raw = st.sb("wqk_raw", [P, 2, KT, K0]), st.sb("wv_raw", [P, KT, PW])
        self.wqk_hi, self.wqk_lo = [st.sb(n, [P, 2, 2, KT, K0], F32R) for n in ("wqk_hi", "wqk_lo")]
        self.wv_hi, self.wv_lo = [st.sb(n, [P, KT, PW], F32R) for n in ("wv_hi", "wv_lo")]
        self.one = st.sb("one", [P, 1])
        self.vbias, self.bv_row = st.sb("vbias", [P, E0]), st.sb("bv_row", [P, E0])
        self.bo_row = st.sb("bo_row", [P, D])

    def input(self, name):
        return self.core.ins[f"L0_xattn_{name}{self.i}"]

    def load_qk(self, sp, h, sem):
        for n, w in enumerate(("wq", "wk")):
            sp.dma_start(self.wqk_raw[:, n], self.input(w)[:, bass.ds(h * K0, K0)].rearrange("(t p) n -> p t n", p=P)
                         ).then_inc(sem, 16)

    def load_v(self, sp, p, sem):
        sp.dma_start(self.wv_raw[:], self.input("wv")[:, bass.ds(p * PW, PW)].rearrange("(t p) n -> p t n", p=P)
                     ).then_inc(sem, 16)

    def times_one(self, n):
        return self.one[:].broadcast_to([P, n])

    def qk_parts(self, s):
        flat = "p a t n -> p (a t n)"
        return self.wqk_raw[:].rearrange(flat), self.wqk_hi[:, s].rearrange(flat), self.wqk_lo[:, s].rearrange(flat)

    def v_parts(self):
        return [w[:].rearrange("p t n -> p (t n)") for w in (self.wv_raw, self.wv_hi, self.wv_lo)]

    def prepare_sync(self, sp, z):
        self.load_qk(sp, 0, z.qk_in)
        self.load_v(sp, 0, z.v_in)
        for row, src in ((self.vbias, "bias_v"), (self.bv_row, "bv"), (self.bo_row, "bo")):
            flat = self.input(src)
            if len(flat.shape) == 4:
                flat = flat.rearrange("a b h k -> (a b h k)")
            sp.dma_start(row[:], flat.rearrange("(o n) -> o n", o=1).broadcast_to([P, flat.shape[0]])
                         ).then_inc(z.rows_in, 16)
        sp.wait_ge(z.rows_in, 48)

    def prepare_pool(self, pool, z, part):
        nc = self.core.nc
        if part == 0:
            nc.gpsimd.memset(self.one[:], 1.0).then_inc(z.one_set, 1)
            pool.wait_ge(z.one_set, 1)
            pool.wait_ge(z.qk_in, 32)
            raw, hi, lo = self.qk_parts(0)
        else:
            pool.wait_ge(z.v_in, 16)
            raw, hi, lo = self.v_parts()
        nc.gpsimd.tensor_tensor(hi, raw, self.times_one(raw.shape[1]), ALU.mult).then_inc(z.split, 1)
        pool.wait_ge(z.split, part + 1)
        nc.gpsimd.tensor_tensor(lo, raw, hi.bitcast(F32), ALU.subtract)


def cross_attention0(core, i, w):
    nc, ins = core.nc, core.ins
    name = f"L0_xattn_%s{i}"
    wo = ins[name % "wo"]
    with core.stage(f"a{i}") as st:
        h_hi, h_lo, c_hi, c_lo = w.h_hi, w.h_lo, core.c_hi, core.c_lo
        wo_raw = st.sb("wo_raw", [P, 2, D])
        wo_hi, wo_lo = st.sb("wo_hi", [P, 2, D], F32R), st.sb("wo_lo", [P, 2, D], F32R)
        q_hi, q_lo = st.sb("q_hi", [P, 2, T], F32R), st.sb("q_lo", [P, 2, T], F32R)
        k_hi, k_lo = st.sb("k_hi", [P, 2, B, NKP], F32R), st.sb("k_lo", [P, 2, B, NKP], F32R)
        v_sb = st.sb("v_sb", [P, 2, TT, PW])
        negmax, den, rden = st.sb("negmax", [P, 2, QT]), st.sb("den", [P, 2, QT]), st.sb("rden", [P, 2, QT])
        prob = st.sb("prob", [P, 2, QT, NKP])
        probT = st.sb("probT", [P, 2, QT * S])
        oT_hi, oT_lo = st.sb("oT_hi", [P, 2, T], F32R), st.sb("oT_lo", [P, 2, T], F32R)
        bias_cols = st.sb("bias_cols", [P, 3, H0])
        hc = st.sb("hc", [P, 2, 3])
        vb = st.sb("vb", [P, PW])
        bk_hi, bk_lo = st.sb("bk_hi", [P, H0], F32R), st.sb("bk_lo", [P, H0], F32R)
        g_ps, s_ps = st.psum("g_ps", [P, 2, 512]), st.psum("s_ps", [P, 2, QT, 512])
        t_ps, o_ps = st.psum("t_ps", [P, 512]), st.psum("o_ps", [P, 512])

        sems = ("bo_added", "wo_in", "wqk_in", "wv_in", "wqk_split", "wv_split", "wo_split", "consts", "kbias",
                "turn_done", "g_hi", "turn_out", "s_done", "max_done", "exp_done", "rden_done", "norm_done", "t_done",
                "t_out", "v_done", "o_hi", "o_lo", "raw_hi", "zero_set", "vb_done", "head_set", "pair_set")
        z = type("Semaphores", (), {n: st.sem(n) for n in sems})
        bq, bk, bkey, bv = (columns(core, name % v) for v in ("bq", "bk", "bias_k", "bias_v"))

        def pairs(eng, body):
            body(0, 0)
            with eng.Fori(0, (NPAIR - 2) // 2) as r:
                body(2 * r + 1, 1)
                body(2 * r + 2, 0)
            body(NPAIR - 1, 1)

        def halves(p):
            last = isinstance(p, int) and p == NPAIR - 1
            return [(0, 2 * p, True, not last), (1, 2 * p + 1, not last, not last)]

        def left_out(kind, n, s, more, after):
            return kind == "G" and (not more or n > 3 and not after)

        with nc.Block() as block:
            @block.sync
            def _(sp):
                def load_qk(h):
                    wait(sp, z.wqk_split, 2 * (h - 1))
                    w.load_qk(sp, h, z.wqk_in)

                load_qk(1)

                def body(p, vs):
                    for s, h, _, after in halves(p):
                        if after:
                            load_qk(h + 2)
                        if s == 0:
                            if after:
                                wait(sp, z.wv_split, 2 * p)
                                w.load_v(sp, p + 1, z.wv_in)
                            wait(sp, z.wo_split, 2 * p)
                            sp.dma_start(wo_raw[:], wo[bass.ds(p * PW, PW), :].rearrange("(h p) n -> p h n", p=P)
                                         ).then_inc(z.wo_in, 16)
                pairs(sp, body)

            @block.gpsimd
            def _(pool):
                core.clear_used(pool)
                nc.gpsimd.memset(k_hi[:, :, :, NK:NKP].bitcast(F32), 0.0).then_inc(z.zero_set, 1)
                nc.gpsimd.memset(k_lo[:, :, :, NK:NKP].bitcast(F32), 0.0).then_inc(z.zero_set, 1)
                nc.gpsimd.tensor_copy(bk_hi[:], bkey).then_inc(z.raw_hi, 1)
                pool.wait_ge(z.raw_hi, 1)
                nc.gpsimd.tensor_tensor(bk_lo[:], bkey, bk_hi[:].bitcast(F32), ALU.subtract).then_inc(z.raw_hi, 1)
                pool.wait_ge(z.raw_hi, 2)

                def split_qk(h, s, free):
                    pool.wait_ge(z.wqk_in, 32 * h)
                    if free is not None:
                        pool.wait_ge(z.turn_done, free)
                    raw, hi, lo = w.qk_parts(s)
                    nc.gpsimd.tensor_tensor(hi, raw, w.times_one(raw.shape[1]), ALU.mult).then_inc(z.wqk_split, 1)
                    pool.wait_ge(z.wqk_split, 2 * h - 1)
                    nc.gpsimd.tensor_tensor(lo, raw, hi.bitcast(F32), ALU.subtract).then_inc(z.wqk_split, 1)

                def split_v(p):
                    pool.wait_ge(z.wv_in, 16 * p)
                    pool.wait_ge(z.turn_done, Turns.v_out(p - 1))
                    raw, hi, lo = w.v_parts()
                    nc.gpsimd.tensor_tensor(hi, raw, w.times_one(raw.shape[1]), ALU.mult).then_inc(z.wv_split, 1)
                    pool.wait_ge(z.wv_split, 2 * p - 1)
                    nc.gpsimd.tensor_tensor(lo, raw, hi.bitcast(F32), ALU.subtract).then_inc(z.wv_split, 1)

                def split_o(p):
                    pool.wait_ge(z.wo_in, 16 * (p + 1))
                    if not (isinstance(p, int) and p == 0):
                        pool.wait_ge(z.turn_done, Turns.number_of_full(p - 1, 1, "Y", B - 1) + 1)
                    raw, hi, lo = [x[:].rearrange("p h n -> p (h n)") for x in (wo_raw, wo_hi, wo_lo)]
                    nc.gpsimd.tensor_tensor(hi, raw, w.times_one(raw.shape[1]), ALU.mult).then_inc(z.wo_split, 1)
                    pool.wait_ge(z.wo_split, 2 * p + 1)
                    nc.gpsimd.tensor_tensor(lo, raw, hi.bitcast(F32), ALU.subtract).then_inc(z.wo_split, 1)

                def key_bias(h, s):
                    wait(pool, z.s_done, B * (h - 1))
                    for part, src in ((k_hi, bk_hi), (k_lo, bk_lo)):
                        nc.gpsimd.tensor_copy(part[:, s, :, S:NK].rearrange("p b o -> p (b o)"),
                                              src[:, bass.ds(h, 1)].bitcast(F32).broadcast_to([P, B])
                                              ).then_inc(z.kbias, 1)

                key_bias(0, 0)
                split_qk(1, 1, None)
                nc.gpsimd.tensor_tensor(core.x[:], core.x[:], w.bo_row[:].rearrange("p (o n) -> p o n", o=1)
                                        .broadcast_to([P, TT, D]), ALU.add).then_inc(z.bo_added, 1)

                def body(p, vs):
                    for s, h, more, after in halves(p):
                        if s == 0 and after:
                            split_v(p + 1)
                        if more:
                            key_bias(h + 1, 1 - s)
                        if after:
                            split_qk(h + 2, s, Turns.qk_out(p, s))
                        if s == 0:
                            split_o(p)
                pairs(pool, body)

            def k_out(part, s, g):
                return part[:, s, 2 * g:2 * g + 2, 0:S]

            @block.scalar
            def _(act):
                def group(number, bank, h, s, g):
                    if g == 0:
                        act.wait_ge(z.head_set, h + 1)
                    act.wait_ge(z.turn_done, number + 1)
                    ps = g_ps[:, bank]
                    if g < 2:
                        nc.scalar.activation(q_hi[:, s, g * 512:(g + 1) * 512], ps, ACT.Identity,
                                             bias=hc[:, s, 0:1]).then_inc(z.g_hi, 1)
                    else:
                        nc.scalar.activation(k_out(k_hi, s, g - 2), ps.rearrange("p (b t) -> p b t", t=S),
                                             ACT.Identity, bias=hc[:, s, 1:2]).then_inc(z.g_hi, 1)

                def step(kind, n, p, s, h):
                    u = B * h + n
                    if kind == "E":
                        act.wait_ge(z.max_done, u + 1)
                        wait(act, z.t_done, u - 1)
                        for qt in range(QT):
                            nc.scalar.activation(prob[:, n % 2, qt, 0:NK], s_ps[:, n % 2, qt, 0:NK], ACT.Exp,
                                                 bias=negmax[:, n % 2, qt:qt + 1],
                                                 accum_out=den[:, n % 2, qt:qt + 1]).then_inc(z.exp_done, 1)
                    elif kind == "G":
                        group(Turns.number(p, s, "G", n), Turns.bank(p, s, "G", n), h + 1, 1 - s, n)
                    elif kind == "C":
                        act.wait_ge(z.t_done, u + 1)
                        wait(act, z.v_done, u - 1)
                        nc.scalar.activation(probT[:, n % 2], t_ps[:], ACT.Copy).then_inc(z.t_out, 1)
                    elif kind == "H":
                        act.wait_ge(z.v_done, u + 1)
                        nc.scalar.activation(oT_hi[:, s, n * S:(n + 1) * S], o_ps[:, 0:S], ACT.Identity,
                                             bias=hc[:, s, 2:3]).then_inc(z.o_hi, 1)

                for g in range(4):
                    group(g, g % 2, 0, 0, g)

                def body(p, vs):
                    for s, h, more, after in halves(p):
                        for kind, n in ACT_STEPS[s]:
                            if not left_out(kind, n, s, more, after):
                                step(kind, n, p, s, h)
                pairs(act, body)

            @block.vector
            def _(dve):
                nc.vector.tensor_scalar(bias_cols[:, 0], bq, float(K0) ** -0.5, None, ALU.mult).then_inc(z.consts, 1)
                nc.vector.tensor_copy(bias_cols[:, 1], bk).then_inc(z.consts, 1)
                nc.vector.tensor_copy(bias_cols[:, 2], bv).then_inc(z.consts, 1)
                dve.wait_ge(z.consts, 3)

                def set_head(h, s):
                    wait(dve, z.o_lo, B * (h - 1))
                    nc.vector.tensor_scalar(hc[:, s], bias_cols[:, :, bass.ds(h, 1)].rearrange("p a o -> p (a o)"),
                                            1.0, None, ALU.mult).then_inc(z.head_set, 1)

                def set_pair(p):
                    if not (isinstance(p, int) and p == 0):
                        dve.wait_ge(z.turn_out, Turns.v_out(p - 1))
                    nc.vector.tensor_scalar(vb[:], w.vbias[:, bass.ds(p * PW, PW)], 1.0, None, ALU.mult
                                            ).then_inc(z.pair_set, 1)

                def group(number, bank, h, s, g):
                    dve.wait_ge(z.g_hi, 4 * h + g + 1)
                    ps = g_ps[:, bank]
                    if g < 2:
                        cols = slice(g * 512, (g + 1) * 512)
                        nc.vector.scalar_tensor_tensor(out=q_lo[:, s, cols], in0=ps, scalar=hc[:, s, 0:1],
                                                       in1=q_hi[:, s, cols].bitcast(F32), op0=ALU.add,
                                                       op1=ALU.subtract).then_inc(z.turn_out, 1)
                    else:
                        nc.vector.scalar_tensor_tensor(out=k_out(k_lo, s, g - 2),
                                                       in0=ps.rearrange("p (b t) -> p b t", t=S),
                                                       scalar=hc[:, s, 1:2],
                                                       in1=k_out(k_hi, s, g - 2).bitcast(F32), op0=ALU.add,
                                                       op1=ALU.subtract).then_inc(z.turn_out, 1)

                def values(number, bank, p, vs, j):
                    dve.wait_ge(z.pair_set, p + 1)
                    dve.wait_ge(z.turn_done, number + 1)
                    nc.vector.tensor_tensor(v_sb[:, vs, 2 * j:2 * j + 2], g_ps[:, bank].rearrange(
                        "p (t d) -> p t d", d=PW), vb[:].rearrange("p (o d) -> p o d", o=1).broadcast_to([P, 2, PW]),
                        ALU.add).then_inc(z.turn_out, 1)

                def step(kind, n, p, s, h, vs):
                    u = B * h + n
                    if kind in "GY":
                        number, bank = Turns.number(p, s, kind, n), Turns.bank(p, s, kind, n)
                    if kind == "M":
                        dve.wait_ge(z.s_done, u + 1)
                        nc.vector.tensor_reduce(negmax[:, n % 2], s_ps[:, n % 2, :, 0:NK], AX.X, ALU.max, negate=True
                                                ).then_inc(z.max_done, 1)
                    elif kind == "N":
                        dve.wait_ge(z.exp_done, 2 * (u + 1))
                        wait(dve, z.norm_done, 2 * (u - 1))
                        nc.vector.reciprocal(rden[:, n % 2], den[:, n % 2]).then_inc(z.rden_done, 1)
                        dve.wait_ge(z.rden_done, u + 1)
                        for qt in range(QT):
                            nc.vector.tensor_scalar(prob[:, n % 2, qt, 0:S], prob[:, n % 2, qt, 0:S],
                                                    rden[:, n % 2, qt:qt + 1], None, ALU.mult
                                                    ).then_inc(z.norm_done, 1)
                    elif kind == "G" and n < 4:
                        group(number, bank, h + 1, 1 - s, n)
                    elif kind == "G":
                        values(number, bank, p + 1, 1 - vs, 2 * s + n - 4)
                    elif kind == "L":
                        dve.wait_ge(z.o_hi, u + 1)
                        cols = slice(n * S, (n + 1) * S)
                        nc.vector.scalar_tensor_tensor(out=oT_lo[:, s, cols], in0=o_ps[:, 0:S],
                                                       scalar=hc[:, s, 2:3],
                                                       in1=oT_hi[:, s, cols].bitcast(F32), op0=ALU.add,
                                                       op1=ALU.subtract).then_inc(z.o_lo, 1)
                    elif kind == "Y":
                        if n == 0:
                            dve.wait_ge(z.bo_added, 1)
                            wait(dve, z.turn_out, number - 1)
                        dve.wait_ge(z.turn_done, number + 1)
                        xb = core.x[:, QT * n:QT * n + QT]
                        nc.vector.tensor_tensor(xb, g_ps[:, bank].rearrange("p (t d) -> p t d", d=D), xb, ALU.add
                                                ).then_inc(z.turn_out, 1)

                set_head(0, 0)
                dve.wait_ge(z.head_set, 1)
                for g in range(4):
                    group(g, g % 2, 0, 0, g)
                nc.vector.tensor_tensor(w.vbias[:], w.bv_row[:], w.vbias[:], ALU.subtract).then_inc(z.vb_done, 1)
                dve.wait_ge(z.vb_done, 1)
                set_pair(0)
                for j in range(4):
                    values(4 + j, j % 2, 0, 0, j)

                def body(p, vs):
                    for s, h, more, after in halves(p):
                        if more:
                            set_head(h + 1, 1 - s)
                            dve.wait_ge(z.head_set, h + 2)
                        if s == 0 and after:
                            set_pair(p + 1)
                        for kind, n in DVE_STEPS[s]:
                            if not left_out(kind, n, s, more, after):
                                step(kind, n, p, s, h, vs)
                pairs(dve, body)

            @block.tensor
            def _(pe):
                def product(out, left, right, start=True, stop=True):
                    (a_hi, a_lo), (b_hi, b_lo) = left, right
                    nc.tensor.matmul(out, a_hi, b_hi, start=start, stop=False)
                    nc.tensor.matmul(out, a_hi, b_lo, start=False, stop=False)
                    return nc.tensor.matmul(out, a_lo, b_hi, start=False, stop=stop)

                def take_turn(number):
                    if not (isinstance(number, int) and number < 2):
                        pe.wait_ge(z.turn_out, number - 1)

                def group(number, bank, h, s, g):
                    take_turn(number)
                    if g == 0:
                        wait(pe, z.wqk_split, 2 * h)
                    n, cols = g // 2, slice(g % 2 * 512, (g % 2 + 1) * 512)
                    src = ((h_hi, h_lo), (c_hi, c_lo))[n]
                    for kt in range(KT):
                        mm = product(g_ps[:, bank], (w.wqk_hi[:, s, n, kt], w.wqk_lo[:, s, n, kt]),
                                     (src[0][:, kt, cols], src[1][:, kt, cols]), kt == 0, kt == KT - 1)
                    mm.then_inc(z.turn_done, 1)

                def values(number, bank, p, j):
                    take_turn(number)
                    wait(pe, z.wv_split, 2 * p)
                    for tj in range(2):
                        tok = slice((2 * j + tj) * P, (2 * j + tj + 1) * P)
                        for kt in range(KT):
                            mm = product(g_ps[:, bank, tj * PW:(tj + 1) * PW], (c_hi[:, kt, tok], c_lo[:, kt, tok]),
                                         (w.wv_hi[:, kt], w.wv_lo[:, kt]), kt == 0, kt == KT - 1)
                    mm.then_inc(z.turn_done, 1)

                def step(kind, n, p, s, h, vs):
                    u = B * h + n
                    if kind in "GY":
                        number, bank = Turns.number(p, s, kind, n), Turns.bank(p, s, kind, n)
                    if kind == "S":
                        if n == 0:
                            pe.wait_ge(z.turn_out, Turns.qk_out(p, s))
                            pe.wait_ge(z.kbias, 2 * (h + 1))
                        wait(pe, z.exp_done, 2 * (u - 1))
                        for qt in range(QT):
                            cols = slice(n * S + qt * P, n * S + (qt + 1) * P)
                            mm = product(s_ps[:, n % 2, qt, 0:NKP], (q_hi[:, s, cols], q_lo[:, s, cols]),
                                         (k_hi[:, s, n], k_lo[:, s, n]))
                        mm.then_inc(z.s_done, 1)
                    elif kind == "G" and n < 4:
                        group(number, bank, h + 1, 1 - s, n)
                    elif kind == "G":
                        values(number, bank, p + 1, 2 * s + n - 4)
                    elif kind == "T":
                        pe.wait_ge(z.norm_done, 2 * (u + 1))
                        wait(pe, z.t_out, u)
                        for kt in range(QT):
                            for qt in range(QT):
                                at = (kt * QT + qt) * P
                                mm = nc.tensor.transpose(t_ps[:, at:at + P], prob[:, n % 2, qt, kt * P:(kt + 1) * P],
                                                         core.ident[:])
                        mm.then_inc(z.t_done, 1)
                    elif kind == "V":
                        pe.wait_ge(z.t_out, u + 1)
                        if n == 0 and s == 0:
                            pe.wait_ge(z.turn_out, Turns.v_out(p))
                        wait(pe, z.o_lo, u)
                        for kt in range(QT):
                            mm = nc.tensor.matmul(o_ps[:, 0:S], v_sb[:, vs, QT * n + kt, s * K0:(s + 1) * K0],
                                                  probT[:, n % 2, kt * S:(kt + 1) * S],
                                                  start=(kt == 0), stop=(kt == QT - 1))
                        mm.then_inc(z.v_done, 1)
                    elif kind == "Y":
                        take_turn(number)
                        pe.wait_ge(z.o_lo, u + 1)
                        pe.wait_ge(z.wo_split, 2 * (p + 1))
                        for qt in range(QT):
                            cols = slice(n * S + qt * P, n * S + (qt + 1) * P)
                            for a in range(2):
                                mm = product(g_ps[:, bank, qt * D:(qt + 1) * D], (oT_hi[:, a, cols], oT_lo[:, a, cols]),
                                             (wo_hi[:, a], wo_lo[:, a]), a == 0, a == 1)
                        mm.then_inc(z.turn_done, 1)

                pe.wait_ge(z.zero_set, 2)
                for g in range(4):
                    group(g, g % 2, 0, 0, g)
                for j in range(4):
                    values(4 + j, j % 2, 0, j)

                def body(p, vs):
                    for s, h, more, after in halves(p):
                        for kind, n in PE_STEPS[s]:
                            if not left_out(kind, n, s, more, after):
                                step(kind, n, p, s, h, vs)
                pairs(pe, body)


def mlp(core, name, w1, b1, w2, b2, gelu, out=None):
    nc, ins = core.nc, core.ins
    with core.stage(name) as st:
        w1_sb, w2_sb = st.sb("w1", [P, KT, F]), st.sb("w2", [P, FT, D])
        b2_row = st.sb("b2_row", [P, D])
        hid = st.sb("hid", [P, FT, T])
        h_ps, y_ps = st.psum("h_ps", [P, 4, 512]), st.psum("y_ps", [P, 4, 512])
        w1_in, w2_in, b2_in, h_done, h_out, y_done, y_out, x_ready, stored = [
            st.sem(n) for n in ("w1_in", "w2_in", "b2_in", "h_done", "h_out", "y_done", "y_out", "x_ready", "stored")]
        with nc.Block() as block:
            @block.gpsimd
            def _(pool):
                core.clear_used(pool)

            @block.sync
            def _(sp):
                sp.dma_start(w1_sb[:], ins[w1].rearrange("(t p) f -> p t f", p=P)).then_inc(w1_in, 16)
                sp.dma_start(w2_sb[:], ins[w2].rearrange("(t p) d -> p t d", p=P)).then_inc(w2_in, 16)
                sp.dma_start(b2_row[:], ins[b2].rearrange("(o n) -> o n", o=1).broadcast_to([P, D])).then_inc(b2_in, 16)
                if out is not None:
                    dst = out.rearrange("b (t p) d -> p (b t) d", p=P)
                    for t in range(TT):
                        sp.wait_ge(y_out, t + 1)
                        sp.dma_start(dst[:, t], core.x[:, t]).then_inc(stored, 16)
                    sp.wait_ge(stored, 16 * TT)

            @block.tensor
            def _(pe):
                pe.wait_ge(w1_in, 16)
                for n in range(2 * FT):
                    half, f = n // FT, n % FT
                    if n >= 4:
                        pe.wait_ge(h_out, n - 3)
                    for kt in range(KT):
                        mm = nc.tensor.matmul(h_ps[:, n % 4], w1_sb[:, kt, f * P:(f + 1) * P],
                                              core.xT[:, kt, half * 512:(half + 1) * 512],
                                              start=(kt == 0), stop=(kt == KT - 1))
                    mm.then_inc(h_done, 1)
                pe.wait_ge(w2_in, 16)
                for t in range(TT):
                    pe.wait_ge(h_out, FT * (t // 4 + 1))
                    if t >= 4:
                        pe.wait_ge(y_out, t - 3)
                    for f in range(FT):
                        mm = nc.tensor.matmul(y_ps[:, t % 4, 0:D], hid[:, f, t * P:(t + 1) * P], w2_sb[:, f],
                                              start=(f == 0), stop=(f == FT - 1))
                    mm.then_inc(y_done, 1)

            @block.scalar
            def _(act):
                for n in range(2 * FT):
                    half, f = n // FT, n % FT
                    act.wait_ge(h_done, n + 1)
                    nc.scalar.activation(hid[:, f, half * 512:(half + 1) * 512], h_ps[:, n % 4], gelu,
                                         bias=columns(core, b1)[:, f:f + 1]).then_inc(h_out, 1)

            @block.vector
            def _(dve):
                dve.wait_ge(b2_in, 16)
                for t in range(TT):
                    nc.vector.tensor_tensor(core.x[:, t], core.x[:, t], b2_row[:], ALU.add).then_inc(x_ready, 1)
                for t in range(TT):
                    dve.wait_ge(y_done, t + 1)
                    dve.wait_ge(x_ready, t + 1)
                    nc.vector.tensor_tensor(core.x[:, t], y_ps[:, t % 4, 0:D], core.x[:, t], ALU.add).then_inc(y_out, 1)


U = 4


class Small:

    def __init__(self, layer):
        self.layer, self.grouped = layer, layer == 2
        self.HD = 8 if self.grouped else 16
        self.NQ = 8 if self.grouped else 4
        self.quads = B * self.NQ
        self.kheads = 1 if self.grouped else 4
        self.NK = S if self.grouped else 2 * S
        self.NKT = self.NK // P
        self.W = 4 * self.HD
        self.VW = self.kheads * self.HD
        self.scale = self.HD ** -0.5 if self.grouped else 1.0 / self.HD
        self.MASK_ROW, self.MAX_ROW = 3 * self.HD, P - 1


def small_projections(core, c, q_stack, k_stack, v_all, q_st, k_st, v_st):
    nc, ins, L = core.nc, core.ins, c.layer
    with core.stage(f"p{L}") as st:
        KW = 64 if c.grouped else D
        wq = st.sb("wq", [P, KT, D])
        wkv = st.sb("wkv", [P, KT, 2 * KW])
        bv_row = st.sb("bv_row", [P, 2 * KW])
        ones = st.sb("ones", [1, 512])
        n_k = c.NK // S
        KM = 1 if c.grouped else KT
        KP = 64 if c.grouped else P
        q_f, q_hi, q_lo = (st.sb("q_f", [P, KT, T]), st.sb("q_hi", [P, KT, T], F32R), st.sb("q_lo", [P, KT, T], F32R))
        k_f = st.sb("k_f", [KP, KM, B, n_k, S])
        k_hi, k_lo = st.sb("k_hi", [KP, KM, B, n_k, S], F32R), st.sb("k_lo", [KP, KM, B, n_k, S], F32R)
        qk_ps, v_ps = st.psum("qk_ps", [P, 4, 512]), st.psum("v_ps", [P, 4, 512])
        w_in, bv_in, qk_done, qk_f, qk_hi, qk_lo, v_done, v_out, stored, qs = [
            st.sem(n) for n in ("w_in", "bv_in", "qk_done", "qk_f", "qk_hi", "qk_lo", "v_done", "v_out", "stored",
                                "qs")]
        ones_set, stacks_zero, v_zero, rows_in = [st.sem(n) for n in ("ones_set", "stacks_zero", "v_zero", "rows_in")]
        bq = columns(core, f"L{L}_xattn_bq" if c.grouped else f"L{L}_xattn_q_b")
        bk = columns(core, f"L{L}_xattn_bk" if c.grouped else f"L{L}_kv_b_k")
        if c.grouped:
            k_cols = lambda kt, m: wkv[:, kt, 0:KW]
            v_cols = lambda kt: wkv[:, kt, KW:2 * KW]
            v_bias = bv_row[:, 0:KW]
        else:
            kv = wkv[:].rearrange("p t (n two) -> p t n two", two=2)
            k_cols = lambda kt, m: kv[:, kt, m * P:(m + 1) * P, 0]
            v_cols = lambda kt: kv[:, kt, :, 1]
            v_bias = bv_row[:].rearrange("p (n two) -> p n two", two=2)[:, :, 1]
        groups = [(False, m, 0, half) for m in range(KT) for half in range(2)]
        groups += [(True, m, src, half) for m in range(KM) for src in range(n_k) for half in range(2)]
        tiles = [(src, t) for src in range(n_k) for t in range(TT)]

        def places(part_q, part_k, g):
            is_k, m, src, half = groups[g]
            if is_k:
                return part_k[:, m, 2 * half:2 * half + 2, src, :]
            return part_q[:, m, half * 512:(half + 1) * 512]

        def stores(part, is_k):
            if is_k:
                for m in range(KM):
                    dst = k_stack[part].rearrange("(b c) t -> c b t", b=B)[m * KP:(m + 1) * KP]
                    yield dst, (k_hi, k_lo)[part][:, m].rearrange("p b s t -> p b (s t)")
            else:
                for m in range(KT):
                    dst = q_stack[part].rearrange("(b c) t -> c b t", b=B)[m * P:(m + 1) * P]
                    yield dst, (q_hi, q_lo)[part][:, m].rearrange("p (b t) -> p b t", b=B)

        with nc.Block() as block:
            @block.gpsimd
            def _(pool):
                core.clear_used(pool)
                nc.gpsimd.memset(ones[:], 1.0).then_inc(ones_set, 1)
                nc.gpsimd.memset(v_st[:], 0.0).then_inc(v_zero, 1)
                nc.gpsimd.memset(q_st[:].bitcast(F32), 0.0).then_inc(stacks_zero, 1)
                nc.gpsimd.memset(k_st[:].bitcast(F32), 0.0).then_inc(stacks_zero, 1)
                pool.wait_ge(v_zero, 1)
                nc.gpsimd.memset(v_st[:, :, :, :, c.HD:c.HD + 1], 1.0)

            @block.sync
            def _(sp):
                view = "(t p) n -> p t n"
                sp.dma_start(wq[:], ins[f"L{L}_xattn_Wq" if c.grouped else f"L{L}_xattn_q_w"].rearrange(view, p=P)
                             ).then_inc(w_in, 16)
                if c.grouped:
                    sp.dma_start(wkv[:, :, 0:KW], ins["L2_xattn_Wk"].rearrange(view, p=P)).then_inc(w_in, 16)
                    sp.dma_start(wkv[:, :, KW:], ins["L2_xattn_Wv"].rearrange(view, p=P)).then_inc(w_in, 16)
                    sp.dma_start(bv_row[:, 0:KW], ins["L2_xattn_bv"].rearrange("(o n) -> o n", o=1)
                                 .broadcast_to([P, KW])).then_inc(bv_in, 16)
                else:
                    sp.dma_start(wkv[:], ins[f"L{L}_xattn_kv_w"].rearrange(view, p=P)).then_inc(w_in, 16)
                    sp.dma_start(bv_row[:], ins[f"L{L}_xattn_kv_b"].rearrange("(o n) -> o n", o=1)
                                 .broadcast_to([P, 2 * KW])).then_inc(bv_in, 16)
                sp.wait_ge(ones_set, 1)
                sp.wait_ge(stacks_zero, 2)
                row = ones[:].rearrange("o (a n) -> o a n", a=1)
                if not c.grouped:
                    m = c.MASK_ROW
                    sp.dma_start(q_st[m:m + 1].bitcast(F32).rearrange("o u j t -> o (u j t)").rearrange(
                        "o (a n) -> o a n", n=512), row.broadcast_to([1, U * 2, 512])).then_inc(rows_in, 16)
                m = c.MAX_ROW
                sp.dma_start(k_st[m:m + 1].bitcast(F32).rearrange("o u j t -> o (u j t)").rearrange(
                    "o (a n) -> o a n", n=256), row[:, :, 0:256].broadcast_to([1, U * c.kheads * c.NK // 256, 256])
                    ).then_inc(rows_in, 16)
                n = 0
                for is_k, until in ((False, 4), (True, len(groups))):
                    for part in range(2):
                        sp.wait_ge((qk_hi, qk_lo)[part], until)
                        for dst, src in stores(part, is_k):
                            sp.dma_start(dst, src.bitcast(F32)).then_inc(stored, 16)
                            n += 1
                sp.wait_ge(stored, 16 * n)
                sp.wait_ge(rows_in, 16 if c.grouped else 32)

            @block.tensor
            def _(pe):
                pe.wait_ge(w_in, 48 if c.grouped else 32)
                for g, (is_k, m, src, half) in enumerate(groups):
                    if g >= 4:
                        pe.wait_ge(qk_f, g - 3)
                    rhs = core.xT if not is_k or src else core.cT
                    for kt in range(KT):
                        lhs = k_cols(kt, m) if is_k else wq[:, kt, m * P:(m + 1) * P]
                        mm = nc.tensor.matmul(qk_ps[0:KP if is_k else P, g % 4], lhs,
                                              rhs[:, kt, half * 512:(half + 1) * 512],
                                              start=(kt == 0), stop=(kt == KT - 1))
                    mm.then_inc(qk_done, 1)
                for n, (src, t) in enumerate(tiles):
                    if n >= 4:
                        pe.wait_ge(v_out, n - 3)
                    lhs = (core.cT, core.xT)[src]
                    for kt in range(KT):
                        mm = nc.tensor.matmul(v_ps[:, n % 4, 0:KW], lhs[:, kt, t * P:(t + 1) * P], v_cols(kt),
                                              start=(kt == 0), stop=(kt == KT - 1))
                    mm.then_inc(v_done, 1)

            @block.vector
            def _(dve):
                for g, (is_k, m, src, half) in enumerate(groups):
                    dve.wait_ge(qk_done, g + 1)
                    ps, out = qk_ps[0:KP if is_k else P, g % 4], places(q_f, k_f, g)
                    if is_k:
                        nc.vector.tensor_scalar(out, ps.rearrange("p (b t) -> p b t", t=S), bk[0:KP, m:m + 1], None,
                                                ALU.add).then_inc(qk_f, 1)
                    else:
                        nc.vector.tensor_scalar(out, ps, bq[:, m:m + 1], c.scale, ALU.add, ALU.mult
                                                ).then_inc(qk_f, 1)
                    if g:
                        dve.wait_ge(qk_hi, g)
                        nc.vector.tensor_tensor(places(q_lo, k_lo, g - 1), places(q_f, k_f, g - 1),
                                                places(q_hi, k_hi, g - 1).bitcast(F32), ALU.subtract
                                                ).then_inc(qk_lo, 1)
                dve.wait_ge(qk_hi, len(groups))
                g = len(groups) - 1
                nc.vector.tensor_tensor(places(q_lo, k_lo, g), places(q_f, k_f, g),
                                        places(q_hi, k_hi, g).bitcast(F32), ALU.subtract).then_inc(qk_lo, 1)
                dve.wait_ge(bv_in, 16)
                for n, (src, t) in enumerate(tiles):
                    dve.wait_ge(v_done, n + 1)
                    b, kt = t // QT, QT * src + t % QT
                    out = v_all[:, b * c.NQ:(b + 1) * c.NQ, kt, :]
                    nc.vector.tensor_tensor(out, v_ps[:, n % 4, 0:KW].rearrange("p (g w) -> p g w", w=c.VW),
                                            v_bias.rearrange("p (g w) -> p g w", w=c.VW), ALU.add).then_inc(v_out, 1)

            @block.scalar
            def _(act):
                for g in range(len(groups)):
                    act.wait_ge(qk_f, g + 1)
                    nc.scalar.activation(places(q_hi, k_hi, g), places(q_f, k_f, g), ACT.Copy).then_inc(qk_hi, 1)


def small_attention(core, c, q_stack, k_stack, v_all, o_all, q_st, k_st, v_st):
    nc, L = core.nc, c.layer
    HD, NKT, KH = c.HD, c.NKT, c.kheads
    NM = 8
    NS = 4 if c.grouped else 8
    NE = 2 if c.grouped else 4
    LQ, LK = 3, 3 if c.grouped else 4
    if c.grouped:
        steps = [("S", 0), ("E", 0), ("S", 1), ("P", 0), ("M", 0), ("S", 2), ("P", 1), ("E", 1), ("S", 3), ("X", 0)]
    else:
        steps = [("S", 0), ("E", 0), ("S", 1), ("P", 0), ("S", 2), ("P", 1), ("M", 0), ("S", 3), ("E", 1), ("P", 2),
                 ("S", 4), ("P", 3), ("S", 5), ("E", 2), ("X", 0), ("S", 6), ("S", 7), ("E", 3)]

    def turned(i):
        return not isinstance(i, int) or 1 <= i <= c.quads

    def iterations(body):
        def flags(i):
            return i < c.quads, 2 <= i <= c.quads + 1, i >= 3

        def run(eng):
            loops = (c.quads - 2 - U) // U
            for i in range(U):
                body(i // U, i, i % U, *flags(i), i + 2 < c.quads)
            with eng.Fori(1, 1 + loops) as r:
                for s in range(U):
                    body(r, U * r + s, s, True, True, True, True)
            for i in range(U * (1 + loops), c.quads + 3):
                body(i // U, i, i % U, *flags(i), i + 2 < c.quads)
        return run

    with core.stage(f"s{L}") as st:
        mx = st.sb("mx", [P, U, NM])
        mxT = st.sb("mxT", [NM, U, P], F32R)
        probT = st.sb("probT", [P, U, NE, 2 * 512])
        oT = st.sb("oT", [P, S])
        rden = st.sb("rden", [P, QT, 4])
        s_ps = st.psum("s_ps", [P, 2, 512])
        st_ps = st.psum("st_ps", [P, 4, 512])
        o_ps, x_ps = st.psum("o_ps", [P, 512]), st.psum("x_ps", [P, 512])
        names = ("v_in", "s_done", "max_done",
                 "mx_turned", "mx_out", "row_in", "st_done", "exp_done", "o_done", "o_out", "x_done", "rden_done",
                 "x_out", "mask_in", "mask_turned", "mask_hi", "mask_lo", "mask_set")
        z = type("Semaphores", (), {n: st.sem(n) for n in names})
        q_in, k_in = st.slot_sems("q_in", U), st.slot_sems("k_in", U)
        if c.grouped:
            mask = st.sb("mask", [P, B * QT, S])
            mT_hi, mT_lo = st.sb("mT_hi", [P, B, NKT, S], F32R), st.sb("mT_lo", [P, B, NKT, S], F32R)
            ident_r = st.sb("ident_r", [P, P], F32R)
            masked = st.sb("masked", [P, 2, 2, S])
            carrier = st.sb("carrier", [P, NS])
            mask_st = st.sb("mask_st", [P, U, QT, S])

        def prob_of(slot, j, kt):
            e, at = (kt, j * S) if c.grouped else (j, kt * S)
            return probT[:, slot, e, at:at + S]

        with nc.Block() as block:
            @block.sync
            def _(sp):
                if c.grouped:
                    sp.dma_start(mask[:], core.ins["mask_Bx1xSxS2_ff0"].rearrange("b o (t p) k -> p (b o t) k", p=P)
                                 ).then_inc(z.mask_in, 16)

                def load(i, s):
                    wait(sp, z.st_done, NE * (i - 3))
                    for n, part in enumerate((0, 0, 1)):
                        sp.dma_start(q_st[n * HD:(n + 1) * HD, s].bitcast(F32),
                                     q_stack[part, bass.ds(i * c.W, c.W), :].rearrange("(j d) t -> d j t", d=HD)
                                     ).then_inc(q_in[s], 16)
                    for n, part in enumerate((0, 1, 0)):
                        sp.dma_start(k_st[n * HD:(n + 1) * HD, s].bitcast(F32),
                                     k_stack[part, bass.ds(i * c.VW, c.VW), :].rearrange("(j d) t -> d j t", d=HD)
                                     ).then_inc(k_in[s], 16)
                    if not c.grouped:
                        m = c.MASK_ROW
                        sp.dma_start(k_st[m:m + 1, s].bitcast(F32),
                                     core.maskrow[bass.ds(i // c.NQ, 1), :].rearrange("b (o t) -> b o t", o=1)
                                     .broadcast_to([1, KH, c.NK])).then_inc(k_in[s], 16)

                load(0, 0)
                load(1, 1)

                def body(r, i, s, st1, st2, st3, ahead):
                    if turned(i):
                        sp.wait_ge(z.mx_out, i)
                        m, s1 = c.MAX_ROW, (s + 3) % U
                        sp.dma_start(q_st[m:m + 1, s1].bitcast(F32).rearrange("o j (t n) -> o (j t) n", n=P),
                                     mxT[:, s1].bitcast(F32)).then_inc(z.row_in, 16)
                    if ahead:
                        load(i + 2, (s + 2) % U)
                iterations(body)(sp)

            @block.gpsimd
            def _(pool):
                core.clear_used(pool)
                if c.grouped:
                    pool.wait_ge(z.mask_in, 16)

                def body(r, i, s, st1, st2, st3, ahead):
                    if st1:
                        if c.grouped:
                            wait(pool, z.max_done, NM * (i - 3))
                            nc.gpsimd.tensor_copy(mask_st[:, s], mask[:, bass.ds((i // c.NQ) * QT, QT)]
                                                  ).then_inc(z.mask_set, 1)
                        wait(pool, z.o_done, i - 3)
                        src = v_all[:, bass.ds(i, 1)].rearrange("p o k (j d) -> p (o k) j d", d=HD)
                        nc.gpsimd.tensor_copy(v_st[:, s, :, :, 0:HD], src).then_inc(z.v_in, 1)
                iterations(body)(pool)

            @block.scalar
            def _(act):
                if c.grouped:
                    for b in range(B):
                        act.wait_ge(z.mask_turned, b + 1)
                        nc.scalar.activation(mT_hi[:, b].rearrange("p k t -> p (k t)"), st_ps[:, b], ACT.Copy
                                             ).then_inc(z.mask_hi, 1)

                def step(kind, n, i, s, st1, st2, st3):
                    if kind == "X" and st3:
                        act.wait_ge(z.o_done, i - 2)
                        wait(act, z.x_done, i - 3)
                        nc.scalar.activation(oT[:], o_ps[:, 0:S], ACT.Copy).then_inc(z.o_out, 1)
                    elif kind == "E" and st2:
                        act.wait_ge(z.st_done, NE * (i - 2) + n + 1)
                        nc.scalar.activation(probT[:, (s + 2) % U, n],
                                             st_ps[:, 2 * (n % 2):2 * (n % 2) + 2].rearrange("p k t -> p (k t)"),
                                             ACT.Exp).then_inc(z.exp_done, 1)

                def body(r, i, s, st1, st2, st3, ahead):
                    for kind, n in steps:
                        if kind == "E":
                            step(kind, n, i, s, st1, st2, st3)
                        if kind == "P" and n == NKT - 1:
                            step("X", 0, i, s, st1, st2, st3)
                iterations(body)(act)

            @block.vector
            def _(dve):
                if c.grouped:
                    nc.vector.tensor_copy(ident_r[:], core.ident[:]).then_inc(z.mask_lo, 1)
                    for b in range(B):
                        dve.wait_ge(z.mask_hi, b + 1)
                        nc.vector.tensor_tensor(mT_lo[:, b].rearrange("p k t -> p (k t)"), st_ps[:, b],
                                                mT_hi[:, b].bitcast(F32).rearrange("p k t -> p (k t)"), ALU.subtract
                                                ).then_inc(z.mask_lo, 1)

                def maxima(n, i, s):
                    if c.grouped:
                        wait(dve, z.max_done, NM * i + 2 * n - 2)
                    dve.wait_ge(z.s_done, NS * i + n + 1)
                    if not c.grouped:
                        nc.vector.tensor_reduce(mx[:, s, n:n + 1], s_ps[:, n % 2, 0:c.NK], AX.X, ALU.max
                                                ).then_inc(z.max_done, 1)
                        return
                    qt, pair = n % 2, n // 2
                    if n == 0:
                        dve.wait_ge(z.mask_set, i + 1)
                    nc.vector.memset(carrier[:, n:n + 1], 0.0)
                    for jj in range(2):
                        m = QT * (2 * pair + jj) + qt
                        nc.vector.tensor_tensor_reduce(
                            out=masked[:, n % 2, jj], in0=s_ps[:, n % 2, jj * S:(jj + 1) * S],
                            in1=mask_st[:, s, qt],
                            scale=1.0, scalar=-3.0e38, op0=ALU.add, op1=ALU.max,
                            accum_out=mx[:, s, m:m + 1]).then_inc(z.max_done, 1)

                def outputs(i):
                    dve.wait_ge(z.x_done, i - 2)
                    wait(dve, z.x_out, QT * (i - 3))
                    xv = x_ps[:, 0:S].rearrange("p (t j w) -> p t j w", t=QT, j=4)
                    nc.vector.reciprocal(rden[:], xv[:, :, :, HD]).then_inc(z.rden_done, 1)
                    dve.wait_ge(z.rden_done, i - 2)
                    for qt in range(QT):
                        nc.vector.tensor_tensor(
                            o_all[:, bass.ds((i - 3) // c.NQ, 1), qt, bass.ds((i - 3) % c.NQ, 1)].rearrange(
                                "p b g (j d) -> p (b g j) d", d=HD),
                            xv[:, qt, :, 0:HD], rden[:, qt].rearrange("p (j o) -> p j o", o=1)
                            .broadcast_to([P, 4, HD]), ALU.mult).then_inc(z.x_out, 1)

                def body(r, i, s, st1, st2, st3, ahead):
                    if st1:
                        wait(dve, z.mx_turned, i - 3)
                    for kind, n in steps:
                        if kind == "S" and st1:
                            maxima(n, i, s)
                        if kind == "X" and st3:
                            outputs(i)
                        if kind == "M" and turned(i):
                            dve.wait_ge(z.mx_turned, i)
                            wait(dve, z.row_in, 16 * (i - 3))
                            nc.vector.tensor_scalar(mxT[:, (s + 3) % U], x_ps[0:NM, S:S + P], -1.0, None, ALU.mult
                                                    ).then_inc(z.mx_out, 1)
                iterations(body)(dve)

            @block.tensor
            def _(pe):
                if c.grouped:
                    pe.wait_ge(z.mask_in, 16)
                    for b in range(B):
                        for kt in range(NKT):
                            for qt in range(QT):
                                at = kt * S + qt * P
                                mm = nc.tensor.transpose(st_ps[:, b, at:at + P],
                                                         mask[:, b * QT + qt, kt * P:(kt + 1) * P], core.ident[:])
                        mm.then_inc(z.mask_turned, 1)
                    pe.wait_ge(z.mask_lo, B + 1)

                def scores(n, i, s, r):
                    if n == 0:
                        pe.wait_ge(q_in[s], 16 * LQ * (r + 1))
                        pe.wait_ge(k_in[s], 16 * LK * (r + 1))
                    wait(pe, z.max_done, NM // NS * (NS * i + n - 1))
                    m = c.MAX_ROW
                    if c.grouped:
                        qt, pair = n % 2, n // 2
                        for jj in range(2):
                            mm = nc.tensor.matmul(s_ps[:, n % 2, jj * S:(jj + 1) * S],
                                                  q_st[0:m, s, 2 * pair + jj, qt * P:(qt + 1) * P], k_st[0:m, s, 0],
                                                  start=True, stop=True)
                    else:
                        j, qt = n // 2, n % 2
                        mm = nc.tensor.matmul(s_ps[:, n % 2], q_st[0:m, s, j, qt * P:(qt + 1) * P], k_st[0:m, s, j],
                                              start=True, stop=True)
                    mm.then_inc(z.s_done, 1)

                def shifted(n, i, s):
                    if n == 0:
                        pe.wait_ge(z.row_in, 16 * (i - 1))
                    wait(pe, z.exp_done, NE * (i - 2) + n - 1)
                    for h in range(2):
                        out = st_ps[:, 2 * (n % 2) + h]
                        if c.grouped:
                            mm = nc.tensor.matmul(out, k_st[:, s, 0, n * P:(n + 1) * P],
                                                  q_st[:, s, 2 * h:2 * h + 2].rearrange("p j t -> p (j t)"),
                                                  start=True, stop=False)
                            for part in (mT_hi, mT_lo):
                                rhs = part[:, bass.ds((i - 2) // c.NQ, 1), n].broadcast_to([P, 2, S])
                                mm = nc.tensor.matmul(out, ident_r[:], rhs, start=False, stop=(part is mT_lo))
                        else:
                            for k in range(2):
                                kt = 2 * h + k
                                mm = nc.tensor.matmul(out[:, k * S:(k + 1) * S],
                                                      k_st[:, s, n, kt * P:(kt + 1) * P], q_st[:, s, n],
                                                      start=True, stop=True)
                    mm.then_inc(z.st_done, 1)

                def values(kt, i, s):
                    if kt == 0:
                        pe.wait_ge(z.exp_done, NE * (i - 2))
                        pe.wait_ge(z.v_in, i - 2)
                        wait(pe, z.o_out, i - 3)
                    for j in range(4):
                        mm = nc.tensor.matmul(o_ps[32 * j:32 * j + 32, 0:S], v_st[:, s, kt, j % KH],
                                              prob_of(s, j, kt), start=(kt == 0), stop=(kt == NKT - 1))
                    if kt == NKT - 1:
                        mm.then_inc(z.o_done, 1)

                def body(r, i, s, st1, st2, st3, ahead):
                    for kind, n in steps:
                        if kind == "S" and st1:
                            scores(n, i, s, r)
                        elif kind == "E" and st2:
                            shifted(n, i, (s + 2) % U)
                        elif kind == "P" and st3:
                            values(n, i, (s + 1) % U)
                        elif kind == "X" and st3:
                            pe.wait_ge(z.o_out, i - 2)
                            wait(pe, z.mx_out, min(i, c.quads) if isinstance(i, int) else i)
                            wait(pe, z.x_out, QT * (i - 3))
                            for qt in range(QT):
                                mm = nc.tensor.transpose(x_ps[:, qt * P:(qt + 1) * P], oT[:, qt * P:(qt + 1) * P],
                                                         core.ident[:])
                            mm.then_inc(z.x_done, 1)
                        elif kind == "M" and turned(i):
                            pe.wait_ge(z.max_done, NM * i)
                            wait(pe, z.x_out, QT * (i - 3))
                            wait(pe, z.mx_out, i - 1)
                            nc.tensor.transpose(x_ps[0:NM, S:S + P], mx[:, (s + 3) % U], core.ident[:]).then_inc(z.mx_turned, 1)
                iterations(body)(pe)


def project_out(core, name, c, o_all, wo, bo, dst):
    nc, ins = core.nc, core.ins
    with core.stage(name) as st:
        w_sb, b_row = st.sb("w", [P, KT, D]), st.sb("b_row", [P, D])
        t_ps, y_ps = st.psum("t_ps", [P, 4, 512]), st.psum("y_ps", [P, 4, 512])
        w_in, b_in, turned, t_out, x_ready, y_done, y_out = [
            st.sem(n) for n in ("w_in", "b_in", "turned", "t_out", "x_ready", "y_done", "y_out")]
        per = P // c.W
        with nc.Block() as block:
            @block.gpsimd
            def _(pool):
                core.clear_used(pool)

            @block.sync
            def _(sp):
                sp.dma_start(w_sb[:], ins[wo].rearrange("(t p) n -> p t n", p=P)).then_inc(w_in, 16)
                sp.dma_start(b_row[:], ins[bo].rearrange("(o n) -> o n", o=1).broadcast_to([P, D])).then_inc(b_in, 16)

            @block.tensor
            def _(pe):
                for half in range(2):
                    for kt in range(KT):
                        for n in range(4):
                            b, qt = 2 * half + n // QT, n % QT
                            mm = nc.tensor.transpose(t_ps[:, KT * half + kt, n * P:(n + 1) * P],
                                                     o_all[:, b, qt, kt * per:(kt + 1) * per].rearrange(
                                                         "p g w -> p (g w)"), core.ident[:])
                        mm.then_inc(turned, 1)
                pe.wait_ge(w_in, 16)
                for t in range(TT):
                    pe.wait_ge(t_out, KT * (t // 4 + 1))
                    if t >= 4:
                        pe.wait_ge(y_out, t - 3)
                    for kt in range(KT):
                        mm = nc.tensor.matmul(y_ps[:, t % 4, 0:D], core.xT[:, kt, t * P:(t + 1) * P], w_sb[:, kt],
                                              start=(kt == 0), stop=(kt == KT - 1))
                    mm.then_inc(y_done, 1)

            @block.vector
            def _(dve):
                for half in range(2):
                    for kt in range(KT):
                        dve.wait_ge(turned, KT * half + kt + 1)
                        nc.vector.tensor_copy(core.xT[:, kt, half * 512:(half + 1) * 512],
                                              t_ps[:, KT * half + kt]).then_inc(t_out, 1)
                dve.wait_ge(b_in, 16)
                for t in range(TT):
                    nc.vector.tensor_tensor(dst[:, t], core.x[:, t], b_row[:], ALU.add).then_inc(x_ready, 1)
                for t in range(TT):
                    dve.wait_ge(y_done, t + 1)
                    dve.wait_ge(x_ready, t + 1)
                    nc.vector.tensor_tensor(dst[:, t], y_ps[:, t % 4, 0:D], dst[:, t], ALU.add).then_inc(y_out, 1)


def final_norm(core, name, gamma, beta):
    nc, ins = core.nc, core.ins
    with core.stage(name) as st:
        g_row, b_row = st.sb("g_row", [P, D]), st.sb("b_row", [P, D])
        stats, mv = st.sb("stats", [P, TT, 6]), st.sb("mv", [P, TT, 2])
        base, power, rstd = st.sb("base", [P, TT]), st.sb("power", [P, TT]), st.sb("rstd", [P, TT])
        rows_in, stats_done, mv_done, base_done, power_set, rstd_done, x_norm, x_scaled = [
            st.sem(n) for n in ("rows_in", "stats_done", "mv_done", "base_done", "power_set", "rstd_done", "x_norm",
                                "x_scaled")]
        with nc.Block() as block:
            @block.sync
            def _(sp):
                for row, src in ((g_row, gamma), (b_row, beta)):
                    sp.dma_start(row[:], ins[src].rearrange("(o n) -> o n", o=1).broadcast_to([P, D])
                                 ).then_inc(rows_in, 16)

            @block.gpsimd
            def _(pool):
                core.clear_used(pool)
                nc.gpsimd.memset(power[:], -0.5).then_inc(power_set, 1)
                pool.wait_ge(power_set, 1)
                pool.wait_ge(base_done, 1)
                nc.gpsimd.tensor_tensor(out=rstd[:], in0=base[:], in1=power[:], op=ALU.pow).then_inc(rstd_done, 1)

            @block.vector
            def _(dve):
                for t in range(TT):
                    nc.vector.bn_stats(stats[:, t, :], core.x[:, t, :]).then_inc(stats_done, 1)
                for t in range(TT):
                    dve.wait_ge(stats_done, t + 1)
                    nc.vector.bn_aggr(mv[:, t, :], stats[:, t, :]).then_inc(mv_done, 1)
                dve.wait_ge(mv_done, TT)
                nc.vector.tensor_scalar(base[:], mv[:, :, 1], EPS, None, ALU.add).then_inc(base_done, 1)
                dve.wait_ge(rstd_done, 1)
                dve.wait_ge(rows_in, 32)
                for t in range(TT):
                    nc.vector.tensor_scalar(core.x[:, t], core.x[:, t], mv[:, t, 0:1], rstd[:, t:t + 1], ALU.subtract,
                                            ALU.mult).then_inc(x_norm, 1)
                for t in range(TT):
                    dve.wait_ge(x_norm, t + 1)
                    nc.vector.tensor_tensor(core.x[:, t], core.x[:, t], g_row[:], ALU.mult).then_inc(x_scaled, 1)
                for t in range(TT):
                    dve.wait_ge(x_scaled, t + 1)
                    nc.vector.tensor_tensor(core.x[:, t], core.x[:, t], b_row[:], ALU.add)


def small_layer(core, layer, wo, bo):
    nc = core.nc
    c = Small(layer)
    turn(core, f"t{layer}", core.x)
    KC = 64 if c.grouped else D
    q_stack = nc.dram_tensor(f"q_stack{layer}", (2, B * D, S), F32).ap()
    k_stack = nc.dram_tensor(f"k_stack{layer}", (2, B * KC, c.NK), F32).ap()
    with core.stage(f"l{layer}", holds_others=True) as st:
        v_all = st.sb("v_all", [P, c.quads, c.NKT, c.VW])
        o_all = st.sb("o_all", [P, B, QT, c.NQ, c.W])
        q_st = st.sb("q_st", [P, U, 4, S], F32R)
        k_st = st.sb("k_st", [P, U, c.kheads, c.NK], F32R)
        v_st = st.sb("v_st", [P, U, c.NKT, c.kheads, 32])
        small_projections(core, c, q_stack, k_stack, v_all, q_st, k_st, v_st)
        small_attention(core, c, q_stack, k_stack, v_all, o_all, q_st, k_st, v_st)
        if c.grouped:
            project_out(core, f"o{layer}", c, o_all, wo, bo, core.x)
            final_norm(core, f"n{layer}", "L2_xattn_gamma", "L2_xattn_beta")
        else:
            a_tok = st.sb("a_tok", [P, TT, D])
            project_out(core, f"o{layer}", c, o_all, wo, bo, a_tok)
            turn(core, f"r{layer}", a_tok, norm="rms", eps=EPS, scale=columns(core, f"L{layer}_xattn_postnorm_w"))


def program(nc, ins, out):
    with ExitStack() as ctx:
        core = Core(nc, ctx, ins)
        setup(core)
        with core.stage("c", holds_others=True) as held:
            core.c_hi, core.c_lo = held.sb("c_hi", [P, KT, T], F32R), held.sb("c_lo", [P, KT, T], F32R)
            for i in (1, 2):
                with core.stage(f"x{i}", holds_others=True) as st:
                    ahead = CrossBuffers(st, core, i)
                    turn(core, f"n0{i}", core.x, norm="ln", eps=LN_EPS0, scale=columns(core, f"L0_xattn_ln{i}_scale"),
                         offset=columns(core, f"L0_xattn_ln{i}_offset"), factor=float(K0) ** -0.5, ahead=ahead)
                    cross_attention0(core, i, ahead)
        turn(core, "n0m", core.x, norm="ln", eps=LN_EPS0, scale=columns(core, "L0_xattn_ln_mlp_scale"),
             offset=columns(core, "L0_xattn_ln_mlp_offset"))
        mlp(core, "m0", "L0_xattn_w_fc1", "L0_xattn_b_fc1", "L0_xattn_w_fc2", "L0_xattn_b_fc2", ACT.Gelu)
        small_layer(core, 1, "L1_xattn_out_w", "L1_xattn_out_b")
        mlp(core, "m1", "L1_xattn_mlp_w1", "L1_xattn_mlp_b1", "L1_xattn_mlp_w2", "L1_xattn_mlp_b2",
            ACT.Gelu_apprx_tanh)
        small_layer(core, 2, "L2_xattn_Wo", "L2_xattn_bo")
        small_layer(core, 3, "L3_xattn_out_w", "L3_xattn_out_b")
        mlp(core, "m3", "L3_xattn_mlp_w1", "L3_xattn_mlp_b1", "L3_xattn_mlp_w2", "L3_xattn_mlp_b2",
            ACT.Gelu_apprx_tanh, out)


def kernel(**inputs):
    import numpy as np
    import concourse.bacc as bacc
    from concourse.bass_utils import run_bass_kernel_spmd

    nc = bacc.Bacc("TRN2", target_bir_lowering=False, num_devices=1)
    arrays, ins = {}, {}
    for name, value in inputs.items():
        a = np.ascontiguousarray(value)
        arrays[name] = a
        ins[name] = nc.dram_tensor(name, a.shape, mybir.dt.from_np(a.dtype), kind="ExternalInput").ap()
    out = nc.dram_tensor("y", (B, S, D), F32, kind="ExternalOutput").ap()
    program(nc, ins, out)
    r = run_bass_kernel_spmd(nc, [arrays], core_ids=[0])
    return r.results[0]["y"]
```

```python
from contextlib import ExitStack

import concourse.bass as bass
from concourse import mybir

P = 128
B = 4
S = 256
D = 256
T = B * S
TT = T // P
KT = D // P
QT = S // P

H0, K0 = 16, 128
E0 = H0 * K0
F = 1024
FT = F // P
LN_EPS0 = 1e-5
EPS = 1e-6
MASKED = -1e30

ALU = mybir.AluOpType
ACT = mybir.ActivationFunctionType
AX = mybir.AxisListType
F32 = mybir.dt.float32
F32R = mybir.dt.float32r
I32 = mybir.dt.int32


def wait(eng, sem, count):
    if isinstance(count, int) and count <= 0:
        return
    eng.wait_ge(sem, count)


class Core:

    def __init__(self, nc, ctx, ins):
        self.nc, self.ctx, self.ins = nc, ctx, ins
        self.used = []
        self.x = self.sb("x_tok", [P, TT, D])
        self.xT = self.sb("xT", [P, KT, T])
        self.cT = self.sb("ctxT", [P, KT, T])
        self.c_hi, self.c_lo = None, None
        self.ident = self.sb("ident", [P, P])
        self.cols = self.sb("cols", [P, 2, P])
        self.maskrow = nc.dram_tensor("maskrow", (B, 2 * S), F32).ap()
        self.wq, self.wkv = self.sb("wq", [P, KT, D]), self.sb("wkv", [P, KT, 2 * D])
        self.bv_row = self.sb("bv_row", [P, 2 * D])

    def sb(self, name, shape, dt=F32):
        return self.ctx.enter_context(self.nc.sbuf_tensor(name, shape, dt))

    def stage(self, name, holds_others=False):
        return Stage(self, name, holds_others)

    def load_projections(self, sp, layer, sem):
        ins, view = self.ins, "(t p) n -> p t n"
        if layer == 2:
            n = 64
            sp.dma_start(self.wq[:], ins["L2_xattn_Wq"].rearrange(view, p=P)).then_inc(sem, 16)
            sp.dma_start(self.wkv[:, :, 0:n], ins["L2_xattn_Wk"].rearrange(view, p=P)).then_inc(sem, 16)
            sp.dma_start(self.wkv[:, :, n:2 * n], ins["L2_xattn_Wv"].rearrange(view, p=P)).then_inc(sem, 16)
            sp.dma_start(self.bv_row[:, 0:n], ins["L2_xattn_bv"].rearrange("(o n) -> o n", o=1).broadcast_to([P, n])
                         ).then_inc(sem, 16)
            return 64
        sp.dma_start(self.wq[:], ins[f"L{layer}_xattn_q_w"].rearrange(view, p=P)).then_inc(sem, 16)
        sp.dma_start(self.wkv[:], ins[f"L{layer}_xattn_kv_w"].rearrange(view, p=P)).then_inc(sem, 16)
        sp.dma_start(self.bv_row[:], ins[f"L{layer}_xattn_kv_b"].rearrange("(o n) -> o n", o=1)
                     .broadcast_to([P, 2 * D])).then_inc(sem, 16)
        return 48

    def clear_used(self, pool):
        for handle in self.used:
            pool.sem_clear(handle)


class Stage:

    def __init__(self, core, name, holds_others):
        self.core, self.name, self.ctx, self.holds_others = core, name, ExitStack(), holds_others
        self.sems = []

    def __enter__(self):
        return self

    def __exit__(self, *a):
        self.ctx.close()
        if not self.holds_others:
            for handle in self.core.used:
                self.core.nc.release_semaphore(handle)
            self.core.used = self.sems

    def sb(self, name, shape, dt=F32):
        return self.ctx.enter_context(self.core.nc.sbuf_tensor(f"{self.name}_{name}", shape, dt))

    def psum(self, name, shape):
        return self.ctx.enter_context(self.core.nc.psum_tensor(f"{self.name}_{name}", shape, F32))

    def sem(self, name):
        self.sems.append(self.core.nc.alloc_semaphore(name=f"{self.name}_{name}"))
        return self.sems[-1]

    def slot_sems(self, name, count):
        return [self.sem(f"{name}{n}") for n in range(count)]


COLS0 = [("L0_xattn_ln1_scale", KT), ("L0_xattn_ln1_offset", KT), ("L0_xattn_bq1", H0), ("L0_xattn_bk1", H0),
         ("L0_xattn_bias_k1", H0), ("L0_xattn_bias_v1", H0), ("L0_xattn_ln_mlp_scale", KT),
         ("L0_xattn_ln_mlp_offset", KT), ("L0_xattn_b_fc1", FT), ("L1_xattn_q_b", KT), ("L1_kv_b_k", KT),
         ("L1_xattn_postnorm_w", KT), ("L1_xattn_mlp_b1", FT), ("L2_xattn_bq", KT)]
COLS1 = [("L0_xattn_ln2_scale", KT), ("L0_xattn_ln2_offset", KT), ("L0_xattn_bq2", H0), ("L0_xattn_bk2", H0),
         ("L0_xattn_bias_k2", H0), ("L0_xattn_bias_v2", H0), ("L3_xattn_q_b", KT), ("L3_kv_b_k", KT),
         ("L3_xattn_postnorm_w", KT), ("L3_xattn_mlp_b1", FT), ("L2_xattn_bk", 1)]
L2_BK = 64


def column_places():
    places = {}
    for n, group in enumerate((COLS0, COLS1)):
        at = 0
        for name, count in group:
            places[name] = (n, at, count)
            at += count
    return places


PLACES = column_places()


def columns(core, name):
    n, at, count = PLACES[name]
    return core.cols[:, n, at:at + count]


def setup(core):
    nc, ins = core.nc, core.ins
    with core.stage("setup") as st:
        c_tok = st.sb("c_tok", [P, TT, D])
        rows = st.sb("rows", [P, 2, P])
        mask_i = st.sb("mask_i", [B, S], I32)
        mask_f = st.sb("mask_f", [B, 2 * S], F32R)
        turned = st.psum("turned", [P, 4, 512])
        turned_cols = st.psum("turned_cols", [P, 2, P])
        ctx_in, rows_in, x_in = st.sem("ctx_in"), st.sem("rows_in"), st.sem("x_in")
        zeroed, ident_made, rows_zeroed = st.sem("zeroed"), st.sem("ident_made"), st.sem("rows_zeroed")
        cols_turned, ctx_turned, masked, mask_out = (
            st.sem("cols_turned"), st.sem("ctx_turned"), st.sem("masked"), st.sem("mask_out"))
        ctx_out, ctx_hi = st.sem("ctx_out"), st.sem("ctx_hi")
        with nc.Block() as block:
            @block.sync
            def _(sp):
                sp.dma_start(c_tok[:], ins["ctx_2048"].rearrange("b (t p) d -> p (b t) d", p=P)).then_inc(ctx_in, 16)
                sp.dma_start(mask_i[:], ins["mask_BxS2_ik0"]).then_inc(ctx_in, 16)
                sp.dma_start(core.x[:], ins["x"].rearrange("b (t p) d -> p (b t) d", p=P)).then_inc(x_in, 16)
                sp.wait_ge(masked, 2)
                sp.dma_start(core.maskrow, mask_f[:].bitcast(F32)).then_inc(mask_out, 16)
                sp.wait_ge(mask_out, 16)
                sp.wait_ge(x_in, 16)

            @block.scalar
            def _(act):
                act.wait_ge(rows_zeroed, 1)
                for name, (n, at, count) in PLACES.items():
                    if name.endswith("kv_b_k"):
                        src = ins[name[:2] + "_xattn_kv_b"].rearrange("(c p two) -> c p two", p=P, two=2)[:, :, 0]
                        act.dma_start(rows[at:at + count, n, :], src, allow_slow_non_contiguous=True
                                      ).then_inc(rows_in, 16)
                    elif name == "L2_xattn_bk":
                        src = ins[name].rearrange("(c p) -> c p", c=1)
                        act.dma_start(rows[at:at + 1, n, 0:L2_BK], src).then_inc(rows_in, 16)
                    else:
                        flat = ins[name]
                        if len(flat.shape) == 4:
                            flat = flat.rearrange("a b h k -> (a b h k)")
                        act.dma_start(rows[at:at + count, n, :], flat.rearrange("(c p) -> c p", p=P)
                                      ).then_inc(rows_in, 16)

            @block.gpsimd
            def _(pool):
                core.clear_used(pool)
                nc.gpsimd.memset(rows[:], 0.0).then_inc(rows_zeroed, 1)
                nc.gpsimd.memset(core.ident[:], 0.0).then_inc(zeroed, 1)
                pool.wait_ge(zeroed, 1)
                nc.gpsimd.affine_select(out=core.ident[:], in_=core.ident[:], compare_op=ALU.not_equal, fill=1.0,
                                        base=0, pattern=[[-1, P]], channel_multiplier=1).then_inc(ident_made, 1)

            @block.tensor
            def _(pe):
                pe.wait_ge(ident_made, 1)
                pe.wait_ge(ctx_in, 32)
                for kt in range(KT):
                    for half in range(2):
                        for i in range(4):
                            t = 4 * half + i
                            mm = nc.tensor.transpose(turned[:, 2 * kt + half, i * P:(i + 1) * P],
                                                     c_tok[:, t, kt * P:(kt + 1) * P], core.ident[:])
                        mm.then_inc(ctx_turned, 1)
                pe.wait_ge(rows_in, 16 * len(PLACES))
                for n in range(2):
                    mm = nc.tensor.transpose(turned_cols[:, n, :], rows[:, n, :], core.ident[:])
                mm.then_inc(cols_turned, 1)

            @block.vector
            def _(dve):
                nc.vector.memset(mask_f[:, S:2 * S].bitcast(F32), 0.0).then_inc(masked, 1)
                dve.wait_ge(ctx_in, 32)
                nc.vector.tensor_scalar(mask_f[:, 0:S], mask_i[:], 0.0, MASKED, ALU.is_equal, ALU.mult
                                        ).then_inc(masked, 1)
                for kt in range(KT):
                    for half in range(2):
                        dve.wait_ge(ctx_turned, 2 * kt + half + 1)
                        nc.vector.tensor_copy(core.cT[:, kt, half * 512:(half + 1) * 512],
                                              turned[:, 2 * kt + half, :]).then_inc(ctx_out, 1)
                dve.wait_ge(ctx_out, 2 * KT)
                for kt in range(KT):
                    nc.vector.tensor_copy(core.c_hi[:, kt], core.cT[:, kt]).then_inc(ctx_hi, 1)
                for kt in range(KT):
                    dve.wait_ge(ctx_hi, kt + 1)
                    nc.vector.tensor_tensor(core.c_lo[:, kt], core.cT[:, kt], core.c_hi[:, kt].bitcast(F32),
                                            ALU.subtract)
                dve.wait_ge(cols_turned, 1)
                nc.vector.tensor_copy(core.cols[:], turned_cols[:])


def turn(core, name, src, norm=None, eps=0.0, scale=None, offset=None, factor=1.0, ahead=None):
    nc, ident = core.nc, core.ident
    with core.stage(name) as st:
        stats = st.sb("stats", [P, TT, 6])
        mv = st.sb("mv", [P, TT, 2])
        msq = st.sb("msq", [P, TT])
        base = st.sb("base", [P, TT])
        power = st.sb("power", [P, TT])
        rstd = st.sb("rstd", [P, TT])
        normed = st.sb("normed", [P, TT, D])
        sc = st.sb("sc", [P, 2 * KT])
        turned = st.psum("turned", [P, 4, 512])
        stats_done, mv_done, msq_done, base_done, power_set, rstd_done, normed_done, sc_done, tile_turned = [
            st.sem(n) for n in ("stats_done", "mv_done", "msq_done", "base_done", "power_set", "rstd_done",
                                "normed_done", "sc_done", "tile_turned")]
        z = type("Semaphores", (), {n: st.sem(n) for n in ("w_in0", "w_in1", "rows_in", "one_set", "split",
                                                           "hi_split", "chunk_out", "chunk_hi")})
        chunks = [(kt, slice(half * 512, (half + 1) * 512)) for half in range(2) for kt in range(KT)]
        with nc.Block() as block:
            if ahead is not None:
                @block.sync
                def _(sp):
                    ahead.prepare_sync(sp, z)

                @block.scalar
                def _(act):
                    ahead.prepare_scalar(act, z)
                    act.wait_ge(sc_done, 1 if offset is None else 2)
                    for n, (kt, cols) in enumerate(chunks):
                        act.wait_ge(tile_turned, n + 1)
                        bias = 0.0 if offset is None else sc[:, KT + kt:KT + kt + 1]
                        nc.scalar.activation(core.xT[:, kt, cols], turned[:, n, :], ACT.Identity, bias=bias,
                                             scale=sc[:, kt:kt + 1]).then_inc(z.chunk_out, 1)

            @block.gpsimd
            def _(pool):
                core.clear_used(pool)
                if norm:
                    nc.gpsimd.memset(power[:], -0.5).then_inc(power_set, 1)
                    pool.wait_ge(power_set, 1)
                    pool.wait_ge(base_done, 1)
                    nc.gpsimd.tensor_tensor(out=rstd[:], in0=base[:], in1=power[:], op=ALU.pow).then_inc(rstd_done, 1)
                if ahead is not None:
                    ahead.prepare_pool(pool, z, 0)
                    ahead.prepare_pool(pool, z, 1)

            @block.vector
            def _(dve):
                if scale is not None:
                    nc.vector.tensor_scalar(sc[:, 0:KT], scale, factor, None, ALU.mult).then_inc(sc_done, 1)
                    if offset is not None:
                        nc.vector.tensor_scalar(sc[:, KT:2 * KT], offset, factor, None, ALU.mult).then_inc(sc_done, 1)
                if norm:
                    for t in range(TT):
                        nc.vector.bn_stats(stats[:, t, :], src[:, t, :]).then_inc(stats_done, 1)
                    for t in range(TT):
                        dve.wait_ge(stats_done, t + 1)
                        nc.vector.bn_aggr(mv[:, t, :], stats[:, t, :]).then_inc(mv_done, 1)
                    dve.wait_ge(mv_done, TT)
                    if norm == "rms":
                        nc.vector.tensor_tensor(msq[:], mv[:, :, 0], mv[:, :, 0], ALU.mult).then_inc(msq_done, 1)
                        dve.wait_ge(msq_done, 1)
                        nc.vector.scalar_tensor_tensor(out=base[:], in0=msq[:], scalar=eps, in1=mv[:, :, 1],
                                                       op0=ALU.add, op1=ALU.add).then_inc(base_done, 1)
                    else:
                        nc.vector.tensor_scalar(base[:], mv[:, :, 1], eps, None, ALU.add).then_inc(base_done, 1)
                    dve.wait_ge(rstd_done, 1)
                    for t in range(TT):
                        if norm == "rms":
                            nc.vector.tensor_scalar(normed[:, t, :], src[:, t, :], rstd[:, t:t + 1], None, ALU.mult
                                                    ).then_inc(normed_done, 1)
                        else:
                            nc.vector.tensor_scalar(normed[:, t, :], src[:, t, :], mv[:, t, 0:1], rstd[:, t:t + 1],
                                                    ALU.subtract, ALU.mult).then_inc(normed_done, 1)
                def trailing(n):
                    kt, cols = chunks[n]
                    dve.wait_ge(z.chunk_hi, n + 1)
                    nc.vector.tensor_tensor(ahead.h_lo[:, kt, cols], core.xT[:, kt, cols],
                                            ahead.h_hi[:, kt, cols].bitcast(F32), ALU.subtract)

                for n, (kt, cols) in enumerate(chunks):
                    if ahead is None:
                        dve.wait_ge(tile_turned, n + 1)
                        nc.vector.tensor_copy(core.xT[:, kt, cols], turned[:, n, :])
                        continue
                    dve.wait_ge(z.chunk_out, n + 1)
                    nc.vector.tensor_copy(ahead.h_hi[:, kt, cols], core.xT[:, kt, cols]).then_inc(z.chunk_hi, 1)
                    if n:
                        trailing(n - 1)
                if ahead is not None:
                    trailing(len(chunks) - 1)

            @block.tensor
            def _(pe):
                for half in range(2):
                    if norm:
                        pe.wait_ge(normed_done, 4 * half + 4)
                    for kt in range(KT):
                        for i in range(4):
                            t = 4 * half + i
                            tile = normed[:, t, kt * P:(kt + 1) * P] if norm else src[:, t, kt * P:(kt + 1) * P]
                            mm = nc.tensor.transpose(turned[:, KT * half + kt, i * P:(i + 1) * P], tile, ident[:])
                        mm.then_inc(tile_turned, 1)


def steps(text):
    return [(w[0], int(w[1])) for w in text.split()]


PE_STEPS = (steps("S0 S1 G0 G1 S2 T0 S3 G2 T1 V0 G3 T2 V1 G4 T3 V2 G5 V3"),
            steps("S0 S1 G0 G1 S2 T0 G2 S3 V0 T1 G3 G4 V1 T2 G5 Y0 V2 T3 Y1 V3 Y2 Y3"))
ACT_STEPS = (steps("E0 G0 E1 G1 C0 E2 C1 G2 H0 E3 C2 H1 G3 C3 H2 H3"),
             steps("E0 G0 E1 C0 G1 E2 G2 H0 C1 G3 C2 H1 E3 H2 C3 H3"))
DVE_STEPS = (steps("M0 M1 N0 G0 N1 M2 C0 G1 M3 N2 C1 L0 G2 N3 C2 L1 G3 C3 L2 G4 G5 L3"),
             steps("M0 M1 N0 G0 M2 N1 C0 G1 N2 G2 C1 L0 G3 M3 G4 C2 G5 L1 N3 L2 C3 Y0 Y1 L3 Y2 Y3"))
NK = S + 1
NKP = NK + 1
NPAIR = H0 // 2
PW = 2 * K0


class Turns:
    AHEAD, PAIR, EVEN = 8, 16, 6

    @classmethod
    def number(cls, p, s, kind, n):
        last = isinstance(p, int) and p == NPAIR - 1
        users = [x for x in PE_STEPS[s] if x[0] == "Y" or x[0] == "G" and not (last and (s or x[1] > 3))]
        return cls.AHEAD + cls.PAIR * p + s * (4 if last else cls.EVEN) + users.index((kind, n))

    @staticmethod
    def bank(p, s, kind, n):
        last = isinstance(p, int) and p == NPAIR - 1
        users = [x for x in PE_STEPS[s] if x[0] == "Y" or x[0] == "G" and not (last and (s or x[1] > 3))]
        return users.index((kind, n)) % 2

    @classmethod
    def qk_out(cls, p, s):
        if s:
            return cls.number(p, 0, "G", 3) + 1
        return 4 if isinstance(p, int) and p == 0 else cls.number_of_full(p - 1, 1, "G", 3) + 1

    @classmethod
    def v_out(cls, p):
        return 8 if isinstance(p, int) and p == 0 else cls.number_of_full(p - 1, 1, "G", 5) + 1

    @classmethod
    def number_of_full(cls, p, s, kind, n):
        users = [x for x in PE_STEPS[s] if x[0] in "YG"]
        return cls.AHEAD + cls.PAIR * p + s * cls.EVEN + users.index((kind, n))


class CrossBuffers:

    def __init__(self, st, core, i):
        self.core, self.i = core, i
        self.h_hi, self.h_lo = st.sb("h_hi", [P, KT, T], F32R), st.sb("h_lo", [P, KT, T], F32R)
        self.wqk_raw, self.wv_raw = st.sb("wqk_raw", [P, 2, KT, K0]), st.sb("wv_raw", [P, KT, PW])
        self.wqk_hi, self.wqk_lo = [st.sb(n, [P, 2, 2, KT, K0], F32R) for n in ("wqk_hi", "wqk_lo")]
        self.wv_hi, self.wv_lo = [st.sb(n, [P, KT, PW], F32R) for n in ("wv_hi", "wv_lo")]
        self.one = st.sb("one", [P, 1])
        self.vbias, self.bv_row = st.sb("vbias", [P, E0]), st.sb("bv_row", [P, E0])
        self.bo_row = st.sb("bo_row", [P, D])

    def input(self, name):
        return self.core.ins[f"L0_xattn_{name}{self.i}"]

    def load_qk(self, sp, h, sem):
        for n, w in enumerate(("wq", "wk")):
            sp.dma_start(self.wqk_raw[:, n], self.input(w)[:, bass.ds(h * K0, K0)].rearrange("(t p) n -> p t n", p=P)
                         ).then_inc(sem, 16)

    def load_v(self, sp, p, sem):
        sp.dma_start(self.wv_raw[:], self.input("wv")[:, bass.ds(p * PW, PW)].rearrange("(t p) n -> p t n", p=P)
                     ).then_inc(sem, 16)

    def times_one(self, n):
        return self.one[:].broadcast_to([P, n])

    def qk_parts(self, s):
        flat = "p a t n -> p (a t n)"
        return self.wqk_raw[:].rearrange(flat), self.wqk_hi[:, s].rearrange(flat), self.wqk_lo[:, s].rearrange(flat)

    def v_parts(self):
        return [w[:].rearrange("p t n -> p (t n)") for w in (self.wv_raw, self.wv_hi, self.wv_lo)]

    def prepare_sync(self, sp, z):
        self.load_qk(sp, 0, z.w_in0)
        self.load_v(sp, 0, z.w_in1)
        for row, src in ((self.vbias, "bias_v"), (self.bv_row, "bv"), (self.bo_row, "bo")):
            flat = self.input(src)
            if len(flat.shape) == 4:
                flat = flat.rearrange("a b h k -> (a b h k)")
            sp.dma_start(row[:], flat.rearrange("(o n) -> o n", o=1).broadcast_to([P, flat.shape[0]])
                         ).then_inc(z.rows_in, 16)
        sp.wait_ge(z.rows_in, 48)

    def prepare_scalar(self, act, z):
        pass

    def prepare_pool(self, pool, z, part):
        nc = self.core.nc
        if part == 0:
            nc.gpsimd.memset(self.one[:], 1.0).then_inc(z.one_set, 1)
            pool.wait_ge(z.one_set, 1)
            pool.wait_ge(z.w_in0, 32)
            raw, hi, lo = self.qk_parts(0)
        else:
            pool.wait_ge(z.w_in1, 16)
            raw, hi, lo = self.v_parts()
        nc.gpsimd.tensor_tensor(hi, raw, self.times_one(raw.shape[1]), ALU.mult).then_inc(z.split, 1)
        pool.wait_ge(z.split, part + 1)
        nc.gpsimd.tensor_tensor(lo, raw, hi.bitcast(F32), ALU.subtract)


def cross_attention0(core, i, w):
    nc, ins = core.nc, core.ins
    name = f"L0_xattn_%s{i}"
    wo = ins[name % "wo"]
    with core.stage(f"a{i}") as st:
        h_hi, h_lo, c_hi, c_lo = w.h_hi, w.h_lo, core.c_hi, core.c_lo
        wo_raw = st.sb("wo_raw", [P, 2, D])
        wo_hi, wo_lo = st.sb("wo_hi", [P, 2, D], F32R), st.sb("wo_lo", [P, 2, D], F32R)
        q_hi, q_lo = st.sb("q_hi", [P, 2, T], F32R), st.sb("q_lo", [P, 2, T], F32R)
        k_hi, k_lo = st.sb("k_hi", [P, 2, B, NKP], F32R), st.sb("k_lo", [P, 2, B, NKP], F32R)
        v_sum = st.sb("v_sum", [P, 2, 512])
        v_hi, v_lo = [st.sb(n, [P, 2, TT, PW], F32R) for n in ("v_hi", "v_lo")]
        negmax, den, rden = st.sb("negmax", [P, 2, QT]), st.sb("den", [P, 2, QT]), st.sb("rden", [P, 2, QT])
        prob = st.sb("prob", [P, 2, QT, NKP])
        pT_hi, pT_lo = [st.sb(n, [P, 2, QT * S], F32R) for n in ("pT_hi", "pT_lo")]
        oT_hi, oT_lo = st.sb("oT_hi", [P, 2, T], F32R), st.sb("oT_lo", [P, 2, T], F32R)
        bias_cols = st.sb("bias_cols", [P, 3, H0])
        hc = st.sb("hc", [P, 2, 3])
        vb = st.sb("vb", [P, PW])
        bk_hi, bk_lo = st.sb("bk_hi", [P, H0], F32R), st.sb("bk_lo", [P, H0], F32R)
        g_ps, s_ps = st.psum("g_ps", [P, 2, 512]), st.psum("s_ps", [P, 2, QT, 512])
        t_ps, o_ps = st.psum("t_ps", [P, 512]), st.psum("o_ps", [P, 512])

        sems = ("bo_added", "wo_in", "wqk_in", "wv_in", "wqk_split", "wv_split", "wo_split", "consts", "kbias",
                "turn_done", "g_hi", "turn_out", "s_done", "max_done", "exp_done", "rden_done", "norm_done", "t_done",
                "t_hi", "t_out", "v_split", "v_done", "o_hi", "o_lo", "raw_hi", "zero_set", "vb_done", "head_set",
                "pair_set")
        z = type("Semaphores", (), {n: st.sem(n) for n in sems})
        bq, bk, bkey, bv = (columns(core, name % v) for v in ("bq", "bk", "bias_k", "bias_v"))

        def pairs(eng, body):
            body(0, 0)
            with eng.Fori(0, (NPAIR - 2) // 2) as r:
                body(2 * r + 1, 1)
                body(2 * r + 2, 0)
            body(NPAIR - 1, 1)

        def halves(p):
            last = isinstance(p, int) and p == NPAIR - 1
            return [(0, 2 * p, True, not last), (1, 2 * p + 1, not last, not last)]

        def left_out(kind, n, s, more, after):
            return kind == "G" and (not more or n > 3 and not after)

        with nc.Block() as block:
            @block.sync
            def _(sp):
                def load_qk(h):
                    wait(sp, z.wqk_split, 2 * (h - 1))
                    w.load_qk(sp, h, z.wqk_in)

                load_qk(1)

                def body(p, vs):
                    for s, h, _, after in halves(p):
                        if after:
                            load_qk(h + 2)
                        if s == 0:
                            if after:
                                wait(sp, z.wv_split, 2 * p)
                                w.load_v(sp, p + 1, z.wv_in)
                            wait(sp, z.wo_split, 2 * p)
                            sp.dma_start(wo_raw[:], wo[bass.ds(p * PW, PW), :].rearrange("(h p) n -> p h n", p=P)
                                         ).then_inc(z.wo_in, 16)
                pairs(sp, body)

            @block.gpsimd
            def _(pool):
                core.clear_used(pool)
                nc.gpsimd.memset(k_hi[:, :, :, NK:NKP].bitcast(F32), 0.0).then_inc(z.zero_set, 1)
                nc.gpsimd.memset(k_lo[:, :, :, NK:NKP].bitcast(F32), 0.0).then_inc(z.zero_set, 1)
                nc.gpsimd.tensor_copy(bk_hi[:], bkey).then_inc(z.raw_hi, 1)
                pool.wait_ge(z.raw_hi, 1)
                nc.gpsimd.tensor_tensor(bk_lo[:], bkey, bk_hi[:].bitcast(F32), ALU.subtract).then_inc(z.raw_hi, 1)
                pool.wait_ge(z.raw_hi, 2)

                def split_qk(h, s, free):
                    pool.wait_ge(z.wqk_in, 32 * h)
                    if free is not None:
                        pool.wait_ge(z.turn_done, free)
                    raw, hi, lo = w.qk_parts(s)
                    nc.gpsimd.tensor_tensor(hi, raw, w.times_one(raw.shape[1]), ALU.mult).then_inc(z.wqk_split, 1)
                    pool.wait_ge(z.wqk_split, 2 * h - 1)
                    nc.gpsimd.tensor_tensor(lo, raw, hi.bitcast(F32), ALU.subtract).then_inc(z.wqk_split, 1)

                def split_v(p):
                    pool.wait_ge(z.wv_in, 16 * p)
                    pool.wait_ge(z.turn_done, Turns.v_out(p - 1))
                    raw, hi, lo = w.v_parts()
                    nc.gpsimd.tensor_tensor(hi, raw, w.times_one(raw.shape[1]), ALU.mult).then_inc(z.wv_split, 1)
                    pool.wait_ge(z.wv_split, 2 * p - 1)
                    nc.gpsimd.tensor_tensor(lo, raw, hi.bitcast(F32), ALU.subtract).then_inc(z.wv_split, 1)

                def split_o(p):
                    pool.wait_ge(z.wo_in, 16 * (p + 1))
                    if not (isinstance(p, int) and p == 0):
                        pool.wait_ge(z.turn_done, Turns.number_of_full(p - 1, 1, "Y", B - 1) + 1)
                    raw, hi, lo = [x[:].rearrange("p h n -> p (h n)") for x in (wo_raw, wo_hi, wo_lo)]
                    nc.gpsimd.tensor_tensor(hi, raw, w.times_one(raw.shape[1]), ALU.mult).then_inc(z.wo_split, 1)
                    pool.wait_ge(z.wo_split, 2 * p + 1)
                    nc.gpsimd.tensor_tensor(lo, raw, hi.bitcast(F32), ALU.subtract).then_inc(z.wo_split, 1)

                def split_values(number, p, vs, j):
                    pool.wait_ge(z.turn_out, number + 1)
                    raw = v_sum[:, j % 2]
                    hi, lo = [x[:, vs, 2 * j:2 * j + 2].rearrange("p t d -> p (t d)") for x in (v_hi, v_lo)]
                    nc.gpsimd.tensor_tensor(hi, raw, w.times_one(512), ALU.mult).then_inc(z.v_split, 1)
                    pool.wait_ge(z.v_split, 8 * p + 2 * j + 1)
                    nc.gpsimd.tensor_tensor(lo, raw, hi.bitcast(F32), ALU.subtract).then_inc(z.v_split, 1)

                def key_bias(h, s):
                    wait(pool, z.s_done, B * (h - 1))
                    for part, src in ((k_hi, bk_hi), (k_lo, bk_lo)):
                        nc.gpsimd.tensor_copy(part[:, s, :, S:NK].rearrange("p b o -> p (b o)"),
                                              src[:, bass.ds(h, 1)].bitcast(F32).broadcast_to([P, B])
                                              ).then_inc(z.kbias, 1)

                key_bias(0, 0)
                split_qk(1, 1, None)
                for j in range(4):
                    split_values(4 + j, 0, 0, j)
                nc.gpsimd.tensor_tensor(core.x[:], core.x[:], w.bo_row[:].rearrange("p (o n) -> p o n", o=1)
                                        .broadcast_to([P, TT, D]), ALU.add).then_inc(z.bo_added, 1)

                def body(p, vs):
                    for s, h, more, after in halves(p):
                        if s == 0 and after:
                            split_v(p + 1)
                        if more:
                            key_bias(h + 1, 1 - s)
                        if after:
                            split_qk(h + 2, s, Turns.qk_out(p, s))
                        if s == 0:
                            split_o(p)
                        if after:
                            for n in (4, 5):
                                split_values(Turns.number(p, s, "G", n), p + 1, 1 - vs, 2 * s + n - 4)
                pairs(pool, body)

            def k_out(part, s, g):
                return part[:, s, 2 * g:2 * g + 2, 0:S]

            @block.scalar
            def _(act):
                def group(number, bank, h, s, g):
                    if g == 0:
                        act.wait_ge(z.head_set, h + 1)
                    act.wait_ge(z.turn_done, number + 1)
                    ps = g_ps[:, bank]
                    if g < 2:
                        nc.scalar.activation(q_hi[:, s, g * 512:(g + 1) * 512], ps, ACT.Identity,
                                             bias=hc[:, s, 0:1]).then_inc(z.g_hi, 1)
                    else:
                        nc.scalar.activation(k_out(k_hi, s, g - 2), ps.rearrange("p (b t) -> p b t", t=S),
                                             ACT.Identity, bias=hc[:, s, 1:2]).then_inc(z.g_hi, 1)

                def step(kind, n, p, s, h):
                    u = B * h + n
                    if kind == "E":
                        act.wait_ge(z.max_done, u + 1)
                        wait(act, z.t_done, u - 1)
                        for qt in range(QT):
                            nc.scalar.activation(prob[:, n % 2, qt, 0:NK], s_ps[:, n % 2, qt, 0:NK], ACT.Exp,
                                                 bias=negmax[:, n % 2, qt:qt + 1],
                                                 accum_out=den[:, n % 2, qt:qt + 1]).then_inc(z.exp_done, 1)
                    elif kind == "G":
                        group(Turns.number(p, s, "G", n), Turns.bank(p, s, "G", n), h + 1, 1 - s, n)
                    elif kind == "C":
                        act.wait_ge(z.t_done, u + 1)
                        wait(act, z.v_done, u - 1)
                        nc.scalar.activation(pT_hi[:, n % 2], t_ps[:], ACT.Copy).then_inc(z.t_hi, 1)
                    elif kind == "H":
                        act.wait_ge(z.v_done, u + 1)
                        nc.scalar.activation(oT_hi[:, s, n * S:(n + 1) * S], o_ps[:, 0:S], ACT.Identity,
                                             bias=hc[:, s, 2:3]).then_inc(z.o_hi, 1)

                for g in range(4):
                    group(g, g % 2, 0, 0, g)

                def body(p, vs):
                    for s, h, more, after in halves(p):
                        for kind, n in ACT_STEPS[s]:
                            if not left_out(kind, n, s, more, after):
                                step(kind, n, p, s, h)
                pairs(act, body)

            @block.vector
            def _(dve):
                nc.vector.tensor_scalar(bias_cols[:, 0], bq, float(K0) ** -0.5, None, ALU.mult).then_inc(z.consts, 1)
                nc.vector.tensor_copy(bias_cols[:, 1], bk).then_inc(z.consts, 1)
                nc.vector.tensor_copy(bias_cols[:, 2], bv).then_inc(z.consts, 1)
                dve.wait_ge(z.consts, 3)

                def set_head(h, s):
                    wait(dve, z.o_lo, B * (h - 1))
                    nc.vector.tensor_scalar(hc[:, s], bias_cols[:, :, bass.ds(h, 1)].rearrange("p a o -> p (a o)"),
                                            1.0, None, ALU.mult).then_inc(z.head_set, 1)

                def set_pair(p):
                    if not (isinstance(p, int) and p == 0):
                        dve.wait_ge(z.turn_out, Turns.v_out(p - 1))
                    nc.vector.tensor_scalar(vb[:], w.vbias[:, bass.ds(p * PW, PW)], 1.0, None, ALU.mult
                                            ).then_inc(z.pair_set, 1)

                def group(number, bank, h, s, g):
                    dve.wait_ge(z.g_hi, 4 * h + g + 1)
                    ps = g_ps[:, bank]
                    if g < 2:
                        cols = slice(g * 512, (g + 1) * 512)
                        nc.vector.scalar_tensor_tensor(out=q_lo[:, s, cols], in0=ps, scalar=hc[:, s, 0:1],
                                                       in1=q_hi[:, s, cols].bitcast(F32), op0=ALU.add,
                                                       op1=ALU.subtract).then_inc(z.turn_out, 1)
                    else:
                        nc.vector.scalar_tensor_tensor(out=k_out(k_lo, s, g - 2),
                                                       in0=ps.rearrange("p (b t) -> p b t", t=S),
                                                       scalar=hc[:, s, 1:2],
                                                       in1=k_out(k_hi, s, g - 2).bitcast(F32), op0=ALU.add,
                                                       op1=ALU.subtract).then_inc(z.turn_out, 1)

                def values(number, bank, p, vs, j):
                    dve.wait_ge(z.pair_set, p + 1)
                    dve.wait_ge(z.turn_done, number + 1)
                    wait(dve, z.v_split, 8 * p + 2 * j - 2)
                    nc.vector.tensor_tensor(v_sum[:, j % 2].rearrange("p (t d) -> p t d", d=PW),
                                            g_ps[:, bank].rearrange("p (t d) -> p t d", d=PW),
                                            vb[:].rearrange("p (o d) -> p o d", o=1).broadcast_to([P, 2, PW]),
                        ALU.add).then_inc(z.turn_out, 1)

                def step(kind, n, p, s, h, vs):
                    u = B * h + n
                    if kind in "GY":
                        number, bank = Turns.number(p, s, kind, n), Turns.bank(p, s, kind, n)
                    if kind == "M":
                        dve.wait_ge(z.s_done, u + 1)
                        nc.vector.tensor_reduce(negmax[:, n % 2], s_ps[:, n % 2, :, 0:NK], AX.X, ALU.max, negate=True
                                                ).then_inc(z.max_done, 1)
                    elif kind == "N":
                        dve.wait_ge(z.exp_done, 2 * (u + 1))
                        wait(dve, z.norm_done, 2 * (u - 1))
                        nc.vector.reciprocal(rden[:, n % 2], den[:, n % 2]).then_inc(z.rden_done, 1)
                        dve.wait_ge(z.rden_done, u + 1)
                        for qt in range(QT):
                            nc.vector.tensor_scalar(prob[:, n % 2, qt, 0:S], prob[:, n % 2, qt, 0:S],
                                                    rden[:, n % 2, qt:qt + 1], None, ALU.mult
                                                    ).then_inc(z.norm_done, 1)
                    elif kind == "G" and n < 4:
                        group(number, bank, h + 1, 1 - s, n)
                    elif kind == "G":
                        values(number, bank, p + 1, 1 - vs, 2 * s + n - 4)
                    elif kind == "C":
                        dve.wait_ge(z.t_hi, u + 1)
                        nc.vector.tensor_tensor(pT_lo[:, n % 2], t_ps[:], pT_hi[:, n % 2].bitcast(F32), ALU.subtract
                                                ).then_inc(z.t_out, 1)
                    elif kind == "L":
                        dve.wait_ge(z.o_hi, u + 1)
                        cols = slice(n * S, (n + 1) * S)
                        nc.vector.scalar_tensor_tensor(out=oT_lo[:, s, cols], in0=o_ps[:, 0:S],
                                                       scalar=hc[:, s, 2:3],
                                                       in1=oT_hi[:, s, cols].bitcast(F32), op0=ALU.add,
                                                       op1=ALU.subtract).then_inc(z.o_lo, 1)
                    elif kind == "Y":
                        if n == 0:
                            dve.wait_ge(z.bo_added, 1)
                            wait(dve, z.turn_out, number - 1)
                        dve.wait_ge(z.turn_done, number + 1)
                        xb = core.x[:, QT * n:QT * n + QT]
                        nc.vector.tensor_tensor(xb, g_ps[:, bank].rearrange("p (t d) -> p t d", d=D), xb, ALU.add
                                                ).then_inc(z.turn_out, 1)

                set_head(0, 0)
                dve.wait_ge(z.head_set, 1)
                nc.vector.tensor_tensor(w.vbias[:], w.bv_row[:], w.vbias[:], ALU.subtract).then_inc(z.vb_done, 1)
                dve.wait_ge(z.vb_done, 1)
                set_pair(0)
                for g in range(4):
                    group(g, g % 2, 0, 0, g)
                for j in range(4):
                    values(4 + j, j % 2, 0, 0, j)

                def body(p, vs):
                    for s, h, more, after in halves(p):
                        if more:
                            set_head(h + 1, 1 - s)
                            dve.wait_ge(z.head_set, h + 2)
                        if s == 0 and after:
                            set_pair(p + 1)
                        for kind, n in DVE_STEPS[s]:
                            if not left_out(kind, n, s, more, after):
                                step(kind, n, p, s, h, vs)
                pairs(dve, body)

            @block.tensor
            def _(pe):
                def product(out, left, right, start=True, stop=True):
                    (a_hi, a_lo), (b_hi, b_lo) = left, right
                    nc.tensor.matmul(out, a_hi, b_hi, start=start, stop=False)
                    nc.tensor.matmul(out, a_hi, b_lo, start=False, stop=False)
                    return nc.tensor.matmul(out, a_lo, b_hi, start=False, stop=stop)

                def take_turn(number):
                    if not (isinstance(number, int) and number < 2):
                        pe.wait_ge(z.turn_out, number - 1)

                def group(number, bank, h, s, g):
                    take_turn(number)
                    if g == 0:
                        wait(pe, z.wqk_split, 2 * h)
                    n, cols = g // 2, slice(g % 2 * 512, (g % 2 + 1) * 512)
                    src = ((h_hi, h_lo), (c_hi, c_lo))[n]
                    for kt in range(KT):
                        mm = product(g_ps[:, bank], (w.wqk_hi[:, s, n, kt], w.wqk_lo[:, s, n, kt]),
                                     (src[0][:, kt, cols], src[1][:, kt, cols]), kt == 0, kt == KT - 1)
                    mm.then_inc(z.turn_done, 1)

                def values(number, bank, p, j):
                    take_turn(number)
                    wait(pe, z.wv_split, 2 * p)
                    for tj in range(2):
                        tok = slice((2 * j + tj) * P, (2 * j + tj + 1) * P)
                        for kt in range(KT):
                            mm = product(g_ps[:, bank, tj * PW:(tj + 1) * PW], (c_hi[:, kt, tok], c_lo[:, kt, tok]),
                                         (w.wv_hi[:, kt], w.wv_lo[:, kt]), kt == 0, kt == KT - 1)
                    mm.then_inc(z.turn_done, 1)

                def step(kind, n, p, s, h, vs):
                    u = B * h + n
                    if kind in "GY":
                        number, bank = Turns.number(p, s, kind, n), Turns.bank(p, s, kind, n)
                    if kind == "S":
                        if n == 0:
                            pe.wait_ge(z.turn_out, Turns.qk_out(p, s))
                            pe.wait_ge(z.kbias, 2 * (h + 1))
                        wait(pe, z.exp_done, 2 * (u - 1))
                        for qt in range(QT):
                            cols = slice(n * S + qt * P, n * S + (qt + 1) * P)
                            mm = product(s_ps[:, n % 2, qt, 0:NKP], (q_hi[:, s, cols], q_lo[:, s, cols]),
                                         (k_hi[:, s, n], k_lo[:, s, n]))
                        mm.then_inc(z.s_done, 1)
                    elif kind == "G" and n < 4:
                        group(number, bank, h + 1, 1 - s, n)
                    elif kind == "G":
                        values(number, bank, p + 1, 2 * s + n - 4)
                    elif kind == "T":
                        pe.wait_ge(z.norm_done, 2 * (u + 1))
                        wait(pe, z.t_out, u)
                        for kt in range(QT):
                            for qt in range(QT):
                                at = (kt * QT + qt) * P
                                mm = nc.tensor.transpose(t_ps[:, at:at + P], prob[:, n % 2, qt, kt * P:(kt + 1) * P],
                                                         core.ident[:])
                        mm.then_inc(z.t_done, 1)
                    elif kind == "V":
                        pe.wait_ge(z.t_out, u + 1)
                        if n == 0 and s == 0:
                            pe.wait_ge(z.v_split, 8 * (p + 1))
                        wait(pe, z.o_lo, u)
                        for kt in range(QT):
                            left = [x[:, vs, QT * n + kt, s * K0:(s + 1) * K0] for x in (v_hi, v_lo)]
                            right = [x[:, n % 2, kt * S:(kt + 1) * S] for x in (pT_hi, pT_lo)]
                            mm = product(o_ps[:, 0:S], left, right, kt == 0, kt == QT - 1)
                        mm.then_inc(z.v_done, 1)
                    elif kind == "Y":
                        take_turn(number)
                        pe.wait_ge(z.o_lo, u + 1)
                        pe.wait_ge(z.wo_split, 2 * (p + 1))
                        for qt in range(QT):
                            cols = slice(n * S + qt * P, n * S + (qt + 1) * P)
                            for a in range(2):
                                mm = product(g_ps[:, bank, qt * D:(qt + 1) * D], (oT_hi[:, a, cols], oT_lo[:, a, cols]),
                                             (wo_hi[:, a], wo_lo[:, a]), a == 0, a == 1)
                        mm.then_inc(z.turn_done, 1)

                pe.wait_ge(z.zero_set, 2)
                for g in range(4):
                    group(g, g % 2, 0, 0, g)
                for j in range(4):
                    values(4 + j, j % 2, 0, j)

                def body(p, vs):
                    for s, h, more, after in halves(p):
                        for kind, n in PE_STEPS[s]:
                            if not left_out(kind, n, s, more, after):
                                step(kind, n, p, s, h, vs)
                pairs(pe, body)


class MlpBuffers:

    def __init__(self, st, core, w1):
        self.core, self.w1 = core, w1
        self.h_hi, self.h_lo = st.sb("h_hi", [P, KT, T], F32R), st.sb("h_lo", [P, KT, T], F32R)
        self.w1_raw = st.sb("w1_raw", [P, 2, KT, F // 2])
        self.w1_hi, self.w1_lo = [st.sb(n, [P, 2, KT, F // 2], F32R) for n in ("w1_hi", "w1_lo")]

    def prepare_sync(self, sp, z):
        for half in range(2):
            src = self.core.ins[self.w1][:, half * (F // 2):(half + 1) * (F // 2)].rearrange("(t p) f -> p t f", p=P)
            sp.dma_start(self.w1_raw[:, half], src).then_inc((z.w_in0, z.w_in1)[half], 16)

    def prepare_scalar(self, act, z):
        for half in range(2):
            act.wait_ge((z.w_in0, z.w_in1)[half], 16)
            self.core.nc.scalar.activation(self.w1_hi[:, half], self.w1_raw[:, half], ACT.Copy).then_inc(z.hi_split, 1)

    def prepare_pool(self, pool, z, part):
        if part == 1:
            for half in range(2):
                pool.wait_ge(z.hi_split, half + 1)
                self.core.nc.gpsimd.tensor_tensor(self.w1_lo[:, half], self.w1_raw[:, half],
                                                  self.w1_hi[:, half].bitcast(F32), ALU.subtract)


def mlp(core, name, w, b1, w2, b2, gelu, next_layer=None, out=None):
    nc, ins = core.nc, core.ins
    with core.stage(name) as st:
        w2_raw, b2_row = st.sb("w2_raw", [P, FT, D]), st.sb("b2_row", [P, D])
        w2_hi, w2_lo = st.sb("w2_hi", [P, FT, D], F32R), st.sb("w2_lo", [P, FT, D], F32R)
        hid = st.sb("hid", [P, 4, 512])
        hid_hi, hid_lo = st.sb("hid_hi", [P, FT, T], F32R), st.sb("hid_lo", [P, FT, T], F32R)
        h_ps, y_ps = st.psum("h_ps", [P, 4, 512]), st.psum("y_ps", [P, 4, 512])
        w2_in, b2_in, w2_hi_done, w2_lo_done, h_done, h_out, hi_done, lo_done, y_done, y_out, x_ready, stored = [
            st.sem(n) for n in ("w2_in", "b2_in", "w2_hi_done", "w2_lo_done", "h_done", "h_out", "hi_done", "lo_done",
                                "y_done", "y_out", "x_ready", "stored")]

        next_in = st.sem("next_in")

        def place(part, n):
            half, f = n // FT, n % FT
            return part[:, f, half * 512:(half + 1) * 512]

        with nc.Block() as block:
            @block.gpsimd
            def _(pool):
                core.clear_used(pool)
                for q in range(4):
                    part = slice(q * FT // 4, (q + 1) * FT // 4)
                    pool.wait_ge(w2_hi_done, q + 1)
                    nc.gpsimd.tensor_tensor(w2_lo[:, part], w2_raw[:, part], w2_hi[:, part].bitcast(F32), ALU.subtract
                                            ).then_inc(w2_lo_done, 1)

            @block.sync
            def _(sp):
                sp.dma_start(w2_raw[:], ins[w2].rearrange("(t p) d -> p t d", p=P)).then_inc(w2_in, 16)
                sp.dma_start(b2_row[:], ins[b2].rearrange("(o n) -> o n", o=1).broadcast_to([P, D])).then_inc(b2_in, 16)
                if next_layer:
                    sp.wait_ge(next_in, core.load_projections(sp, next_layer, next_in))
                if out is not None:
                    dst = out.rearrange("b (t p) d -> p (b t) d", p=P)
                    for t in range(0, TT, 2):
                        sp.wait_ge(y_out, t + 2)
                        sp.dma_start(dst[:, t:t + 2], core.x[:, t:t + 2]).then_inc(stored, 16)
                    sp.wait_ge(stored, 8 * TT)

            @block.tensor
            def _(pe):
                def product(out, left, right, start, stop):
                    (a_hi, a_lo), (b_hi, b_lo) = left, right
                    nc.tensor.matmul(out, a_hi, b_hi, start=start, stop=False)
                    nc.tensor.matmul(out, a_hi, b_lo, start=False, stop=False)
                    return nc.tensor.matmul(out, a_lo, b_hi, start=False, stop=stop)

                for n in range(2 * FT):
                    half, f = n // FT, n % FT
                    if n >= 4:
                        pe.wait_ge(h_out, n - 3)
                    fh, at = f // (FT // 2), f % (FT // 2) * P
                    cols = slice(half * 512, (half + 1) * 512)
                    for kt in range(KT):
                        mm = product(h_ps[:, n % 4], (w.w1_hi[:, fh, kt, at:at + P], w.w1_lo[:, fh, kt, at:at + P]),
                                     (w.h_hi[:, kt, cols], w.h_lo[:, kt, cols]), kt == 0, kt == KT - 1)
                    mm.then_inc(h_done, 1)
                pe.wait_ge(w2_lo_done, 4)
                for t in range(TT):
                    tok = slice(t * P, (t + 1) * P)
                    if t >= 4:
                        pe.wait_ge(y_out, t - 3)
                    for f in range(FT):
                        if t % 4 == 0:
                            pe.wait_ge(lo_done, FT * (t // 4) + f + 1)
                        mm = product(y_ps[:, t % 4, 0:D], (hid_hi[:, f, tok], hid_lo[:, f, tok]),
                                     (w2_hi[:, f], w2_lo[:, f]), f == 0, f == FT - 1)
                    mm.then_inc(y_done, 1)

            @block.scalar
            def _(act):
                for n in range(2 * FT):
                    half, f = n // FT, n % FT
                    act.wait_ge(h_done, n + 1)
                    wait(act, lo_done, n - 3)
                    nc.scalar.activation(hid[:, n % 4], h_ps[:, n % 4], gelu, bias=columns(core, b1)[:, f:f + 1]
                                         ).then_inc(h_out, 1)
                    if 2 <= n < 6:
                        part = slice((n - 2) * FT // 4, (n - 1) * FT // 4)
                        act.wait_ge(w2_in, 16)
                        nc.scalar.activation(w2_hi[:, part], w2_raw[:, part], ACT.Copy).then_inc(w2_hi_done, 1)

            @block.vector
            def _(dve):
                def trailing(n):
                    dve.wait_ge(hi_done, n + 1)
                    nc.vector.tensor_tensor(place(hid_lo, n), hid[:, n % 4], place(hid_hi, n).bitcast(F32),
                                            ALU.subtract).then_inc(lo_done, 1)

                for n in range(2 * FT):
                    dve.wait_ge(h_out, n + 1)
                    nc.vector.tensor_copy(place(hid_hi, n), hid[:, n % 4]).then_inc(hi_done, 1)
                    if n:
                        trailing(n - 1)
                    if n == 2:
                        dve.wait_ge(b2_in, 16)
                    if 3 <= n < 3 + TT:
                        nc.vector.tensor_tensor(core.x[:, n - 3], core.x[:, n - 3], b2_row[:], ALU.add
                                                ).then_inc(x_ready, 1)
                trailing(2 * FT - 1)
                for t in range(TT):
                    dve.wait_ge(y_done, t + 1)
                    dve.wait_ge(x_ready, t + 1)
                    nc.vector.tensor_tensor(core.x[:, t], y_ps[:, t % 4, 0:D], core.x[:, t], ALU.add).then_inc(y_out, 1)


def norm_and_mlp(core, layer, src, w1, b1, w2, b2, gelu, next_layer=None, out=None, **norm):
    with core.stage(f"w{layer}", holds_others=True) as st:
        w = MlpBuffers(st, core, w1)
        turn(core, f"r{layer}", src, ahead=w, **norm)
        mlp(core, f"m{layer}", w, b1, w2, b2, gelu, next_layer, out)


U = 4


class Small:

    def __init__(self, layer):
        self.layer, self.grouped = layer, layer == 2
        self.HD = 8 if self.grouped else 16
        self.NQ = 8 if self.grouped else 4
        self.quads = B * self.NQ
        self.kheads = 1 if self.grouped else 4
        self.NK = S if self.grouped else 2 * S
        self.NKT = self.NK // P
        self.W = 4 * self.HD
        self.VW = self.kheads * self.HD
        self.scale = self.HD ** -0.5 if self.grouped else 1.0 / self.HD
        self.MASK_ROW, self.MAX_ROW = 3 * self.HD, P - 1


def load_stacks(core, c, sp, q_stack, k_stack, q_st, k_st, i, s, q_in, k_in):
    HD = c.HD
    for n, part in enumerate((0, 0, 1)):
        sp.dma_start(q_st[n * HD:(n + 1) * HD, s].bitcast(F32),
                     q_stack[part, bass.ds(i * c.W, c.W), :].rearrange("(j d) t -> d j t", d=HD)).then_inc(q_in, 16)
    for n, part in enumerate((0, 1, 0)):
        sp.dma_start(k_st[n * HD:(n + 1) * HD, s].bitcast(F32),
                     k_stack[part, bass.ds(i * c.VW, c.VW), :].rearrange("(j d) t -> d j t", d=HD)).then_inc(k_in, 16)
    if not c.grouped:
        m = c.MASK_ROW
        sp.dma_start(k_st[m:m + 1, s].bitcast(F32),
                     core.maskrow[bass.ds(i // c.NQ, 1), :].rearrange("b (o t) -> b o t", o=1)
                     .broadcast_to([1, c.kheads, c.NK])).then_inc(k_in, 16)


def small_projections(core, c, q_stack, k_stack, v_all, q_st, k_st, v_st, mask):
    nc, ins, L = core.nc, core.ins, c.layer
    with core.stage(f"p{L}") as st:
        KW = 64 if c.grouped else D
        wq, wkv, bv_row = core.wq, core.wkv, core.bv_row
        ones = st.sb("ones", [1, 512])
        n_k = c.NK // S
        KM = 1 if c.grouped else KT
        KP = 64 if c.grouped else P
        q_f, q_hi, q_lo = (st.sb("q_f", [P, KT, T]), st.sb("q_hi", [P, KT, T], F32R), st.sb("q_lo", [P, KT, T], F32R))
        k_f = st.sb("k_f", [KP, KM, B, n_k, S])
        k_hi, k_lo = st.sb("k_hi", [KP, KM, B, n_k, S], F32R), st.sb("k_lo", [KP, KM, B, n_k, S], F32R)
        qk_ps, v_ps = st.psum("qk_ps", [P, 4, 512]), st.psum("v_ps", [P, 4, 512])
        mask_in, qk_done, qk_f, qk_hi, qk_lo, v_done, v_out, stored = [
            st.sem(n) for n in ("mask_in", "qk_done", "qk_f", "qk_hi", "qk_lo", "v_done", "v_out",
                                "stored")]
        ones_set, stacks_zero, v_zero, rows_in, first_in = [
            st.sem(n) for n in ("ones_set", "stacks_zero", "v_zero", "rows_in", "first_in")]
        bq = columns(core, f"L{L}_xattn_bq" if c.grouped else f"L{L}_xattn_q_b")
        bk = columns(core, f"L{L}_xattn_bk" if c.grouped else f"L{L}_kv_b_k")
        if c.grouped:
            k_cols = lambda kt, m: wkv[:, kt, 0:KW]
            v_cols = lambda kt: wkv[:, kt, KW:2 * KW]
            v_bias = bv_row[:, 0:KW]
        else:
            kv = wkv[:].rearrange("p t (n two) -> p t n two", two=2)
            k_cols = lambda kt, m: kv[:, kt, m * P:(m + 1) * P, 0]
            v_cols = lambda kt: kv[:, kt, :, 1]
            v_bias = bv_row[:].rearrange("p (n two) -> p n two", two=2)[:, :, 1]
        groups = [(True, m, src, half) for m in range(KM) for src in range(n_k) for half in range(2)]
        groups += [(False, m, 0, half) for m in range(KT) for half in range(2)]
        tiles = [(src, t) for src in range(n_k) for t in range(TT)]

        def places(part_q, part_k, g):
            is_k, m, src, half = groups[g]
            if is_k:
                return part_k[:, m, 2 * half:2 * half + 2, src, :]
            return part_q[:, m, half * 512:(half + 1) * 512]

        def store(part, is_k, m):
            if is_k:
                return (k_stack[part].rearrange("(b c) t -> c b t", b=B)[m * KP:(m + 1) * KP],
                        (k_hi, k_lo)[part][:, m].rearrange("p b s t -> p b (s t)"))
            return (q_stack[part].rearrange("(b c) t -> c b t", b=B)[m * P:(m + 1) * P],
                    (q_hi, q_lo)[part][:, m].rearrange("p (b t) -> p b t", b=B))

        with nc.Block() as block:
            @block.gpsimd
            def _(pool):
                core.clear_used(pool)
                nc.gpsimd.memset(ones[:], 1.0).then_inc(ones_set, 1)
                nc.gpsimd.memset(v_st[:], 0.0).then_inc(v_zero, 1)
                nc.gpsimd.memset(q_st[:].bitcast(F32), 0.0).then_inc(stacks_zero, 1)
                nc.gpsimd.memset(k_st[:].bitcast(F32), 0.0).then_inc(stacks_zero, 1)
                pool.wait_ge(v_zero, 1)
                nc.gpsimd.memset(v_st[:, :, :, :, c.HD:c.HD + 1], 1.0)

            @block.sync
            def _(sp):
                if c.grouped:
                    sp.dma_start(mask[:], ins["mask_Bx1xSxS2_ff0"].rearrange("b o (t p) k -> p (b o t) k", p=P)
                                 ).then_inc(mask_in, 16)
                n = 0
                for g, (is_k, m, _, _) in enumerate(groups):
                    if g + 1 == len(groups) or groups[g + 1][:2] != (is_k, m):
                        for part in range(2):
                            sp.wait_ge((qk_hi, qk_lo)[part], g + 1)
                            dst, src = store(part, is_k, m)
                            sp.dma_start(dst, src.bitcast(F32)).then_inc(stored, 16)
                            n += 1
                sp.wait_ge(ones_set, 1)
                sp.wait_ge(stacks_zero, 2)
                row = ones[:].rearrange("o (a n) -> o a n", a=1)
                if not c.grouped:
                    m = c.MASK_ROW
                    sp.dma_start(q_st[m:m + 1].bitcast(F32).rearrange("o u j t -> o (u j t)").rearrange(
                        "o (a n) -> o a n", n=512), row.broadcast_to([1, U * 2, 512])).then_inc(rows_in, 16)
                m = c.MAX_ROW
                sp.dma_start(k_st[m:m + 1].bitcast(F32).rearrange("o u j t -> o (u j t)").rearrange(
                    "o (a n) -> o a n", n=256), row[:, :, 0:256].broadcast_to([1, U * c.kheads * c.NK // 256, 256])
                    ).then_inc(rows_in, 16)
                sp.wait_ge(stored, 16 * n)
                sp.wait_ge(rows_in, 16 if c.grouped else 32)
                for i in range(2):
                    load_stacks(core, c, sp, q_stack, k_stack, q_st, k_st, i, i, first_in, first_in)
                if c.grouped:
                    sp.wait_ge(mask_in, 16)
                sp.wait_ge(first_in, 2 * 16 * (6 if c.grouped else 7))

            @block.tensor
            def _(pe):
                for g, (is_k, m, src, half) in enumerate(groups):
                    if g >= 4:
                        pe.wait_ge(qk_f, g - 3)
                    rhs = core.xT if not is_k or src else core.cT
                    for kt in range(KT):
                        lhs = k_cols(kt, m) if is_k else wq[:, kt, m * P:(m + 1) * P]
                        mm = nc.tensor.matmul(qk_ps[0:KP if is_k else P, g % 4], lhs,
                                              rhs[:, kt, half * 512:(half + 1) * 512],
                                              start=(kt == 0), stop=(kt == KT - 1))
                    mm.then_inc(qk_done, 1)
                for n, (src, t) in enumerate(tiles):
                    if n >= 4:
                        pe.wait_ge(v_out, n - 3)
                    lhs = (core.cT, core.xT)[src]
                    for kt in range(KT):
                        mm = nc.tensor.matmul(v_ps[:, n % 4, 0:KW], lhs[:, kt, t * P:(t + 1) * P], v_cols(kt),
                                              start=(kt == 0), stop=(kt == KT - 1))
                    mm.then_inc(v_done, 1)

            @block.vector
            def _(dve):
                for g, (is_k, m, src, half) in enumerate(groups):
                    dve.wait_ge(qk_done, g + 1)
                    ps, out = qk_ps[0:KP if is_k else P, g % 4], places(q_f, k_f, g)
                    if is_k:
                        nc.vector.tensor_scalar(out, ps.rearrange("p (b t) -> p b t", t=S), bk[0:KP, m:m + 1], None,
                                                ALU.add).then_inc(qk_f, 1)
                    else:
                        nc.vector.tensor_scalar(out, ps, bq[:, m:m + 1], c.scale, ALU.add, ALU.mult
                                                ).then_inc(qk_f, 1)
                    if g:
                        dve.wait_ge(qk_hi, g)
                        nc.vector.tensor_tensor(places(q_lo, k_lo, g - 1), places(q_f, k_f, g - 1),
                                                places(q_hi, k_hi, g - 1).bitcast(F32), ALU.subtract
                                                ).then_inc(qk_lo, 1)
                dve.wait_ge(qk_hi, len(groups))
                g = len(groups) - 1
                nc.vector.tensor_tensor(places(q_lo, k_lo, g), places(q_f, k_f, g),
                                        places(q_hi, k_hi, g).bitcast(F32), ALU.subtract).then_inc(qk_lo, 1)
                for n, (src, t) in enumerate(tiles):
                    dve.wait_ge(v_done, n + 1)
                    b, kt = t // QT, QT * src + t % QT
                    out = v_all[:, b * c.NQ:(b + 1) * c.NQ, kt, :]
                    nc.vector.tensor_tensor(out, v_ps[:, n % 4, 0:KW].rearrange("p (g w) -> p g w", w=c.VW),
                                            v_bias.rearrange("p (g w) -> p g w", w=c.VW), ALU.add).then_inc(v_out, 1)

            @block.scalar
            def _(act):
                for g in range(len(groups)):
                    act.wait_ge(qk_f, g + 1)
                    nc.scalar.activation(places(q_hi, k_hi, g), places(q_f, k_f, g), ACT.Copy).then_inc(qk_hi, 1)


def small_attention(core, c, q_stack, k_stack, v_all, o_all, q_st, k_st, v_st, mask):
    nc, L = core.nc, c.layer
    HD, NKT, KH = c.HD, c.NKT, c.kheads
    NM = 8
    NS = 4 if c.grouped else 8
    NE = 2 if c.grouped else 4
    LQ, LK = 3, 3 if c.grouped else 4
    if c.grouped:
        pe_steps, act_steps = steps("S0 E0 M0 S1 P0 S2 P1 S3 E1 X0"), steps("E0 O0 E1")
        dve_steps = steps("S0 M0 S1 S2 S3 X0")
    else:
        pe_steps = steps("S0 E0 S1 M0 P0 S2 P1 S3 E1 S4 P2 S5 E2 S6 P3 S7 E3 X0")
        act_steps, dve_steps = steps("E0 E1 E2 O0 E3"), steps("S0 S1 S2 M0 S3 S4 S5 S6 S7 X0")

    def turned(i):
        return not isinstance(i, int) or 1 <= i <= c.quads

    def iterations(body):
        def flags(i):
            return i < c.quads, 2 <= i <= c.quads + 1, i >= 3

        def run(eng):
            loops = (c.quads - 2 - U) // U
            for i in range(U):
                body(i // U, i, i % U, *flags(i), i + 2 < c.quads)
            with eng.Fori(1, 1 + loops) as r:
                for s in range(U):
                    body(r, U * r + s, s, True, True, True, True)
            for i in range(U * (1 + loops), c.quads + 3):
                body(i // U, i, i % U, *flags(i), i + 2 < c.quads)
        return run

    with core.stage(f"s{L}") as st:
        mx = st.sb("mx", [P, U, NM])
        mxT = st.sb("mxT", [NM, U, P], F32R)
        probT = st.sb("probT", [P, U, NE, 2 * 512])
        oT = st.sb("oT", [P, S])
        rden = st.sb("rden", [P, QT, 4])
        s_ps = st.psum("s_ps", [P, 2, 512])
        st_ps = st.psum("st_ps", [P, 4, 512])
        o_ps, x_ps = st.psum("o_ps", [P, 512]), st.psum("x_ps", [P, 512])
        names = ("v_in", "s_done", "max_done",
                 "mx_turned", "mx_out", "row_in", "st_done", "exp_done", "o_done", "o_out", "x_done", "rden_done",
                 "x_out", "mask_turned", "mask_hi", "mask_lo", "mask_set")
        z = type("Semaphores", (), {n: st.sem(n) for n in names})
        q_in, k_in = st.slot_sems("q_in", U), st.slot_sems("k_in", U)
        if c.grouped:
            mT_hi, mT_lo = st.sb("mT_hi", [P, B, NKT, S], F32R), st.sb("mT_lo", [P, B, NKT, S], F32R)
            ident_r = st.sb("ident_r", [P, P], F32R)
            masked = st.sb("masked", [P, 2, 2, S])
            carrier = st.sb("carrier", [P, NS])
            mask_st = st.sb("mask_st", [P, U, QT, S])

        def prob_of(slot, j, kt):
            e, at = (kt, j * S) if c.grouped else (j, kt * S)
            return probT[:, slot, e, at:at + S]

        with nc.Block() as block:
            @block.sync
            def _(sp):

                def load(i, s):
                    wait(sp, z.st_done, NE * (i - 3))
                    load_stacks(core, c, sp, q_stack, k_stack, q_st, k_st, i, s, q_in[s], k_in[s])

                def body(r, i, s, st1, st2, st3, ahead):
                    if turned(i):
                        sp.wait_ge(z.mx_out, i)
                        m, s1 = c.MAX_ROW, (s + 3) % U
                        sp.dma_start(q_st[m:m + 1, s1].bitcast(F32).rearrange("o j (t n) -> o (j t) n", n=P),
                                     mxT[:, s1].bitcast(F32)).then_inc(z.row_in, 16)
                    if ahead:
                        load(i + 2, (s + 2) % U)
                iterations(body)(sp)

            @block.gpsimd
            def _(pool):
                core.clear_used(pool)
                def body(r, i, s, st1, st2, st3, ahead):
                    if st1:
                        if c.grouped:
                            wait(pool, z.max_done, NM * (i - 3))
                            nc.gpsimd.tensor_copy(mask_st[:, s], mask[:, bass.ds((i // c.NQ) * QT, QT)]
                                                  ).then_inc(z.mask_set, 1)
                        wait(pool, z.o_done, i - 3)
                        src = v_all[:, bass.ds(i, 1)].rearrange("p o k (j d) -> p (o k) j d", d=HD)
                        nc.gpsimd.tensor_copy(v_st[:, s, :, :, 0:HD], src).then_inc(z.v_in, 1)
                iterations(body)(pool)

            @block.scalar
            def _(act):
                if c.grouped:
                    for b in range(B):
                        act.wait_ge(z.mask_turned, b + 1)
                        nc.scalar.activation(mT_hi[:, b].rearrange("p k t -> p (k t)"), st_ps[:, b], ACT.Copy
                                             ).then_inc(z.mask_hi, 1)

                def step(kind, n, i, s, st1, st2, st3):
                    if kind == "O" and st3:
                        act.wait_ge(z.o_done, i - 2)
                        wait(act, z.x_done, i - 3)
                        nc.scalar.activation(oT[:], o_ps[:, 0:S], ACT.Copy).then_inc(z.o_out, 1)
                    elif kind == "E" and st2:
                        act.wait_ge(z.st_done, NE * (i - 2) + n + 1)
                        nc.scalar.activation(probT[:, (s + 2) % U, n],
                                             st_ps[:, 2 * (n % 2):2 * (n % 2) + 2].rearrange("p k t -> p (k t)"),
                                             ACT.Exp).then_inc(z.exp_done, 1)

                def body(r, i, s, st1, st2, st3, ahead):
                    for kind, n in act_steps:
                        step(kind, n, i, s, st1, st2, st3)
                iterations(body)(act)

            @block.vector
            def _(dve):
                if c.grouped:
                    nc.vector.tensor_copy(ident_r[:], core.ident[:]).then_inc(z.mask_lo, 1)
                    for b in range(B):
                        dve.wait_ge(z.mask_hi, b + 1)
                        nc.vector.tensor_tensor(mT_lo[:, b].rearrange("p k t -> p (k t)"), st_ps[:, b],
                                                mT_hi[:, b].bitcast(F32).rearrange("p k t -> p (k t)"), ALU.subtract
                                                ).then_inc(z.mask_lo, 1)

                def maxima(n, i, s):
                    if c.grouped:
                        wait(dve, z.max_done, NM * i + 2 * n - 2)
                    dve.wait_ge(z.s_done, NS * i + n + 1)
                    if not c.grouped:
                        nc.vector.tensor_reduce(mx[:, s, n:n + 1], s_ps[:, n % 2, 0:c.NK], AX.X, ALU.max
                                                ).then_inc(z.max_done, 1)
                        return
                    qt, pair = n % 2, n // 2
                    if n == 0:
                        dve.wait_ge(z.mask_set, i + 1)
                    nc.vector.memset(carrier[:, n:n + 1], 0.0)
                    for jj in range(2):
                        m = QT * (2 * pair + jj) + qt
                        nc.vector.tensor_tensor_reduce(
                            out=masked[:, n % 2, jj], in0=s_ps[:, n % 2, jj * S:(jj + 1) * S],
                            in1=mask_st[:, s, qt],
                            scale=1.0, scalar=-3.0e38, op0=ALU.add, op1=ALU.max,
                            accum_out=mx[:, s, m:m + 1]).then_inc(z.max_done, 1)

                def outputs(i):
                    dve.wait_ge(z.x_done, i - 2)
                    wait(dve, z.x_out, i - 3)
                    xv = x_ps[:, 0:S].rearrange("p (t j w) -> p t j w", t=QT, j=4)
                    nc.vector.reciprocal(rden[:], xv[:, :, :, HD]).then_inc(z.rden_done, 1)
                    dve.wait_ge(z.rden_done, i - 2)
                    nc.vector.tensor_tensor(
                        o_all[:, :, bass.ds(i - 3, 1)].rearrange("p t g (j d) -> p t (g j) d", d=HD),
                        xv[:, :, :, 0:HD], rden[:].rearrange("p t (j o) -> p t j o", o=1)
                        .broadcast_to([P, QT, 4, HD]), ALU.mult).then_inc(z.x_out, 1)

                def body(r, i, s, st1, st2, st3, ahead):
                    if st1:
                        wait(dve, z.mx_turned, i - 3)
                    for kind, n in dve_steps:
                        if kind == "S" and st1:
                            maxima(n, i, s)
                        if kind == "X" and st3:
                            outputs(i)
                        if kind == "M" and turned(i):
                            dve.wait_ge(z.mx_turned, i)
                            wait(dve, z.row_in, 16 * (i - 3))
                            nc.vector.tensor_scalar(mxT[:, (s + 3) % U], x_ps[0:NM, S:S + P], -1.0, None, ALU.mult
                                                    ).then_inc(z.mx_out, 1)
                iterations(body)(dve)

            @block.tensor
            def _(pe):
                if c.grouped:
                    for b in range(B):
                        for kt in range(NKT):
                            for qt in range(QT):
                                at = kt * S + qt * P
                                mm = nc.tensor.transpose(st_ps[:, b, at:at + P],
                                                         mask[:, b * QT + qt, kt * P:(kt + 1) * P], core.ident[:])
                        mm.then_inc(z.mask_turned, 1)
                    pe.wait_ge(z.mask_lo, B + 1)

                def scores(n, i, s, r):
                    if n == 0:
                        loads = r if s < 2 else r + 1
                        wait(pe, q_in[s], 16 * LQ * loads)
                        wait(pe, k_in[s], 16 * LK * loads)
                    wait(pe, z.max_done, NM // NS * (NS * i + n - 1))
                    m = c.MAX_ROW
                    if c.grouped:
                        qt, pair = n % 2, n // 2
                        for jj in range(2):
                            mm = nc.tensor.matmul(s_ps[:, n % 2, jj * S:(jj + 1) * S],
                                                  q_st[0:m, s, 2 * pair + jj, qt * P:(qt + 1) * P], k_st[0:m, s, 0],
                                                  start=True, stop=True)
                    else:
                        j, qt = n // 2, n % 2
                        mm = nc.tensor.matmul(s_ps[:, n % 2], q_st[0:m, s, j, qt * P:(qt + 1) * P], k_st[0:m, s, j],
                                              start=True, stop=True)
                    mm.then_inc(z.s_done, 1)

                def shifted(n, i, s):
                    if n == 0:
                        pe.wait_ge(z.row_in, 16 * (i - 1))
                    wait(pe, z.exp_done, NE * (i - 2) + n - 1)
                    for h in range(2):
                        out = st_ps[:, 2 * (n % 2) + h]
                        if c.grouped:
                            mm = nc.tensor.matmul(out, k_st[:, s, 0, n * P:(n + 1) * P],
                                                  q_st[:, s, 2 * h:2 * h + 2].rearrange("p j t -> p (j t)"),
                                                  start=True, stop=False)
                            for part in (mT_hi, mT_lo):
                                rhs = part[:, bass.ds((i - 2) // c.NQ, 1), n].broadcast_to([P, 2, S])
                                mm = nc.tensor.matmul(out, ident_r[:], rhs, start=False, stop=(part is mT_lo))
                        else:
                            for k in range(2):
                                kt = 2 * h + k
                                mm = nc.tensor.matmul(out[:, k * S:(k + 1) * S],
                                                      k_st[:, s, n, kt * P:(kt + 1) * P], q_st[:, s, n],
                                                      start=True, stop=True)
                    mm.then_inc(z.st_done, 1)

                def values(kt, i, s):
                    if kt == 0:
                        pe.wait_ge(z.exp_done, NE * (i - 2))
                        pe.wait_ge(z.v_in, i - 2)
                        wait(pe, z.o_out, i - 3)
                    for j in range(4):
                        mm = nc.tensor.matmul(o_ps[32 * j:32 * j + 32, 0:S], v_st[:, s, kt, j % KH],
                                              prob_of(s, j, kt), start=(kt == 0), stop=(kt == NKT - 1))
                    if kt == NKT - 1:
                        mm.then_inc(z.o_done, 1)

                def body(r, i, s, st1, st2, st3, ahead):
                    for kind, n in pe_steps:
                        if kind == "S" and st1:
                            scores(n, i, s, r)
                        elif kind == "E" and st2:
                            shifted(n, i, (s + 2) % U)
                        elif kind == "P" and st3:
                            values(n, i, (s + 1) % U)
                        elif kind == "X" and st3:
                            pe.wait_ge(z.o_out, i - 2)
                            wait(pe, z.mx_out, min(i, c.quads) if isinstance(i, int) else i)
                            wait(pe, z.x_out, i - 3)
                            for qt in range(QT):
                                mm = nc.tensor.transpose(x_ps[:, qt * P:(qt + 1) * P], oT[:, qt * P:(qt + 1) * P],
                                                         core.ident[:])
                            mm.then_inc(z.x_done, 1)
                        elif kind == "M" and turned(i):
                            pe.wait_ge(z.max_done, NM * i)
                            wait(pe, z.x_out, i - 3)
                            wait(pe, z.mx_out, i - 1)
                            nc.tensor.transpose(x_ps[0:NM, S:S + P], mx[:, (s + 3) % U], core.ident[:]
                                                ).then_inc(z.mx_turned, 1)
                iterations(body)(pe)


def project_out(core, name, c, o_all, wo, bo, dst):
    nc, ins = core.nc, core.ins
    with core.stage(name) as st:
        w_sb, b_row = st.sb("w", [P, KT, D]), st.sb("b_row", [P, D])
        t_ps, y_ps = st.psum("t_ps", [P, 4, 512]), st.psum("y_ps", [P, 4, 512])
        w_in, b_in, turned, t_out, x_ready, y_done, y_out = [
            st.sem(n) for n in ("w_in", "b_in", "turned", "t_out", "x_ready", "y_done", "y_out")]
        per = P // c.W
        with nc.Block() as block:
            @block.gpsimd
            def _(pool):
                core.clear_used(pool)

            @block.sync
            def _(sp):
                sp.dma_start(w_sb[:], ins[wo].rearrange("(t p) n -> p t n", p=P)).then_inc(w_in, 16)
                sp.dma_start(b_row[:], ins[bo].rearrange("(o n) -> o n", o=1).broadcast_to([P, D])).then_inc(b_in, 16)

            @block.tensor
            def _(pe):
                for half in range(2):
                    for kt in range(KT):
                        for n in range(4):
                            b, qt = 2 * half + n // QT, n % QT
                            mm = nc.tensor.transpose(t_ps[:, KT * half + kt, n * P:(n + 1) * P],
                                                     o_all[:, qt, b * c.NQ + kt * per:b * c.NQ + (kt + 1) * per]
                                                     .rearrange("p g w -> p (g w)"), core.ident[:])
                        mm.then_inc(turned, 1)
                pe.wait_ge(w_in, 16)
                for t in range(TT):
                    pe.wait_ge(t_out, KT * (t // 4 + 1))
                    if t >= 4:
                        pe.wait_ge(y_out, t - 3)
                    for kt in range(KT):
                        mm = nc.tensor.matmul(y_ps[:, t % 4, 0:D], core.xT[:, kt, t * P:(t + 1) * P], w_sb[:, kt],
                                              start=(kt == 0), stop=(kt == KT - 1))
                    mm.then_inc(y_done, 1)

            @block.vector
            def _(dve):
                for half in range(2):
                    for kt in range(KT):
                        dve.wait_ge(turned, KT * half + kt + 1)
                        nc.vector.tensor_copy(core.xT[:, kt, half * 512:(half + 1) * 512],
                                              t_ps[:, KT * half + kt]).then_inc(t_out, 1)
                dve.wait_ge(b_in, 16)
                for t in range(TT):
                    nc.vector.tensor_tensor(dst[:, t], core.x[:, t], b_row[:], ALU.add).then_inc(x_ready, 1)
                for t in range(TT):
                    dve.wait_ge(y_done, t + 1)
                    dve.wait_ge(x_ready, t + 1)
                    nc.vector.tensor_tensor(dst[:, t], y_ps[:, t % 4, 0:D], dst[:, t], ALU.add).then_inc(y_out, 1)


def final_norm(core, name, gamma, beta, next_layer):
    nc, ins = core.nc, core.ins
    with core.stage(name) as st:
        g_row, b_row = st.sb("g_row", [P, D]), st.sb("b_row", [P, D])
        stats, mv = st.sb("stats", [P, TT, 6]), st.sb("mv", [P, TT, 2])
        base, power, rstd = st.sb("base", [P, TT]), st.sb("power", [P, TT]), st.sb("rstd", [P, TT])
        rows_in, stats_done, mv_done, base_done, power_set, rstd_done, x_norm, x_scaled = [
            st.sem(n) for n in ("rows_in", "stats_done", "mv_done", "base_done", "power_set", "rstd_done", "x_norm",
                                "x_scaled")]
        next_in = st.sem("next_in")
        with nc.Block() as block:
            @block.sync
            def _(sp):
                for row, src in ((g_row, gamma), (b_row, beta)):
                    sp.dma_start(row[:], ins[src].rearrange("(o n) -> o n", o=1).broadcast_to([P, D])
                                 ).then_inc(rows_in, 16)
                sp.wait_ge(next_in, core.load_projections(sp, next_layer, next_in))

            @block.gpsimd
            def _(pool):
                core.clear_used(pool)
                nc.gpsimd.memset(power[:], -0.5).then_inc(power_set, 1)
                pool.wait_ge(power_set, 1)
                pool.wait_ge(base_done, 1)
                nc.gpsimd.tensor_tensor(out=rstd[:], in0=base[:], in1=power[:], op=ALU.pow).then_inc(rstd_done, 1)

            @block.vector
            def _(dve):
                for t in range(TT):
                    nc.vector.bn_stats(stats[:, t, :], core.x[:, t, :]).then_inc(stats_done, 1)
                for t in range(TT):
                    dve.wait_ge(stats_done, t + 1)
                    nc.vector.bn_aggr(mv[:, t, :], stats[:, t, :]).then_inc(mv_done, 1)
                dve.wait_ge(mv_done, TT)
                nc.vector.tensor_scalar(base[:], mv[:, :, 1], EPS, None, ALU.add).then_inc(base_done, 1)
                dve.wait_ge(rstd_done, 1)
                dve.wait_ge(rows_in, 32)
                for t in range(TT):
                    nc.vector.tensor_scalar(core.x[:, t], core.x[:, t], mv[:, t, 0:1], rstd[:, t:t + 1], ALU.subtract,
                                            ALU.mult).then_inc(x_norm, 1)
                for t in range(TT):
                    dve.wait_ge(x_norm, t + 1)
                    nc.vector.tensor_tensor(core.x[:, t], core.x[:, t], g_row[:], ALU.mult).then_inc(x_scaled, 1)
                for t in range(TT):
                    dve.wait_ge(x_scaled, t + 1)
                    nc.vector.tensor_tensor(core.x[:, t], core.x[:, t], b_row[:], ALU.add)


def small_layer(core, layer, wo, bo, out=None):
    nc = core.nc
    c = Small(layer)
    turn(core, f"t{layer}", core.x)
    KC = 64 if c.grouped else D
    q_stack = nc.dram_tensor(f"q_stack{layer}", (2, B * D, S), F32).ap()
    k_stack = nc.dram_tensor(f"k_stack{layer}", (2, B * KC, c.NK), F32).ap()
    with core.stage(f"a{layer}", holds_others=True) as outer:
        a_tok = core.x if c.grouped else outer.sb("a_tok", [P, TT, D])
        with core.stage(f"l{layer}", holds_others=True) as st:
            v_all = st.sb("v_all", [P, c.quads, c.NKT, c.VW])
            o_all = st.sb("o_all", [P, QT, c.quads, c.W])
            q_st = st.sb("q_st", [P, U, 4, S], F32R)
            k_st = st.sb("k_st", [P, U, c.kheads, c.NK], F32R)
            v_st = st.sb("v_st", [P, U, c.NKT, c.kheads, 32])
            mask = st.sb("mask", [P, B * QT, S]) if c.grouped else None
            small_projections(core, c, q_stack, k_stack, v_all, q_st, k_st, v_st, mask)
            small_attention(core, c, q_stack, k_stack, v_all, o_all, q_st, k_st, v_st, mask)
            project_out(core, f"o{layer}", c, o_all, wo, bo, a_tok)
        if c.grouped:
            final_norm(core, f"n{layer}", "L2_xattn_gamma", "L2_xattn_beta", 3)
        else:
            name = f"L{layer}_xattn_%s"
            norm_and_mlp(core, layer, a_tok, name % "mlp_w1", name % "mlp_b1", name % "mlp_w2", name % "mlp_b2",
                         ACT.Gelu_apprx_tanh, 2 if layer == 1 else None, out, norm="rms", eps=EPS,
                         scale=columns(core, name % "postnorm_w"))


def program(nc, ins, out):
    with ExitStack() as ctx:
        core = Core(nc, ctx, ins)
        with core.stage("c", holds_others=True) as held:
            core.c_hi, core.c_lo = held.sb("c_hi", [P, KT, T], F32R), held.sb("c_lo", [P, KT, T], F32R)
            setup(core)
            for i in (1, 2):
                with core.stage(f"x{i}", holds_others=True) as st:
                    ahead = CrossBuffers(st, core, i)
                    turn(core, f"n0{i}", core.x, norm="ln", eps=LN_EPS0, scale=columns(core, f"L0_xattn_ln{i}_scale"),
                         offset=columns(core, f"L0_xattn_ln{i}_offset"), factor=float(K0) ** -0.5, ahead=ahead)
                    cross_attention0(core, i, ahead)
        norm_and_mlp(core, 0, core.x, "L0_xattn_w_fc1", "L0_xattn_b_fc1", "L0_xattn_w_fc2", "L0_xattn_b_fc2",
                     ACT.Gelu, 1, norm="ln", eps=LN_EPS0, scale=columns(core, "L0_xattn_ln_mlp_scale"),
                     offset=columns(core, "L0_xattn_ln_mlp_offset"))
        small_layer(core, 1, "L1_xattn_out_w", "L1_xattn_out_b")
        small_layer(core, 2, "L2_xattn_Wo", "L2_xattn_bo")
        small_layer(core, 3, "L3_xattn_out_w", "L3_xattn_out_b", out)


def kernel(**inputs):
    import numpy as np
    import concourse.bacc as bacc
    from concourse.bass_utils import run_bass_kernel_spmd

    nc = bacc.Bacc("TRN2", target_bir_lowering=False, num_devices=1)
    arrays, ins = {}, {}
    for name, value in inputs.items():
        a = np.ascontiguousarray(value)
        arrays[name] = a
        ins[name] = nc.dram_tensor(name, a.shape, mybir.dt.from_np(a.dtype), kind="ExternalInput").ap()
    out = nc.dram_tensor("y", (B, S, D), F32, kind="ExternalOutput").ap()
    program(nc, ins, out)
    r = run_bass_kernel_spmd(nc, [arrays], core_ids=[0])
    return r.results[0]["y"]
```
